# Optimizing a Trainium2 kernel written in Bass

```python
import numpy as np
import jax
import jax.numpy as jnp

def _softmax(x, axis=-1):
    return jax.nn.softmax(x, axis=axis)

def _gelu(x):
    return jax.nn.gelu(x, approximate=True)

def _silu(x):
    return jax.nn.silu(x)

def _sigmoid(x):
    return jax.nn.sigmoid(x)

def _layernorm(x, axis=-1, eps=1e-05):
    m = jnp.mean(x, axis=axis, keepdims=True)
    v = jnp.var(x, axis=axis, keepdims=True)
    return (x - m) / jnp.sqrt(v + eps)

def _scatter_add(tgt, idx, src, axis=0):
    return tgt.at[idx].add(src)

def _segment_sum(src, seg, n):
    return jax.ops.segment_sum(src, seg, n)
kernel_name = 'mk_decoder_preln_d1_seqx_r8_63e151'

def setup_inputs(seed: int=0):
    np.random.seed(seed)
    _w = jnp.asarray

    def _rec_inputs():
        import jax
        import jax.numpy as jnp
        _rk = jax.random.key(seed)
        x = -0.000125 + 0.9999 * jax.random.normal(jax.random.fold_in(_rk, 1), (4, 256, 256), jnp.float32)
        _lenS = 256 - jax.random.randint(jax.random.fold_in(_rk, 7), (4,), 0, max(1, 256 // 4) + 1, jnp.int32)
        _lenS2 = 256 - jax.random.randint(jax.random.fold_in(_rk, 8), (4,), 0, max(1, 256 // 4) + 1, jnp.int32)
        itok_BxS_13_99985 = jax.random.randint(jax.random.fold_in(_rk, 11), (4, 256), 13, 99986, jnp.int32)
        _ctx_2048P = jax.random.normal(jax.random.fold_in(_rk, 12), (4, 16, 256), jnp.float32)
        _ctx_2048c = jax.random.dirichlet(jax.random.fold_in(_rk, 512), 0.3 * jnp.ones((16,), jnp.float32), (4, 256))
        _ctx_2048t = jnp.einsum('bsk,bkd->bsd', _ctx_2048c, _ctx_2048P)
        _ctx_2048t = _ctx_2048t * jax.lax.rsqrt(jnp.mean(jnp.square(_ctx_2048t)) + 1e-12) * 0.953939
        ctx_2048 = 6.82029e-06 + 0.0200006 * (_ctx_2048t + 0.3 * jax.random.normal(jax.random.fold_in(_rk, 612), (4, 256, 256), jnp.float32))
        return (x, itok_BxS_13_99985, ctx_2048)
    x, itok_BxS_13_99985, ctx_2048 = _rec_inputs()

    def _L0_attn_setup():
        import jax, jax.numpy as jnp
        import numpy as np
        import math
        D = 256
        H = 16
        KV = 4
        DH = D // H
        REP = H // KV
        LAMBDA_INIT = 0.8 - 0.6 * math.exp(-0.3 * 0)
        ROPE_BASE = 10000.0
        EPS = 1e-05

        def _rope(x, cos, sin):
            x1, x2 = (x[..., ::2], x[..., 1::2])
            c = cos[None, None]
            s = sin[None, None]
            o1 = x1 * c - x2 * s
            o2 = x1 * s + x2 * c
            return jnp.stack([o1, o2], axis=-1).reshape(x.shape)

        def _forward(x, Wq, Wk, Wv, Wo, lambda_q1, lambda_k1, lambda_q2, lambda_k2, gn_w, gn_b):
            B, T, _ = x.shape
            q = (x @ Wq).reshape(B, T, H, 2 * DH).transpose(0, 2, 1, 3)
            k = (x @ Wk).reshape(B, T, KV, 2 * DH).transpose(0, 2, 1, 3)
            v = (x @ Wv).reshape(B, T, KV, 2 * DH).transpose(0, 2, 1, 3)
            q1, q2 = (q[..., :DH], q[..., DH:])
            k1, k2 = (k[..., :DH], k[..., DH:])
            inv = 1.0 / ROPE_BASE ** (jnp.arange(0, DH, 2, dtype=jnp.float32) / DH)
            freqs = jnp.arange(T, dtype=jnp.float32)[:, None] * inv[None, :]
            cos, sin = (jnp.cos(freqs), jnp.sin(freqs))
            q1, q2 = (_rope(q1, cos, sin), _rope(q2, cos, sin))
            k1, k2 = (_rope(k1, cos, sin), _rope(k2, cos, sin))
            k1 = jnp.repeat(k1, REP, axis=1)
            k2 = jnp.repeat(k2, REP, axis=1)
            v = jnp.repeat(v, REP, axis=1)
            mask = jnp.triu(jnp.full((T, T), -jnp.inf, dtype=x.dtype), k=1)[None, None]
            scale = 1.0 / math.sqrt(DH)
            s1 = jnp.einsum('bhtd,bhsd->bhts', q1, k1) * scale + mask
            s2 = jnp.einsum('bhtd,bhsd->bhts', q2, k2) * scale + mask
            a1 = jax.nn.softmax(s1, axis=-1)
            a2 = jax.nn.softmax(s2, axis=-1)
            lam = jnp.exp(jnp.sum(lambda_q1 * lambda_k1)) - jnp.exp(jnp.sum(lambda_q2 * lambda_k2)) + LAMBDA_INIT
            diff = a1 - lam * a2
            out = jnp.einsum('bhts,bhsd->bhtd', diff, v)
            out = out.transpose(0, 2, 1, 3)
            mean = jnp.mean(out, axis=(1, 3), keepdims=True)
            var = jnp.var(out, axis=(1, 3), keepdims=True)
            out = (out - mean) * jax.lax.rsqrt(var + EPS)
            out = out * gn_w.reshape(1, 1, H, 2 * DH) + gn_b.reshape(1, 1, H, 2 * DH)
            out = out.reshape(B, T, 2 * H * DH) * (1.0 - LAMBDA_INIT)
            return out @ Wo
        key = jax.random.key(seed)
        ks = jax.random.split(key, 12)
        B, T = (1, 256)
        s = 0.02
        return {'x': jax.random.normal(ks[0], (B, T, D), jnp.float32), 'Wq': jax.random.normal(ks[1], (D, 2 * H * DH), jnp.float32) * s, 'Wk': jax.random.normal(ks[2], (D, 2 * KV * DH), jnp.float32) * s, 'Wv': jax.random.normal(ks[3], (D, 2 * KV * DH), jnp.float32) * s, 'Wo': jax.random.normal(ks[4], (2 * H * DH, D), jnp.float32) * s, 'lambda_q1': jax.random.normal(ks[5], (DH,), jnp.float32) * 0.1, 'lambda_k1': jax.random.normal(ks[6], (DH,), jnp.float32) * 0.1, 'lambda_q2': jax.random.normal(ks[7], (DH,), jnp.float32) * 0.1, 'lambda_k2': jax.random.normal(ks[8], (DH,), jnp.float32) * 0.1, 'gn_w': jnp.ones((2 * H * DH,), jnp.float32), 'gn_b': jnp.zeros((2 * H * DH,), jnp.float32)}
    _L0_attn_all = _L0_attn_setup()
    _L0_attn_in = {k: v for k, v in _L0_attn_all.items() if k in ('Wq', 'Wk', 'Wv', 'Wo', 'lambda_q1', 'lambda_k1', 'lambda_q2', 'lambda_k2', 'gn_w', 'gn_b')}
    del _L0_attn_all

    def _L0_xattn_setup():
        import jax, jax.numpy as jnp
        import numpy as np
        B, S, D = (4, 512, 256)
        E = 4
        F = 1024 // E
        VOCAB = 12500
        key = jax.random.key(seed)
        k1, k2, k3, k4, k5 = jax.random.split(key, 5)
        hidden_states = jax.random.normal(k1, (B, S, D), dtype=jnp.float32)
        token_ids = jax.random.randint(k2, (B, S), 0, VOCAB, dtype=jnp.int64)
        Wg = jax.random.normal(k3, (E, F, D), dtype=jnp.float32) * 0.02
        Wu = jax.random.normal(k4, (E, F, D), dtype=jnp.float32) * 0.02
        Wd = jax.random.normal(k5, (E, D, F), dtype=jnp.float32) * 0.02
        return {'hidden_states': hidden_states, 'token_ids': token_ids, 'Wg': Wg, 'Wu': Wu, 'Wd': Wd}
    _L0_xattn_all = _L0_xattn_setup()
    _L0_xattn_in = {k: v for k, v in _L0_xattn_all.items() if k in ()}
    del _L0_xattn_all

    def _L0_ffn_setup():
        import jax, jax.numpy as jnp
        import numpy as np
        B, S, H, I, E, TOP_K, NS = (2, 256, 256, 176, 8, 2, 2)
        SI = I * NS
        INIT = 0.02
        key = jax.random.key(seed)
        ks = jax.random.split(key, 9)
        f32 = jnp.float32
        return {'hidden_states': jax.random.normal(ks[0], (B, S, H), f32), 'router_w': jax.random.normal(ks[1], (E, H), f32) * INIT, 'gate_w': jax.random.normal(ks[2], (E, H, I), f32) * INIT, 'up_w': jax.random.normal(ks[3], (E, H, I), f32) * INIT, 'down_w': jax.random.normal(ks[4], (E, I, H), f32) * INIT, 's_gate_w': jax.random.normal(ks[5], (H, SI), f32) * INIT, 's_gate_b': jnp.zeros((SI,), f32), 's_up_w': jax.random.normal(ks[6], (H, SI), f32) * INIT, 's_up_b': jnp.zeros((SI,), f32), 's_down_w': jax.random.normal(ks[7], (SI, H), f32) * INIT, 's_down_b': jnp.zeros((H,), f32)}
    _L0_ffn_all = _L0_ffn_setup()
    _L0_ffn_in = {k: v for k, v in _L0_ffn_all.items() if k in ('router_w', 'gate_w', 'up_w', 'down_w', 's_gate_w', 's_gate_b', 's_up_w', 's_up_b', 's_down_w', 's_down_b')}
    del _L0_ffn_all
    return {'x': x, 'itok_BxS_13_99985': itok_BxS_13_99985, 'ctx_2048': ctx_2048, 'L0_attn_Wq': _L0_attn_in['Wq'], 'L0_attn_Wk': _L0_attn_in['Wk'], 'L0_attn_Wv': _L0_attn_in['Wv'], 'L0_attn_Wo': _L0_attn_in['Wo'], 'L0_attn_lambda_q1': _L0_attn_in['lambda_q1'], 'L0_attn_lambda_k1': _L0_attn_in['lambda_k1'], 'L0_attn_lambda_q2': _L0_attn_in['lambda_q2'], 'L0_attn_lambda_k2': _L0_attn_in['lambda_k2'], 'L0_attn_gn_w': _L0_attn_in['gn_w'], 'L0_attn_gn_b': _L0_attn_in['gn_b'], 'L0_ffn_router_w': _L0_ffn_in['router_w'], 'L0_ffn_gate_w': _L0_ffn_in['gate_w'], 'L0_ffn_up_w': _L0_ffn_in['up_w'], 'L0_ffn_down_w': _L0_ffn_in['down_w'], 'L0_ffn_s_gate_w': _L0_ffn_in['s_gate_w'], 'L0_ffn_s_gate_b': _L0_ffn_in['s_gate_b'], 'L0_ffn_s_up_w': _L0_ffn_in['s_up_w'], 'L0_ffn_s_up_b': _L0_ffn_in['s_up_b'], 'L0_ffn_s_down_w': _L0_ffn_in['s_down_w'], 'L0_ffn_s_down_b': _L0_ffn_in['s_down_b']}

def reference(x, itok_BxS_13_99985, ctx_2048, L0_attn_Wq, L0_attn_Wk, L0_attn_Wv, L0_attn_Wo, L0_attn_lambda_q1, L0_attn_lambda_k1, L0_attn_lambda_q2, L0_attn_lambda_k2, L0_attn_gn_w, L0_attn_gn_b, L0_ffn_router_w, L0_ffn_gate_w, L0_ffn_up_w, L0_ffn_down_w, L0_ffn_s_gate_w, L0_ffn_s_gate_b, L0_ffn_s_up_w, L0_ffn_s_up_b, L0_ffn_s_down_w, L0_ffn_s_down_b):
    import jax
    import jax.numpy as jnp

    def _L0_attn_ref(x, Wq, Wk, Wv, Wo, lambda_q1, lambda_k1, lambda_q2, lambda_k2, gn_w, gn_b):
        import jax, jax.numpy as jnp
        import numpy as np
        import math
        D = 256
        H = 16
        KV = 4
        DH = D // H
        REP = H // KV
        LAMBDA_INIT = 0.8 - 0.6 * math.exp(-0.3 * 0)
        ROPE_BASE = 10000.0
        EPS = 1e-05

        def _rope(x, cos, sin):
            x1, x2 = (x[..., ::2], x[..., 1::2])
            c = cos[None, None]
            s = sin[None, None]
            o1 = x1 * c - x2 * s
            o2 = x1 * s + x2 * c
            return jnp.stack([o1, o2], axis=-1).reshape(x.shape)

        def _forward(x, Wq, Wk, Wv, Wo, lambda_q1, lambda_k1, lambda_q2, lambda_k2, gn_w, gn_b):
            B, T, _ = x.shape
            q = (x @ Wq).reshape(B, T, H, 2 * DH).transpose(0, 2, 1, 3)
            k = (x @ Wk).reshape(B, T, KV, 2 * DH).transpose(0, 2, 1, 3)
            v = (x @ Wv).reshape(B, T, KV, 2 * DH).transpose(0, 2, 1, 3)
            q1, q2 = (q[..., :DH], q[..., DH:])
            k1, k2 = (k[..., :DH], k[..., DH:])
            inv = 1.0 / ROPE_BASE ** (jnp.arange(0, DH, 2, dtype=jnp.float32) / DH)
            freqs = jnp.arange(T, dtype=jnp.float32)[:, None] * inv[None, :]
            cos, sin = (jnp.cos(freqs), jnp.sin(freqs))
            q1, q2 = (_rope(q1, cos, sin), _rope(q2, cos, sin))
            k1, k2 = (_rope(k1, cos, sin), _rope(k2, cos, sin))
            k1 = jnp.repeat(k1, REP, axis=1)
            k2 = jnp.repeat(k2, REP, axis=1)
            v = jnp.repeat(v, REP, axis=1)
            mask = jnp.triu(jnp.full((T, T), -jnp.inf, dtype=x.dtype), k=1)[None, None]
            scale = 1.0 / math.sqrt(DH)
            s1 = jnp.einsum('bhtd,bhsd->bhts', q1, k1) * scale + mask
            s2 = jnp.einsum('bhtd,bhsd->bhts', q2, k2) * scale + mask
            a1 = jax.nn.softmax(s1, axis=-1)
            a2 = jax.nn.softmax(s2, axis=-1)
            lam = jnp.exp(jnp.sum(lambda_q1 * lambda_k1)) - jnp.exp(jnp.sum(lambda_q2 * lambda_k2)) + LAMBDA_INIT
            diff = a1 - lam * a2
            out = jnp.einsum('bhts,bhsd->bhtd', diff, v)
            out = out.transpose(0, 2, 1, 3)
            mean = jnp.mean(out, axis=(1, 3), keepdims=True)
            var = jnp.var(out, axis=(1, 3), keepdims=True)
            out = (out - mean) * jax.lax.rsqrt(var + EPS)
            out = out * gn_w.reshape(1, 1, H, 2 * DH) + gn_b.reshape(1, 1, H, 2 * DH)
            out = out.reshape(B, T, 2 * H * DH) * (1.0 - LAMBDA_INIT)
            return out @ Wo
        return _forward(x, Wq, Wk, Wv, Wo, lambda_q1, lambda_k1, lambda_q2, lambda_k2, gn_w, gn_b)

    def _L0_xattn_ref(hidden_states, token_ids, Wg, Wu, Wd):
        import jax, jax.numpy as jnp
        import numpy as np
        B, S, D = (4, 512, 256)
        E = 4
        F = 1024 // E
        VOCAB = 12500
        tokens_per_expert = VOCAB // E
        tid = jnp.clip(token_ids, 0, VOCAB - 1)
        expert_ids = jnp.minimum(tid // tokens_per_expert, E - 1)
        out = jnp.zeros_like(hidden_states)
        for e in range(E):
            g = jax.nn.silu(jnp.einsum('bsd,fd->bsf', hidden_states, Wg[e]))
            u = jnp.einsum('bsd,fd->bsf', hidden_states, Wu[e])
            y = jnp.einsum('bsf,df->bsd', g * u, Wd[e])
            out = jnp.where((expert_ids == e)[..., None], y, out)
        return out

    def _L0_ffn_ref(hidden_states, router_w, gate_w, up_w, down_w, s_gate_w, s_gate_b, s_up_w, s_up_b, s_down_w, s_down_b):
        import jax, jax.numpy as jnp
        import numpy as np
        B, S, H, I, E, TOP_K, NS = (2, 256, 256, 176, 8, 2, 2)
        SI = I * NS
        INIT = 0.02
        b, s, h = hidden_states.shape
        x = hidden_states.reshape(-1, h)
        T = x.shape[0]
        num_experts = router_w.shape[0]
        logits = x @ router_w.T
        probs = jax.nn.softmax(logits.astype(jnp.float32), axis=-1)
        topk_w, topk_idx = jax.lax.top_k(probs, TOP_K)
        topk_w = topk_w / jnp.sum(topk_w, axis=-1, keepdims=True)
        combine = jnp.zeros((T, num_experts), probs.dtype)
        combine = combine.at[jnp.arange(T)[:, None], topk_idx].add(topk_w)

        def expert_step(acc, ws):
            gw, uw, dw, ce = ws
            out = jax.nn.silu(x @ gw) * (x @ uw) @ dw
            return (acc + ce[:, None].astype(out.dtype) * out, None)
        moe_out, _ = jax.lax.scan(expert_step, jnp.zeros_like(x), (gate_w, up_w, down_w, combine.T))
        shared = jax.nn.silu(x @ s_gate_w + s_gate_b) * (x @ s_up_w + s_up_b) @ s_down_w + s_down_b
        return (moe_out + shared).reshape(b, s, h)
    x = x + _L0_attn_ref(_layernorm(x, axis=-1), L0_attn_Wq, L0_attn_Wk, L0_attn_Wv, L0_attn_Wo, L0_attn_lambda_q1, L0_attn_lambda_k1, L0_attn_lambda_q2, L0_attn_lambda_k2, L0_attn_gn_w, L0_attn_gn_b)
    x = x + _L0_xattn_ref(_layernorm(x, axis=-1), itok_BxS_13_99985, ctx_2048, ctx_2048, ctx_2048)
    x = x + _L0_ffn_ref(_layernorm(x, axis=-1), L0_ffn_router_w, L0_ffn_gate_w, L0_ffn_up_w, L0_ffn_down_w, L0_ffn_s_gate_w, L0_ffn_s_gate_b, L0_ffn_s_up_w, L0_ffn_s_up_b, L0_ffn_s_down_w, L0_ffn_s_down_b)
    return x

_drawn_inputs = setup_inputs


def setup_inputs(seed=0):
    import zlib

    import numpy as np

    out = dict(_drawn_inputs(seed))
    spreads = {'L0_attn_gn_w': (1.0, 0.2),
     'L0_attn_gn_b': (0.0, 0.1),
     'L0_ffn_s_gate_b': (0.0, 0.8),
     'L0_ffn_s_up_b': (0.0, 0.8),
     'L0_ffn_s_down_b': (0.0, 0.267)}
    factors = {'L0_attn_lambda_q1': 8.0,
     'L0_attn_lambda_k1': 6.975,
     'L0_attn_lambda_q2': 8.0,
     'L0_attn_lambda_k2': 8.0,
     'L0_ffn_router_w': 7.039,
     'L0_ffn_gate_w': 6.17,
     'L0_ffn_up_w': 6.089,
     'L0_ffn_down_w': 6.099,
     'L0_ffn_s_gate_w': 2.948,
     'L0_ffn_s_up_w': 2.914,
     'L0_ffn_s_down_w': 2.775}
    for name, (base, spread) in spreads.items():
        noise = np.random.default_rng([zlib.crc32(name.encode()), seed]).standard_normal(out[name].shape)
        drawn = base * np.exp(spread * noise) if base else spread * noise
        out[name] = jnp.asarray(drawn.astype(out[name].dtype))
    for name, factor in factors.items():
        out[name] = (out[name] * factor).astype(out[name].dtype)
    return out
```

```python
from contextlib import ExitStack

import numpy as np

import concourse.bass as bass
from concourse import mybir

F32 = mybir.dt.float32
F32R = mybir.dt.float32r
BF16 = mybir.dt.bfloat16
I32 = mybir.dt.int32
U32 = mybir.dt.uint32
ALU = mybir.AluOpType
ACT = mybir.ActivationFunctionType
AX_X = mybir.AxisListType.X

P = 128
NB, T, D = 4, 256, 256
NT, ND = T // P, D // P
H, KV, DH = 16, 4, 16
REP = H // KV
VW = 2 * DH
QC, KC = H * VW, KV * VW
NG = KV
LAMBDA_INIT = 0.2
EPS = 1e-5
E1, VOCAB = 4, 12500
E2, INNER = 8, 176
SI = 2 * INNER
HID = E2 * INNER + SI
NCH = (HID + P - 1) // P
LAST = HID - (NCH - 1) * P
NGR = 1 + E2
MASKED = -1.0e30

C_ID, C_BLK, C_MASK, C_COS, C_SIN = 0, P, 2 * P, 3 * P, 3 * P + NT * DH
C_IOTA = C_SIN + NT * DH
C_ROW0, C_ROW1, C_EPS, C_HALF = C_IOTA + 8, C_IOTA + 9, C_IOTA + 10, C_IOTA + 11
C_TWO = C_IOTA + 12
NCONST = C_TWO + P

UNITS = [u for g in range(NG) for u in ((g, 0, 0, 4), (g, 1, 0, 2), (g, 1, 2, 2))]
NU = len(UNITS)
HGROUPS = [(0, 4), (4, 4), (8, 4), (12, NCH - 12)]


class Signal:

    def __init__(self, sem, per):
        self.sem, self.per = sem, per

    def __call__(self, i, k):
        return self.sem, (i + 1) * self.per + k


def three_pass(pe, out, lhs_h, lhs_l, rhs_h, rhs_l, start, stop):
    pe.matmul(out, lhs_h, rhs_l, start=start, stop=False, skip_group_check=True)
    pe.matmul(out, lhs_h, rhs_h, start=False, stop=False, skip_group_check=True)
    return pe.matmul(out, lhs_l, rhs_h, start=False, stop=stop, skip_group_check=True)


def build(nc, a, out):
    ctx = ExitStack()
    with ctx:
        def sb(name, shape, dt=F32):
            return ctx.enter_context(nc.sbuf_tensor(name, shape, dt))

        def psum(name, shape):
            return ctx.enter_context(nc.psum_tensor(name, shape, F32))

        def sem(name):
            return ctx.enter_context(nc.semaphore(name))

        signals = []

        def sig(name, per):
            signals.append(Signal(sem(name), per))
            return signals[-1]

        wqkv_h, wqkv_l = (sb(n, [P, ND, QC + 2 * KC], F32R) for n in ("wqkv_h", "wqkv_l"))
        wo_h, wo_l = (sb(n, [P, NG, D], F32R) for n in ("wo_h", "wo_l"))
        ct_h, ct_l = (sb(n, [P, ND, E1, D], F32R) for n in ("ct_h", "ct_l"))
        gu_h, gu_l = (sb(n, [P, E2, ND, 2 * INNER], F32R) for n in ("gu_h", "gu_l"))
        sg_h, sg_l = (sb(n, [P, ND, SI + E2 + SI], F32R) for n in ("sg_h", "sg_l"))
        dn_h, dn_l = (sb(n, [P, NCH, D], F32R) for n in ("dn_h", "dn_l"))
        bias_r = sb("bias_r", [P, 2 * SI + D], F32R)

        const = sb("const", [P, NCONST])
        ident = const[:, C_ID:C_ID + P]
        ident_r = sb("ident_r", [P, P], F32R)
        two_r = sb("two_r", [P, P], F32R)
        ident_b = sb("ident_b", [P, P], BF16)
        mask_b = sb("mask_b", [P, 4, P], BF16)
        lam_in = sb("lam_in", [P, 4, DH])
        lam = sb("lam", [P, 8])
        gn_wb = sb("gn_wb", [P, 2, NG])

        x_in = sb("x_in", [P, NT, D])
        x_res = sb("x_res", [P, NT, D])
        x1 = sb("x1", [P, NT, D])
        stat_a = sb("stat_a", [P, NT, 6])
        mv_a = sb("mv_a", [P, NT, 2])
        rstd_a = sb("rstd_a", [P, NT, 2])
        xt_kt = sb("xt_kt", [P, 4 * T], F32R)
        xta_h = xt_kt[:, 0:2 * T].rearrange("p (c t) -> p c t", c=ND)
        xta_l = xt_kt[:, 2 * T:4 * T].rearrange("p (c t) -> p c t", c=ND)
        kt = xt_kt[:, :].rearrange("p (g t) -> p g t", g=KV)
        probs = sb("probs", [P, 2, 1024])
        rot = probs[:, :, :].rearrange("p a b -> p (a b)")
        qk = sb("qk", [P, NT, QC + KC])
        stack = sb("stack", [P, 2, 8, 4, DH], F32R)
        qt = sb("qt", [P, 2, 4, P], F32R)
        vpad = sb("vpad", [P, 2, NT, 96 + KV * P], F32R)
        nmax = sb("nmax", [P, 2, 8])
        rsum = sb("rsum", [P, 2, 8])
        rinv = sb("rinv", [P, 2, 8])
        dt_h, dt_l = (sb(n, [P, 2, 4 * P], F32R) for n in ("dt_h", "dt_l"))
        y_h = qt[:, :, :, :].rearrange("p a h t -> p (a h t)").rearrange("p (g t) -> p g t", g=NG)
        y_l = dt_h[:, :, :].rearrange("p a t -> p (a t)").rearrange("p (g t) -> p g t", g=NG)
        ao = sb("ao", [P, NG, T])
        gstat = sb("gstat", [P, NG, 6])
        gmv = sb("gmv", [P, NG, 2])
        gtmp = sb("gtmp", [P, 6, NG])

        xb = sb("xb", [P, NT, D])
        stat_b = sb("stat_b", [P, NT, 6])
        mv_b = sb("mv_b", [P, NT, 2])
        rstd_b = sb("rstd_b", [P, NT, 2])
        xtb_h, xtb_l = (sb(n, [P, ND, T], F32R) for n in ("xtb_h", "xtb_l"))
        hid = sb("hid", [P, HID])
        z = hid[:, 0:2 * D].rearrange("p (t d) -> p t d", t=NT)
        zt = hid[:, 2 * D:4 * D].rearrange("p (t d) -> p t d", t=NT)
        xnb = hid[:, 4 * D:6 * D].rearrange("p (t d) -> p t d", t=NT)
        ht_h, ht_l = (sb(n, [P, 2, 4 * P], F32R) for n in ("ht_h", "ht_l"))
        act_g = sb("act_g", [P, 2, SI])
        tok = sb("tok", [P, NT], I32)
        routed = sb("routed", [P, E1 - 1, NT], U32)
        rt = sb("rt", [P, 8, 8])
        top_i = sb("top_i", [P, 8], U32)
        comb = sb("comb", [P, E2])

        s_bank = psum("s_bank", [P, 4, 512])
        tr_bank = psum("tr_bank", [P, 512])
        o_bank = psum("o_bank", [P, 512])
        b_bank = psum("b_bank", [P, 2, 512])

        NPIECE = 23
        w_in = [sem("w_in0"), sem("w_in1")]
        s_const, s_lam, s_gn, s_bias = sem("s_const"), sem("s_lam"), sem("s_gn"), sem("s_bias")
        w_high, w_low, w_set = sem("w_high"), sem("w_low"), sem("w_set")
        c_mm = sem("c_mm")
        dve_passed = sem("dve_passed")
        set_v, set_a = sem("set_v"), sem("set_a")

        x_loaded, tok_loaded = sig("x_loaded", 16), sig("tok_loaded", 16)
        a_res, a_stat, a_aggr, a_rstd, a_xn = (sig("a_res", 1), sig("a_stat", 2), sig("a_aggr", 2),
                                               sig("a_rstd", 2), sig("a_xn", 2))
        a_xt_mm, a_xt_h, a_xt_l = sig("a_xt_mm", 1), sig("a_xt_h", 1), sig("a_xt_l", 1)
        a_qkv, a_mul, a_rot = sig("a_qkv", 2), sig("a_mul", 4), sig("a_rot", 4)
        a_vh, a_vl = sig("a_vh", 2), sig("a_vl", 2)
        a_st_h, a_st_l, a_st_mm, a_st = sig("a_st_h", 10), sig("a_st_l", 10), sig("a_st_mm", 10), sig("a_st", 10)
        a_s, a_max, a_exp = sig("a_s", NU), sig("a_max", NU), sig("a_exp", NU)
        a_inv, a_rho, a_p1, a_diff = sig("a_inv", NU), sig("a_rho", NU), sig("a_p1", NU), sig("a_diff", NU)
        a_dt_mm, a_dt_h, a_dt_l, a_pv = (sig("a_dt_mm", NU), sig("a_dt_h", NU), sig("a_dt_l", NU),
                                         sig("a_pv", NU))
        a_o, a_gst, a_gag = sig("a_o", NG), sig("a_gst", NG), sig("a_gag", NG)
        a_gmm, a_gv, a_gp = sig("a_gmm", 2), sig("a_gv", 5), sig("a_gp", 2)
        a_y, a_yh, a_yl = sig("a_y", NG), sig("a_yh", NG), sig("a_yl", NG)
        a_wo, a_x1 = sig("a_wo", 1), sig("a_x1", 1)

        b_x, b_stat, b_aggr, b_rstd, b_xn = (sig("b_x", 1), sig("b_stat", 4), sig("b_aggr", 4),
                                             sig("b_rstd", 4), sig("b_xn", 4))
        NTR = 3 + NT * len(HGROUPS)
        b_tr, b_tr_h, b_tr_l = sig("b_tr", NTR), sig("b_tr_h", NTR), sig("b_tr_l", NTR)
        b_mask, b_zy, b_e0, b_sel = sig("b_mask", 3), sig("b_zy", 4), sig("b_e0", 4), sig("b_sel", 12)
        b_zz, b_th, b_p, b_x2 = sig("b_zz", 2), sig("b_th", 2), sig("b_p", 2), sig("b_x2", 2)
        b_up, b_tanh, b_a, b_hid = (sig("b_up", NT * NGR), sig("b_tanh", NT * NGR), sig("b_a", NT * NGR),
                                    sig("b_hid", NT * NGR))
        RV = 12
        b_rv, b_re = sig("b_rv", NT * RV), sig("b_re", NT)
        b_down, b_out, b_store = sig("b_down", NT), sig("b_out", NT), sig("b_store", 16)

        def rows(w):
            return w.rearrange("(c p) n -> c p n", p=P)

        stage = [hid[:, 0:880], hid[:, 880:1760]]
        pieces = []
        for c in range(ND):
            pieces.append(([(wqkv_h[:, c, 0:QC], wqkv_l[:, c, 0:QC], 0, QC, P, 1.0),
                            (wqkv_h[:, c, QC:QC + KC], wqkv_l[:, c, QC:QC + KC], QC, KC, P, DH ** -0.5),
                            (wqkv_h[:, c, QC + KC:], wqkv_l[:, c, QC + KC:], QC + KC, KC, P, 1.0)],
                           [(0, QC, P, rows(a["L0_attn_Wq"])[c]), (QC, KC, P, rows(a["L0_attn_Wk"])[c]),
                            (QC + KC, KC, P, rows(a["L0_attn_Wv"])[c])]))
        for c in range(0, NG, 2):
            pieces.append(([(wo_h[:, c:c + 2, :], wo_l[:, c:c + 2, :], 0, 2 * D, P, 1.0)],
                           [(D * k, D, P, rows(a["L0_attn_Wo"])[c + k]) for k in range(2)]))
        for c in range(ND):
            pieces.append(([(sg_h[:, c, :], sg_l[:, c, :], 0, 2 * SI + E2, P, 1.0)],
                           [(0, SI, P, rows(a["L0_ffn_s_gate_w"])[c]),
                            (SI, E2, P, a["L0_ffn_router_w"].rearrange("e (c p) -> c p e", p=P)[c]),
                            (SI + E2, SI, P, rows(a["L0_ffn_s_up_w"])[c])]))
        for e in range(E2):
            pieces.append(([(gu_h[:, e, :, :], gu_l[:, e, :, :], 0, 4 * INNER, P, 1.0)],
                           [(k * INNER, INNER, P, rows(w[e])[k // 2])
                            for k, w in enumerate((a["L0_ffn_gate_w"], a["L0_ffn_up_w"]) * 2)]))
        down = a["L0_ffn_down_w"].rearrange("e i h -> (e i) h")
        down = rows(down)
        full = E2 * INNER // P
        for c in range(0, full, 3):
            n = min(3, full - c)
            pieces.append(([(dn_h[:, c:c + n, :], dn_l[:, c:c + n, :], 0, n * D, P, 1.0)],
                           [(D * k, D, P, down[c + k]) for k in range(n)]))
        s_down = a["L0_ffn_s_down_w"]
        n = NCH - 1 - full
        pieces.append(([(dn_h[:, full:full + n, :], dn_l[:, full:full + n, :], 0, n * D, P, 1.0),
                        (dn_h[0:LAST, NCH - 1, :], dn_l[0:LAST, NCH - 1, :], n * D, D, LAST, 1.0)],
                       [(D * k, D, P, s_down[k * P:(k + 1) * P, :]) for k in range(n)]
                       + [(n * D, D, LAST, s_down[n * P:SI, :])]))
        NW = len(pieces)
        landed = [0, 0]
        piece_in = []
        for k, (_, loads) in enumerate(pieces):
            landed[k % 2] += 16 * len(loads)
            piece_in.append(landed[k % 2])
        parts_done = [sum(len(p[0]) for p in pieces[:k + 1]) for k in range(NW)]
        ctx_in = []
        for e in range(E1):
            landed[(NW + e) % 2] += 16
            ctx_in.append(landed[(NW + e) % 2])
        NPARTS = parts_done[-1]

        def staged(k, off, cols, r):
            return stage[k % 2][0:r, off:off + cols]

        def like(ap, to):
            return ap.rearrange("p (a b) -> p a b", a=to.shape[1]) if len(to.shape) == 3 else ap

        x_dram = a["x"].rearrange("b (t p) d -> b p t d", p=P)
        out_dram = out.rearrange("b (t p) d -> b p t d", p=P)
        tok_dram = a["itok_BxS_13_99985"].rearrange("b (t p) -> b p t", p=P)
        SETV, SETA = 22, 3

        def stack_parts(j):
            w = j - 2
            if j < 2:
                src, slots = qk[:, j, QC:QC + KC], (slice(0, 2), slice(2, 4))
            else:
                src, slots = qk[:, w % 2, (w // 2) * P:(w // 2 + 1) * P], (slice(0, 4, 2), slice(1, 4, 2))
            src = src.rearrange("p (m d) -> p m d", d=DH).unsqueeze(2).to_broadcast([P, 8, 2, DH])
            return src, stack[:, j % 2, :, slots[0], :], stack[:, j % 2, :, slots[1], :]

        block = ctx.enter_context(nc.Block())

        @block.sync
        def _(sp):
            sp.dma_start(const[:, :], a["consts"]).then_inc(s_const, 16)
            for s in signals:
                sp.sem_inc(s.sem, s.per)
            for k, (_, loads) in enumerate(pieces):
                if k >= 2:
                    sp.wait_ge(w_low, parts_done[k - 2])
                for off, cols, r, src in loads:
                    sp.dma_start(staged(k, off, cols, r), src, allow_slow_non_contiguous=cols == E2).then_inc(w_in[k % 2], 16)
                if k == 1:
                    for j, name in enumerate(("q1", "k1", "q2", "k2")):
                        v = a["L0_attn_lambda_" + name].rearrange("(o d) -> o d", o=1)
                        sp.dma_start(lam_in[:, j, :], v.to_broadcast([P, DH])).then_inc(s_lam, 16)
                    for j, name in enumerate(("w", "b")):
                        sp.dma_start(gn_wb[:, j, :], a["L0_attn_gn_" + name].rearrange("(g p) -> p g", p=P),
                                     allow_slow_non_contiguous=True).then_inc(s_gn, 16)
            for e in range(E1):
                k = NW + e
                if e < 2:
                    sp.wait_ge(w_low, parts_done[k - 2])
                else:
                    sp.wait_ge(c_mm, e - 1)
                sp.dma_start(staged(k, 0, 2 * D, P).rearrange("p (c d) -> p c d", c=ND),
                             a["ctx_2048"][e].rearrange("(c p) d -> p c d", p=P)).then_inc(w_in[k % 2], 16)
            off = 0
            for name in ("s_gate_b", "s_up_b", "s_down_b"):
                v = a["L0_ffn_" + name].rearrange("(o n) -> o n", o=1)
                n = v.shape[1]
                sp.dma_start(probs[0:2, 0, off:off + n], v.to_broadcast([2, n])).then_inc(s_bias, 16)
                off += n
            with sp.Fori(0, NB) as i:
                sp.wait_ge(*a_xt_mm(i, 0))
                sp.dma_start(x_in[:, :, :], x_dram[i]).then_inc(x_loaded.sem, 16)
                sp.wait_ge(*b_mask(i, 0))
                sp.dma_start(tok[:, :], tok_dram[i], allow_slow_non_contiguous=True).then_inc(tok_loaded.sem, 16)
                sp.wait_ge(*b_out(i, NT))
                sp.dma_start(out_dram[i], xb[:, :, :]).then_inc(b_store.sem, 16)
            sp.wait_ge(*b_store(NB, 0))

        @block.gpsimd
        def _(pool):
            def a_norm(i):
                pool.wait_ge(*a_aggr(i, 2))
                pool.tensor_tensor(rstd_a[:, :, 0], mv_a[:, :, 1], const[:, C_EPS:C_EPS + 1].to_broadcast([P, NT]),
                                   ALU.add).then_inc(a_rstd.sem, 1)
                pool.wait_ge(*a_rstd(i, 1))
                pool.tensor_tensor(rstd_a[:, :, 1], rstd_a[:, :, 0],
                                   const[:, C_HALF:C_HALF + 1].to_broadcast([P, NT]),
                                   ALU.pow).then_inc(a_rstd.sem, 1)

            def a_rotate(i, t):
                n = QC + KC
                c = rot[:, 0:n].rearrange("p (m two) -> p m two", two=2)
                s = rot[:, n:2 * n].rearrange("p (m two) -> p m two", two=2)
                o = qk[:, t, :].rearrange("p (m two) -> p m two", two=2)
                pool.wait_ge(*a_mul(i, 2 * t + 2))
                if t == 0:
                    pool.wait_ge(*a_st_l(i, 0))
                pool.tensor_tensor(o[:, :, 0], c[:, :, 0], s[:, :, 1], ALU.subtract).then_inc(a_rot.sem, 1)
                pool.tensor_tensor(o[:, :, 1], c[:, :, 1], s[:, :, 0], ALU.add).then_inc(a_rot.sem, 1)

            def a_stack(i, j):
                src, hi, lo = stack_parts(j)
                pool.wait_ge(*a_st_h(i, j + 1))
                pool.tensor_tensor(lo, src, hi.bitcast(F32), ALU.subtract).then_inc(a_st_l.sem, 1)

            def a_scale(i, u):
                g, t, h0, nh = UNITS[u]
                p1 = probs[:, u % 2, 0:512].rearrange("p (h s) -> p h s", h=nh)
                pool.wait_ge(*a_exp(i, u + 1))
                pool.wait_ge(*a_inv(i, u + 1))
                pool.tensor_tensor(p1, p1, rinv[:, u % 2, 0:nh].unsqueeze(2).to_broadcast([P, nh, 512 // nh]),
                                   ALU.mult).then_inc(a_p1.sem, 1)

            def a_group(i):
                pool.wait_ge(*a_gv(i, 5))
                pool.tensor_tensor(gtmp[:, 4, :], gtmp[:, 3, :], const[:, C_HALF:C_HALF + 1].to_broadcast([P, NG]),
                                   ALU.pow).then_inc(a_gp.sem, 1)
                pool.wait_ge(*a_gp(i, 1))
                pool.tensor_tensor(gtmp[:, 5, :], gtmp[:, 4, :], gn_wb[:, 0, :], ALU.mult).then_inc(a_gp.sem, 1)

            def b_norm(i, k):
                pool.wait_ge(*b_aggr(i, 2 * k + 2))
                pool.tensor_tensor(rstd_b[:, :, 0], mv_b[:, :, 1], const[:, C_EPS:C_EPS + 1].to_broadcast([P, NT]),
                                   ALU.add).then_inc(b_rstd.sem, 1)
                pool.wait_ge(*b_rstd(i, 2 * k + 1))
                pool.tensor_tensor(rstd_b[:, :, 1], rstd_b[:, :, 0],
                                   const[:, C_HALF:C_HALF + 1].to_broadcast([P, NT]),
                                   ALU.pow).then_inc(b_rstd.sem, 1)

            def b_square(i, t):
                pool.wait_ge(*b_th(i, t + 1))
                pool.tensor_tensor(z[:, t, :], z[:, t, :], z[:, t, :], ALU.mult).then_inc(b_zz.sem, 1)

            pool.wait_ge(s_const, 16)
            pool.wait_ge(set_v, SETV)
            with pool.Fori(0, NB) as i:
                a_norm(i)
                for t in range(NT):
                    a_rotate(i, t)
                for j in range(4):
                    a_stack(i, j)
                for u in range(NU):
                    a_scale(i, u)
                    if u % 3 == 1 and u < NU - 3:
                        a_stack(i, 4 + 2 * (u // 3))
                        a_stack(i, 5 + 2 * (u // 3))
                a_group(i)
                b_norm(i, 0)
                for t in range(NT):
                    b_square(i, t)
                b_norm(i, 1)

        @block.scalar
        def _(act):
            act.preload_act_table(ACT.Exp)
            n = 0
            for k, (parts, _) in enumerate(pieces):
                act.wait_ge(w_in[k % 2], piece_in[k])
                for hi, lo, off, cols, r, scale in parts:
                    act.activation(hi, like(staged(k, off, cols, r), hi), ACT.Copy, scale=scale).then_inc(w_high, 1)
            for e in range(E1):
                act.wait_ge(c_mm, e + 1)
                act.activation(ct_h[:, :, e, :], s_bank[:, e, :].rearrange("p (c f) -> p c f", c=ND), ACT.Copy
                               ).then_inc(w_high, 1)
            act.wait_ge(set_v, 5)
            act.activation(lam[:, 2:4], lam[:, 0:2], ACT.Exp).then_inc(set_a, 1)

            def a_keep(i):
                act.wait_ge(*x_loaded(i, 16))
                act.wait_ge(*a_x1(i, 0))
                act.activation(x_res[:, :, :], x_in[:, :, :], ACT.Copy).then_inc(a_res.sem, 1)

            def a_xt(i):
                act.wait_ge(*a_xt_mm(i, 1))
                act.wait_ge(*a_s(i, 0))
                act.activation(xt_kt[:, 0:2 * T], tr_bank[:, :], ACT.Copy).then_inc(a_xt_h.sem, 1)

            def a_values(i, t):
                act.wait_ge(*a_qkv(i, t + 1))
                act.wait_ge(*a_pv(i, 0))
                v = s_bank[:, 2 * t + 1, KC:2 * KC].rearrange("p (g d) -> p g d", g=KV)
                act.activation(vpad[:, 0, t, 96:].rearrange("p (g d) -> p g d", g=KV)[:, :, 0:VW], v, ACT.Copy
                               ).then_inc(a_vh.sem, 1)

            def a_stack(i, j):
                act.wait_ge(*a_st_mm(i, j + 1))
                if j < 2:
                    dst, w = kt[:, :, j * P:(j + 1) * P], 0
                else:
                    dst, w = qt[:, j % 2, :, :], j - 2
                    if w >= 2:
                        act.wait_ge(*a_s(i, 3 * ((w - 2) // 2) + (3 if w % 2 else 1)))
                    else:
                        act.wait_ge(*a_wo(i, 0))
                act.activation(dst, tr_bank[:, :].rearrange("p (g s) -> p g s", g=4), ACT.Copy
                               ).then_inc(a_st.sem, 1)

            def a_exps(i, u):
                g, t, h0, nh = UNITS[u]
                n = 512 // nh
                act.wait_ge(*a_max(i, u + 1))
                if u >= 2:
                    act.wait_ge(*a_dt_mm(i, u - 1))
                else:
                    act.wait_ge(*a_rot(i, 4))
                for half in range(2):
                    for h in range(nh):
                        o = half * 512 + h * n
                        j = half * nh + h
                        last = act.activation(probs[:, u % 2, o:o + n], s_bank[:, 2 * (u % 2) + half, h * n:(h + 1) * n],
                                              ACT.Exp, bias=nmax[:, u % 2, j:j + 1],
                                              accum_out=rsum[:, u % 2, j:j + 1])
                last.then_inc(a_exp.sem, 1)

            def a_diff_h(i, u):
                act.wait_ge(*a_dt_mm(i, u + 1))
                if u >= 2:
                    act.wait_ge(*a_pv(i, u - 1))
                else:
                    act.wait_ge(*a_wo(i, 0))
                act.activation(dt_h[:, u % 2, :], tr_bank[:, :], ACT.Copy).then_inc(a_dt_h.sem, 1)

            def a_out(i, g):
                act.wait_ge(*a_pv(i, 3 * g + 3))
                act.wait_ge(*a_yl(i, 0))
                act.activation(ao[:, g, :], o_bank[:, 0:T], ACT.Copy).then_inc(a_o.sem, 1)

            def a_y_high(i, g):
                act.wait_ge(*a_y(i, g + 1))
                act.activation(y_h[:, g, :], ao[:, g, :], ACT.Identity, bias=gn_wb[:, 1, g:g + 1]
                               ).then_inc(a_yh.sem, 1)

            def b_high(i, k, dst, src, r=P):
                act.wait_ge(*b_tr(i, k + 1))
                act.activation(dst, src, ACT.Copy).then_inc(b_tr_h.sem, 1)

            def b_first(i, k):
                act.wait_ge(*b_zy(i, k + 1))
                act.activation(z[:, k % 2, :], b_bank[:, 0, 0:D], ACT.Copy).then_inc(b_e0.sem, 1)

            def b_tanh_z(i, t):
                act.wait_ge(*b_sel(i, 3 * t + 3))
                act.activation(zt[:, t, :], z[:, t, :], ACT.Tanh, scale=0.5).then_inc(b_th.sem, 1)

            def b_router(i, t):
                act.wait_ge(*b_rv(i, RV * t + 1))
                act.activation(rt[:, 1, :], b_bank[:, 0, SI:SI + E2], ACT.Exp, bias=rt[:, 0, 0:1],
                               accum_out=rt[:, 0, 1:2]).then_inc(b_re.sem, 1)

            def b_act(i, t, n):
                k = NGR * t + n
                cols = SI if n == 0 else INNER
                act.wait_ge(*b_up(i, k + 1))
                if k >= 2:
                    act.wait_ge(*b_hid(i, k - 1))
                bank = 0 if n == 0 else n % 2
                act.activation(act_g[:, k % 2, 0:cols], b_bank[:, bank, 0:cols], ACT.Tanh, scale=0.5
                               ).then_inc(b_tanh.sem, 1)

            act.wait_ge(w_set, 1)
            with act.Fori(0, NB) as i:
                a_keep(i)
                a_xt(i)
                for t in range(NT):
                    a_values(i, t)
                for j in range(4):
                    a_stack(i, j)
                for u in range(NU):
                    a_exps(i, u)
                    a_diff_h(i, u)
                    g, sub = u // 3, u % 3
                    if sub == 2:
                        if g < NG - 1:
                            a_stack(i, 2 * g + 4)
                            a_stack(i, 2 * g + 5)
                        a_out(i, g)
                for g in range(NG):
                    a_y_high(i, g)
                b_high(i, 0, xtb_h[:, :, :], b_bank[:, 0, :].rearrange("p (c t) -> p c t", c=ND))
                for t in range(NT):
                    b_first(i, t)
                    b_tanh_z(i, t)
                b_high(i, 1, xtb_h[:, :, :], b_bank[:, 0, :].rearrange("p (c t) -> p c t", c=ND))
                for t in range(NT):
                    b_first(i, 2 + t)
                b_high(i, 2, xtb_h[:, :, :], b_bank[:, 0, :].rearrange("p (c t) -> p c t", c=ND))
                for t in range(NT):
                    b_router(i, t)
                    for n in range(NGR):
                        b_act(i, t, n)
                    for j, (c0, n) in enumerate(HGROUPS):
                        b_high(i, 3 + 4 * t + j, ht_h[:, j % 2, 0:n * P], b_bank[:, 0, 0:n * P])

        @block.vector
        def _(dve):
            done = [0]

            def step(ins):
                ins.then_inc(set_v, 1)
                done[0] += 1

            def after():
                dve.wait_ge(set_v, done[0])

            dve.wait_ge(s_lam, 64)
            step(dve.tensor_tensor(lam_in[:, 0, :], lam_in[:, 0, :], lam_in[:, 1, :], ALU.mult))
            step(dve.tensor_tensor(lam_in[:, 2, :], lam_in[:, 2, :], lam_in[:, 3, :], ALU.mult))
            after()
            step(dve.tensor_reduce(lam[:, 0:2], lam_in[:, 0:4:2, :], AX_X, ALU.add))
            dve.wait_ge(s_const, 16)
            step(dve.tensor_copy(ident_r[:, :], ident))
            step(dve.tensor_copy(ident_b[:, :], ident))
            step(dve.tensor_copy(two_r[:, :], const[:, C_TWO:C_TWO + P]))
            for j in range(4):
                step(dve.tensor_copy(mask_b[:, j, :], const[:, C_MASK:C_MASK + P]))
            step(dve.memset(vpad[:, :, :, :].bitcast(F32), 0.0))
            step(dve.memset(bias_r[:, :].bitcast(F32), 0.0))
            dve.wait_ge(s_gn, 32)
            step(dve.tensor_scalar(gn_wb[:, :, :], gn_wb[:, :, :], 1.0 - LAMBDA_INIT, None, ALU.mult))
            n = 0
            for k, (parts, _) in enumerate(pieces):
                dve.wait_ge(w_in[k % 2], piece_in[k])
                for hi, lo, off, cols, r, scale in parts:
                    n += 1
                    dve.wait_ge(w_high, n)
                    src = like(staged(k, off, cols, r), hi)
                    dve.scalar_tensor_tensor(lo, src, scale, hi.bitcast(F32), ALU.mult, ALU.subtract
                                             ).then_inc(w_low, 1)
            for e in range(E1):
                n += 1
                dve.wait_ge(w_high, n)
                dve.tensor_tensor(ct_l[:, :, e, :], s_bank[:, e, :].rearrange("p (c f) -> p c f", c=ND),
                                  ct_h[:, :, e, :].bitcast(F32), ALU.subtract).then_inc(w_low, 1)
            dve.wait_ge(set_a, 1)
            step(dve.tensor_tensor(lam[:, 4:5], lam[:, 3:4], lam[:, 2:3], ALU.subtract))
            after()
            step(dve.tensor_scalar(lam[:, 5:6], lam[:, 4:5], -LAMBDA_INIT, None, ALU.add))
            nb = 2 * SI + D
            raw, hi2 = probs[0:2, 0, 0:nb], bias_r[0:2, :]
            low = probs[0:2, 1, 0:nb]
            dve.wait_ge(s_bias, 48)
            after()
            step(dve.tensor_copy(hi2, raw))
            after()
            step(dve.tensor_tensor(low, raw, hi2.bitcast(F32), ALU.subtract))
            after()
            step(dve.tensor_scalar(low, low, const[0:2, C_ROW1:C_ROW1 + 1], None, ALU.mult))
            after()
            step(dve.tensor_scalar(raw, hi2.bitcast(F32), const[0:2, C_ROW0:C_ROW0 + 1], None, ALU.mult))
            after()
            step(dve.tensor_tensor(hi2, raw, low, ALU.add))
            after()
            dve.wait_ge(w_low, NPARTS + E1)
            step(dve.tensor_scalar(lam[:, 6:7], lam[:, 5:6], 1.0, None, ALU.mult))
            while done[0] < SETV - 1:
                step(dve.tensor_scalar(lam[:, 7:8], lam[:, 5:6], 1.0, None, ALU.mult))
                after()
            step(dve.tensor_scalar(rt[:, 7, :], const[:, C_IOTA:C_IOTA + 8], 1.0, None, ALU.mult))
            assert done[0] == SETV, done[0]
            after()
            dve.tensor_scalar(lam[:, 7:8], lam[:, 5:6], 1.0, None, ALU.mult).then_inc(w_set, 1)
            dve.wait_ge(w_set, 1)
            neg_lam = lam[:, 5:6]
            iota = const[:, C_IOTA:C_IOTA + 8]

            def settled():
                dve.sem_inc(dve_passed, 1)

            def a_norm(i):
                dve.wait_ge(*x_loaded(i, 16))
                for t in range(NT):
                    dve.bn_stats(stat_a[:, t, :], x_in[:, t, :]).then_inc(a_stat.sem, 1)
                for t in range(NT):
                    dve.wait_ge(*a_stat(i, t + 1))
                    settled()
                    dve.bn_aggr(mv_a[:, t, :], stat_a[:, t, :]).then_inc(a_aggr.sem, 1)
                dve.wait_ge(*a_res(i, 1))
                dve.wait_ge(*a_rstd(i, 2))
                for t in range(NT):
                    dve.tensor_scalar(x_in[:, t, :], x_in[:, t, :], mv_a[:, t, 0:1], rstd_a[:, t, 1:2],
                                      ALU.subtract, ALU.mult).then_inc(a_xn.sem, 1)

            def a_xt(i):
                dve.wait_ge(*a_xt_h(i, 1))
                dve.tensor_tensor(xt_kt[:, 2 * T:4 * T], tr_bank[:, :], xt_kt[:, 0:2 * T].bitcast(F32), ALU.subtract
                                  ).then_inc(a_xt_l.sem, 1)

            def a_rotate(i, t):
                n = QC + KC
                x = s_bank[:, 2 * t:2 * t + 2, :].rearrange("p b c -> p (b c)")[:, 0:n]
                dve.wait_ge(*a_qkv(i, t + 1))
                dve.wait_ge(*a_vh(i, t + 1))
                if t == 0:
                    dve.wait_ge(*a_dt_mm(i, 0))
                else:
                    dve.wait_ge(*a_rot(i, 2))
                for k, c0 in enumerate((C_COS, C_SIN)):
                    tab = const[:, c0 + t * DH:c0 + (t + 1) * DH].unsqueeze(1).to_broadcast([P, n // DH, DH])
                    dve.tensor_tensor(rot[:, k * n:(k + 1) * n].rearrange("p (m d) -> p m d", d=DH),
                                      x.rearrange("p (m d) -> p m d", d=DH), tab, ALU.mult).then_inc(a_mul.sem, 1)
                v = s_bank[:, 2 * t + 1, KC:2 * KC].rearrange("p (g d) -> p g d", g=KV)
                vh, vl = (vpad[:, s, t, 96:].rearrange("p (g d) -> p g d", g=KV)[:, :, 0:VW] for s in range(2))
                dve.wait_ge(*a_pv(i, 0))
                dve.tensor_tensor(vl, v, vh.bitcast(F32), ALU.subtract).then_inc(a_vl.sem, 1)

            def a_stack(i, j):
                src, hi, lo = stack_parts(j)
                dve.wait_ge(*a_rot(i, 4))
                dve.wait_ge(*a_st_mm(i, max(j - 1, 0)))
                dve.tensor_copy(hi, src).then_inc(a_st_h.sem, 1)

            def a_maxima(i, u):
                g, t, h0, nh = UNITS[u]
                dve.wait_ge(*a_s(i, u + 1))
                if u >= 2:
                    dve.wait_ge(*a_exp(i, u - 1))
                dve.tensor_reduce(nmax[:, u % 2, 0:2 * nh],
                                  s_bank[:, 2 * (u % 2):2 * (u % 2) + 2, :].rearrange("p b (h s) -> p (b h) s", h=nh),
                                  AX_X, ALU.max, negate=True).then_inc(a_max.sem, 1)

            def a_combine(i, u):
                g, t, h0, nh = UNITS[u]
                n = 512 // nh
                dve.wait_ge(*a_exp(i, u + 1))
                dve.reciprocal(rinv[:, u % 2, 0:2 * nh], rsum[:, u % 2, 0:2 * nh]).then_inc(a_inv.sem, 1)
                dve.wait_ge(*a_inv(i, u + 1))
                dve.tensor_scalar(rsum[:, u % 2, nh:2 * nh], rinv[:, u % 2, nh:2 * nh], neg_lam, None, ALU.mult
                                  ).then_inc(a_rho.sem, 1)
                dve.wait_ge(*a_rho(i, u + 1))
                dve.wait_ge(*a_p1(i, u + 1))
                for h in range(nh):
                    p1 = probs[:, u % 2, h * n:(h + 1) * n]
                    last = dve.scalar_tensor_tensor(p1, probs[:, u % 2, 512 + h * n:512 + (h + 1) * n],
                                                    rsum[:, u % 2, nh + h:nh + h + 1], p1, ALU.mult, ALU.add)
                last.then_inc(a_diff.sem, 1)

            def a_diff_l(i, u):
                dve.wait_ge(*a_dt_h(i, u + 1))
                dve.tensor_tensor(dt_l[:, u % 2, :], tr_bank[:, :], dt_h[:, u % 2, :].bitcast(F32), ALU.subtract
                                  ).then_inc(a_dt_l.sem, 1)

            def a_gstat(i, g):
                dve.wait_ge(*a_o(i, g + 1))
                dve.bn_stats(gstat[:, g, :], ao[:, g, :]).then_inc(a_gst.sem, 1)
                dve.wait_ge(*a_gst(i, g + 1))
                settled()
                dve.bn_aggr(gmv[:, g, :], gstat[:, g, :]).then_inc(a_gag.sem, 1)

            def a_group(i):
                dve.wait_ge(*a_gmm(i, 1))
                dve.tensor_copy(gtmp[:, 0, :], o_bank[:, 0:NG]).then_inc(a_gv.sem, 1)
                dve.wait_ge(*a_gv(i, 1))
                dve.tensor_tensor(gtmp[:, 1, :], gmv[:, :, 0], gtmp[:, 0, :], ALU.subtract).then_inc(a_gv.sem, 1)
                dve.wait_ge(*a_gv(i, 2))
                dve.tensor_tensor(gtmp[:, 2, :], gtmp[:, 1, :], gtmp[:, 1, :], ALU.mult).then_inc(a_gv.sem, 1)
                dve.wait_ge(*a_gv(i, 3))
                dve.tensor_tensor(gtmp[:, 2, :], gtmp[:, 2, :], gmv[:, :, 1], ALU.add).then_inc(a_gv.sem, 1)
                dve.wait_ge(*a_gmm(i, 2))
                dve.tensor_scalar(gtmp[:, 3, :], o_bank[:, NG:2 * NG], EPS, None, ALU.add).then_inc(a_gv.sem, 1)
                dve.wait_ge(*a_gp(i, 2))
                for g in range(NG):
                    dve.tensor_scalar(ao[:, g, :], ao[:, g, :], gtmp[:, 0, g:g + 1], gtmp[:, 5, g:g + 1],
                                      ALU.subtract, ALU.mult).then_inc(a_y.sem, 1)
                for g in range(NG):
                    dve.wait_ge(*a_yh(i, g + 1))
                    dve.scalar_tensor_tensor(y_l[:, g, :], ao[:, g, :], gn_wb[:, 1, g:g + 1],
                                             y_h[:, g, :].bitcast(F32), ALU.add, ALU.subtract).then_inc(a_yl.sem, 1)

            def a_residual(i):
                dve.wait_ge(*a_wo(i, 1))
                dve.wait_ge(*b_x(i, 0))
                dve.tensor_tensor(x1[:, :, :], tr_bank[:, :].rearrange("p (t d) -> p t d", t=NT), x_res[:, :, :], ALU.add
                                  ).then_inc(a_x1.sem, 1)

            def b_take(i):
                dve.wait_ge(*a_x1(i, 1))
                dve.wait_ge(*b_store(i, 0))
                dve.tensor_copy(xb[:, :, :], x1[:, :, :]).then_inc(b_x.sem, 1)
                dve.wait_ge(*b_x(i, 1))
                dve.wait_ge(*tok_loaded(i, 16))
                dve.wait_ge(*b_sel(i, 0))
                for e in range(1, E1):
                    dve.tensor_scalar(routed[:, e - 1, :], tok[:, :], float(e * (VOCAB // E1)), None, ALU.is_ge
                                      ).then_inc(b_mask.sem, 1)

            def b_norm(i, k):
                for t in range(NT):
                    dve.bn_stats(stat_b[:, t, :], xb[:, t, :]).then_inc(b_stat.sem, 1)
                for t in range(NT):
                    dve.wait_ge(*b_stat(i, 2 * k + t + 1))
                    settled()
                    dve.bn_aggr(mv_b[:, t, :], stat_b[:, t, :]).then_inc(b_aggr.sem, 1)
                dve.wait_ge(*b_rstd(i, 2 * k + 2))
                if k == 0:
                    dve.wait_ge(*b_tr(i, 0))
                for t in range(NT):
                    dve.tensor_scalar(xnb[:, t, :], xb[:, t, :], mv_b[:, t, 0:1], rstd_b[:, t, 1:2],
                                      ALU.subtract, ALU.mult).then_inc(b_xn.sem, 1)

            def b_low(i, k, dst, src, high):
                dve.wait_ge(*b_tr_h(i, k + 1))
                dve.tensor_tensor(dst, src, high.bitcast(F32), ALU.subtract).then_inc(b_tr_l.sem, 1)

            def b_select(i, k):
                t = k % 2
                dve.wait_ge(*b_e0(i, k + 1))
                if k == 0:
                    dve.wait_ge(*b_mask(i, 3))
                for e in range(1, E1):
                    if e > 1:
                        dve.wait_ge(*b_sel(i, 3 * k + e - 1))
                    settled()
                    dve.copy_predicated(z[:, t, :], routed[:, e - 1, t:t + 1].to_broadcast([P, D]),
                                        b_bank[:, e // 2, (e % 2) * D:(e % 2 + 1) * D]).then_inc(b_sel.sem, 1)

            def b_gate(i, t):
                dve.wait_ge(*b_zz(i, t + 1))
                dve.scalar_tensor_tensor(z[:, t, :], zt[:, t, :], 1.0, z[:, t, :], ALU.add, ALU.mult
                                         ).then_inc(b_p.sem, 1)

            def b_add(i, t):
                dve.wait_ge(*b_sel(i, 3 * (2 + t) + 3))
                dve.scalar_tensor_tensor(xb[:, t, :], z[:, t, :], 0.5, xb[:, t, :], ALU.mult, ALU.add
                                         ).then_inc(b_x2.sem, 1)

            def b_router(i, t):
                k = RV * t
                dve.wait_ge(*b_up(i, NGR * t + 1))
                dve.tensor_reduce(rt[:, 0, 0:1], b_bank[:, 0, SI:SI + E2], AX_X, ALU.max, negate=True
                                  ).then_inc(b_rv.sem, 1)
                dve.wait_ge(*b_re(i, t + 1))
                dve.reciprocal(rt[:, 0, 2:3], rt[:, 0, 1:2]).then_inc(b_rv.sem, 1)
                dve.wait_ge(*b_rv(i, k + 2))
                dve.tensor_scalar(rt[:, 2, :], rt[:, 1, :], rt[:, 0, 2:3], None, ALU.mult).then_inc(b_rv.sem, 1)
                dve.wait_ge(*b_rv(i, k + 3))
                settled()
                dve.max(rt[:, 3, :], rt[:, 2, :]).then_inc(b_rv.sem, 1)
                dve.wait_ge(*b_rv(i, k + 4))
                settled()
                dve.max_index(top_i[:, :], rt[:, 3, :], rt[:, 2, :]).then_inc(b_rv.sem, 1)
                dve.tensor_tensor(rt[:, 0, 3:4], rt[:, 3, 0:1], rt[:, 3, 1:2], ALU.add).then_inc(b_rv.sem, 1)
                dve.wait_ge(*b_rv(i, k + 6))
                dve.reciprocal(rt[:, 0, 4:5], rt[:, 0, 3:4]).then_inc(b_rv.sem, 1)
                dve.tensor_copy(rt[:, 4, :], top_i[:, :]).then_inc(b_rv.sem, 1)
                dve.wait_ge(*b_rv(i, k + 8))
                dve.tensor_scalar(rt[:, 5, 0:2], rt[:, 3, 0:2], rt[:, 0, 4:5], 0.5, ALU.mult, ALU.mult
                                  ).then_inc(b_rv.sem, 1)
                dve.wait_ge(*b_rv(i, k + 9))
                if t == 1:
                    dve.wait_ge(*b_hid(i, NGR))
                else:
                    dve.wait_ge(*b_hid(i, 0))
                dve.tensor_scalar(comb[:, :], iota, rt[:, 4, 0:1], rt[:, 5, 0:1], ALU.is_equal, ALU.mult
                                  ).then_inc(b_rv.sem, 1)
                dve.tensor_scalar(rt[:, 6, :], iota, rt[:, 4, 1:2], rt[:, 5, 1:2], ALU.is_equal, ALU.mult
                                  ).then_inc(b_rv.sem, 1)
                dve.wait_ge(*b_rv(i, k + 11))
                dve.tensor_tensor(comb[:, :], comb[:, :], rt[:, 6, :], ALU.add).then_inc(b_rv.sem, 1)

            def b_mul(i, t, n):
                k = NGR * t + n
                cols = SI if n == 0 else INNER
                gate = b_bank[:, 0 if n == 0 else n % 2, 0:cols]
                up = b_bank[:, 1, 0:SI] if n == 0 else b_bank[:, n % 2, INNER:2 * INNER]
                h = act_g[:, k % 2, 0:cols]
                dve.wait_ge(*b_tanh(i, k + 1))
                dve.scalar_tensor_tensor(h, h, 1.0, gate, ALU.add, ALU.mult).then_inc(b_a.sem, 1)
                dve.wait_ge(*b_a(i, k + 1))
                if n == 0 and t == 1:
                    dve.wait_ge(*b_tr(i, 3 + len(HGROUPS)))
                if n == 1:
                    dve.wait_ge(*b_rv(i, RV * t + RV))
                col = E2 * INNER if n == 0 else (n - 1) * INNER
                share = 0.5 if n == 0 else comb[:, n - 1:n]
                dve.scalar_tensor_tensor(hid[:, col:col + cols], h, share, up, ALU.mult, ALU.mult
                                         ).then_inc(b_hid.sem, 1)

            def b_final(i, t):
                dve.wait_ge(*b_down(i, t + 1))
                dve.tensor_tensor(xb[:, t, :], b_bank[:, 1, 0:D], xb[:, t, :], ALU.add).then_inc(b_out.sem, 1)

            with dve.Fori(0, NB) as i:
                a_norm(i)
                a_xt(i)
                for t in range(NT):
                    a_rotate(i, t)
                for j in range(4):
                    a_stack(i, j)
                for u in range(NU):
                    a_maxima(i, u)
                    a_combine(i, u)
                    a_diff_l(i, u)
                    if u % 3 == 1 and u < NU - 3:
                        a_stack(i, 4 + 2 * (u // 3))
                        a_stack(i, 5 + 2 * (u // 3))
                    if u % 3 == 2:
                        a_gstat(i, u // 3)
                a_group(i)
                a_residual(i)
                b_take(i)
                b_norm(i, 0)
                bb = b_bank[:, 0, :].rearrange("p (c t) -> p c t", c=ND)
                b_low(i, 0, xtb_l[:, :, :], bb, xtb_h[:, :, :])
                for t in range(NT):
                    b_select(i, t)
                    b_gate(i, t)
                b_low(i, 1, xtb_l[:, :, :], bb, xtb_h[:, :, :])
                for t in range(NT):
                    b_select(i, 2 + t)
                    b_add(i, t)
                dve.wait_ge(*b_x2(i, 2))
                b_norm(i, 1)
                b_low(i, 2, xtb_l[:, :, :], bb, xtb_h[:, :, :])
                for t in range(NT):
                    b_router(i, t)
                    for n in range(NGR):
                        b_mul(i, t, n)
                    for j, (c0, n) in enumerate(HGROUPS):
                        b_low(i, 3 + 4 * t + j, ht_l[:, j % 2, 0:n * P], b_bank[:, 0, 0:n * P],
                              ht_h[:, j % 2, 0:n * P])
                    b_final(i, t)

        @block.tensor
        def _(pe):
            pe.wait_ge(s_const, 16)
            for e in range(E1):
                k = NW + e
                pe.wait_ge(w_in[k % 2], ctx_in[e])
                for c in range(ND):
                    for f in range(ND):
                        last = pe.transpose(s_bank[:, e, c * D + f * P:c * D + (f + 1) * P],
                                            stage[k % 2][:, f * D + c * P:f * D + (c + 1) * P], ident)
                last.then_inc(c_mm, 1)
            pe.wait_ge(w_set, 1)

            def transposes(bank, src):
                for c in range(ND):
                    for t in range(NT):
                        last = pe.transpose(bank[:, c * T + t * P:c * T + (t + 1) * P], src[:, t, c * P:(c + 1) * P],
                                            ident)
                return last

            def a_xt(i):
                pe.wait_ge(*a_xn(i, 2))
                pe.wait_ge(*a_x1(i, 0))
                transposes(tr_bank, x_in).then_inc(a_xt_mm.sem, 1)

            def a_project(i, t):
                if t == 0:
                    pe.wait_ge(*a_xt_l(i, 1))
                    pe.wait_ge(*a_exp(i, 0))
                tok_t = slice(t * P, (t + 1) * P)
                for b, c0, n in ((0, 0, QC), (1, QC, 2 * KC)):
                    for c in range(ND):
                        last = three_pass(pe, s_bank[:, 2 * t + b, 0:n], xta_h[:, c, tok_t], xta_l[:, c, tok_t],
                                          wqkv_h[:, c, c0:c0 + n], wqkv_l[:, c, c0:c0 + n], c == 0, c == ND - 1)
                last.then_inc(a_qkv.sem, 1)

            def a_stack(i, j):
                pe.wait_ge(*a_st_l(i, j + 1))
                if j == 0:
                    pe.wait_ge(*a_xt_l(i, 1))
                elif j < 4 or j % 2:
                    pe.wait_ge(*a_st(i, j))
                else:
                    pe.wait_ge(*a_dt_l(i, 3 * (j // 2 - 1)))
                for b in range(4):
                    last = pe.matmul(tr_bank[:, b * P:(b + 1) * P],
                                     stack[:, j % 2, 2 * b:2 * b + 2, :, :].rearrange("p a b c -> p (a b c)"),
                                     ident_r[:, :], start=True, stop=True)
                last.then_inc(a_st_mm.sem, 1)

            def a_scores(i, u):
                g, t, h0, nh = UNITS[u]
                n = 512 // nh
                pe.wait_ge(*a_st(i, 2 * g + t + 3))
                if u >= 2:
                    pe.wait_ge(*a_exp(i, u - 1))
                else:
                    pe.wait_ge(*a_mul(i, 4))
                    pe.wait_ge(*a_vl(i, 2))
                for half in range(2):
                    s = s_bank[:, 2 * (u % 2) + half, :].rearrange("p (h s) -> p h s", h=nh)
                    pe.matmul(s[:, :, n - P:n], ident_b[:, :], mask_b[:, 0:nh, :], start=True, stop=False,
                              skip_group_check=True)
                for h in range(nh):
                    for half in range(2):
                        r = slice(half * 64, half * 64 + 64)
                        last = pe.matmul(s_bank[:, 2 * (u % 2) + half, h * n:(h + 1) * n],
                                         qt[r, (2 * g + t) % 2, h0 + h, :], kt[r, g, 0:n], start=False, stop=True,
                                         skip_group_check=True)
                last.then_inc(a_s.sem, 1)

            def a_diff_t(i, u):
                pe.wait_ge(*a_diff(i, u + 1))
                g, t, h0, nh = UNITS[u]
                if u % 3 == 2 or u % 3 == 1:
                    pe.wait_ge(*a_dt_l(i, u))
                else:
                    pe.wait_ge(*a_st(i, 2 * g + 4))
                for b in range(4):
                    last = pe.transpose(tr_bank[:, b * P:(b + 1) * P], probs[:, u % 2, b * P:(b + 1) * P], ident)
                last.then_inc(a_dt_mm.sem, 1)

            def a_values(i, u):
                g, t, h0, nh = UNITS[u]
                pe.wait_ge(*a_dt_l(i, u + 1))
                if u == 0:
                    pe.wait_ge(*a_gv(i, 0))
                elif u % 3 == 0:
                    pe.wait_ge(*a_o(i, g))
                o = o_bank[:, t * P:(t + 1) * P]
                for b in range(4):
                    h, s = (b, 0) if t == 0 else (h0 + b // 2, b % 2)
                    w0 = 96 + P * g - VW * h
                    cols = slice(b * P, (b + 1) * P)
                    last = three_pass(pe, o, vpad[:, 0, s, w0:w0 + P], vpad[:, 1, s, w0:w0 + P],
                                      dt_h[:, u % 2, cols], dt_l[:, u % 2, cols],
                                      u % 3 == 0 and b == 0, b == 3)
                last.then_inc(a_pv.sem, 1)

            def a_group(i):
                pe.wait_ge(*a_gag(i, NG))
                block_mean = const[:, C_BLK:C_BLK + P]
                pe.matmul(o_bank[:, 0:NG], block_mean, gmv[:, :, 0], start=True, stop=True).then_inc(a_gmm.sem, 1)
                pe.wait_ge(*a_gv(i, 4))
                pe.matmul(o_bank[:, NG:2 * NG], block_mean, gtmp[:, 2, :], start=True, stop=True
                          ).then_inc(a_gmm.sem, 1)

            def a_output(i):
                pe.wait_ge(*a_yl(i, NG))
                pe.wait_ge(*a_dt_l(i, NU))
                for t in range(NT):
                    for g in range(NG):
                        tt = slice(t * P, (t + 1) * P)
                        last = three_pass(pe, tr_bank[:, t * D:(t + 1) * D], y_h[:, g, tt], y_l[:, g, tt],
                                          wo_h[:, g, :], wo_l[:, g, :], t == 0 and g == 0, g == NG - 1)
                last.then_inc(a_wo.sem, 1)

            def b_xt(i, k, src):
                if k == 1:
                    pe.wait_ge(*b_p(i, 2))
                else:
                    pe.wait_ge(*b_xn(i, 2 + k))
                if k == 0:
                    pe.wait_ge(*b_out(i, 0))
                transposes(b_bank[:, 0, :], src).then_inc(b_tr.sem, 1)

            def b_routed(i, k):
                t = k % 2
                if t == 0:
                    pe.wait_ge(*b_tr_l(i, k // 2 + 1))
                else:
                    pe.wait_ge(*b_sel(i, 3 * k))
                tt = slice(t * P, (t + 1) * P)
                for b in range(2):
                    for c in range(ND):
                        last = three_pass(pe, b_bank[:, b, :], xtb_h[:, c, tt], xtb_l[:, c, tt],
                                          ct_h[:, c, 2 * b:2 * b + 2, :].rearrange("p e d -> p (e d)"),
                                          ct_l[:, c, 2 * b:2 * b + 2, :].rearrange("p e d -> p (e d)"),
                                          c == 0, c == ND - 1)
                last.then_inc(b_zy.sem, 1)

            def b_shared(i, t):
                if t == 0:
                    pe.wait_ge(*b_tr_l(i, 3))
                else:
                    pe.wait_ge(*b_out(i, 1))
                tt = slice(t * P, (t + 1) * P)
                for b, c0, n in ((0, 0, SI + E2), (1, SI + E2, SI)):
                    o = b_bank[:, b, 0:n]
                    for c in range(ND):
                        three_pass(pe, o, xtb_h[:, c, tt], xtb_l[:, c, tt], sg_h[:, c, c0:c0 + n],
                                   sg_l[:, c, c0:c0 + n], c == 0, False)
                    last = pe.matmul(b_bank[:, b, 0:SI], two_r[:, :], bias_r[:, b * SI:(b + 1) * SI], start=False, stop=True,
                                     skip_group_check=True)
                last.then_inc(b_up.sem, 1)

            def b_expert(i, t, n):
                pe.wait_ge(*b_hid(i, NGR * t + max(n - 1, 1)))
                tt = slice(t * P, (t + 1) * P)
                for c in range(ND):
                    last = three_pass(pe, b_bank[:, n % 2, 0:2 * INNER], xtb_h[:, c, tt], xtb_l[:, c, tt],
                                      gu_h[:, n - 1, c, :], gu_l[:, n - 1, c, :], c == 0, c == ND - 1)
                last.then_inc(b_up.sem, 1)

            def b_hidden_t(i, t, j):
                c0, n = HGROUPS[j]
                if j == 0:
                    pe.wait_ge(*b_hid(i, NGR * (t + 1)))
                for c in range(c0, c0 + n):
                    r = P if c < NCH - 1 else LAST
                    last = pe.transpose(b_bank[0:r, 0, (c - c0) * P:(c - c0 + 1) * P], hid[:, c * P:c * P + r], ident)
                last.then_inc(b_tr.sem, 1)

            def b_down_mm(i, t, j):
                c0, n = HGROUPS[j]
                o = b_bank[:, 1, 0:D]
                for c in range(c0, c0 + n):
                    r = P if c < NCH - 1 else LAST
                    cols = slice((c - c0) * P, (c - c0 + 1) * P)
                    three_pass(pe, o, ht_h[0:r, j % 2, cols], ht_l[0:r, j % 2, cols], dn_h[0:r, c, :], dn_l[0:r, c, :],
                               c == 0, False)
                if j == len(HGROUPS) - 1:
                    pe.matmul(o, two_r[:, :], bias_r[:, 2 * SI:], start=False, stop=True, skip_group_check=True
                              ).then_inc(b_down.sem, 1)

            with pe.Fori(0, NB) as i:
                a_xt(i)
                for t in range(NT):
                    a_project(i, t)
                for j in range(4):
                    a_stack(i, j)
                a_scores(i, 0)
                for u in range(NU):
                    g, sub = u // 3, u % 3
                    if sub < 2:
                        a_scores(i, u + 1)
                    a_diff_t(i, u)
                    if sub == 2 and g < NG - 1:
                        pe.wait_ge(*a_dt_l(i, u + 1))
                        a_stack(i, 2 * g + 4)
                        a_stack(i, 2 * g + 5)
                        a_scores(i, u + 1)
                    a_values(i, u)
                a_group(i)
                a_output(i)
                b_xt(i, 0, xnb)
                b_routed(i, 0)
                b_routed(i, 1)
                b_xt(i, 1, z)
                b_routed(i, 2)
                b_routed(i, 3)
                b_xt(i, 2, xnb)
                for t in range(NT):
                    b_shared(i, t)
                    for n in range(1, NGR):
                        b_expert(i, t, n)
                    b_hidden_t(i, t, 0)
                    for j in range(len(HGROUPS)):
                        pe.wait_ge(*b_tr_l(i, 3 + 4 * t + j + 1))
                        if j + 1 < len(HGROUPS):
                            b_hidden_t(i, t, j + 1)
                        b_down_mm(i, t, j)


INPUTS = ["x", "itok_BxS_13_99985", "ctx_2048", "L0_attn_Wq", "L0_attn_Wk", "L0_attn_Wv", "L0_attn_Wo",
          "L0_attn_lambda_q1", "L0_attn_lambda_k1", "L0_attn_lambda_q2", "L0_attn_lambda_k2", "L0_attn_gn_w",
          "L0_attn_gn_b", "L0_ffn_router_w", "L0_ffn_gate_w", "L0_ffn_up_w", "L0_ffn_down_w", "L0_ffn_s_gate_w",
          "L0_ffn_s_gate_b", "L0_ffn_s_up_w", "L0_ffn_s_up_b", "L0_ffn_s_down_w", "L0_ffn_s_down_b"]


def constants():
    c = np.zeros((P, NCONST), np.float32)
    r = np.arange(P)
    c[:, C_ID:C_ID + P] = np.eye(P)
    c[:, C_BLK:C_BLK + P] = (r[:, None] // VW == r[None, :] // VW) / VW
    c[:, C_MASK:C_MASK + P] = np.where(r[None, :] > r[:, None], MASKED, 0.0)
    inv = (np.float32(1.0) / np.float32(10000.0) ** (np.arange(0, DH, 2, dtype=np.float32) / np.float32(DH)))
    angle = np.arange(T, dtype=np.float32)[:, None] * inv.astype(np.float32)[None, :]
    for col, f in ((C_COS, np.cos), (C_SIN, np.sin)):
        tab = np.repeat(f(angle), 2, axis=1).reshape(NT, P, DH).transpose(1, 0, 2)
        c[:, col:col + NT * DH] = tab.reshape(P, NT * DH)
    c[:, C_IOTA:C_IOTA + 8] = np.arange(8)
    c[0, C_ROW0] = 1.0
    c[1, C_ROW1] = 1.0
    c[:, C_EPS] = EPS
    c[:, C_HALF] = -0.5
    c[0:2, C_TWO:C_TWO + P] = 1.0
    return c


def kernel(**inputs):
    import concourse.bacc as bacc
    from concourse.bass_utils import run_bass_kernel_spmd

    nc = bacc.Bacc("TRN2", target_bir_lowering=False, num_devices=1)
    arrays, aps = {}, {}
    for name in INPUTS:
        arr = np.ascontiguousarray(inputs[name])
        arrays["dram_" + name] = arr
        aps[name] = nc.dram_tensor("dram_" + name, arr.shape, mybir.dt.from_np(arr.dtype), kind="ExternalInput").ap()
    arrays["dram_consts"] = constants()
    aps["consts"] = nc.dram_tensor("dram_consts", (P, NCONST), F32, kind="ExternalInput").ap()
    out = nc.dram_tensor("out", (NB, T, D), F32, kind="ExternalOutput").ap()
    build(nc, aps, out)
    r = run_bass_kernel_spmd(nc, [arrays], core_ids=[0])
    return r.results[0]["out"]
```

```python
from contextlib import ExitStack

import numpy as np

import concourse.bass as bass
from concourse import mybir

F32 = mybir.dt.float32
F32R = mybir.dt.float32r
BF16 = mybir.dt.bfloat16
I32 = mybir.dt.int32
U32 = mybir.dt.uint32
ALU = mybir.AluOpType
ACT = mybir.ActivationFunctionType
AX_X = mybir.AxisListType.X

P = 128
NB, T, D = 4, 256, 256
NT, ND = T // P, D // P
H, KV, DH = 16, 4, 16
REP = H // KV
VW = 2 * DH
QC, KC = H * VW, KV * VW
NG = KV
LAMBDA_INIT = 0.2
EPS = 1e-5
E1, VOCAB = 4, 12500
E2, INNER = 8, 176
SI = 2 * INNER
HID = E2 * INNER + SI
NCH = (HID + P - 1) // P
LAST = HID - (NCH - 1) * P
NGR = 1 + E2
MASKED = -1.0e30

C_ID, C_BLK, C_MASK, C_COS, C_SIN = 0, P, 2 * P, 3 * P, 3 * P + NT * DH
C_IOTA = C_SIN + NT * DH
C_ROW0, C_ROW1, C_EPS, C_HALF = C_IOTA + 8, C_IOTA + 9, C_IOTA + 10, C_IOTA + 11
C_OUT = C_IOTA + 12
C_TWO = C_IOTA + 13
NCONST = C_TWO + P

UNITS = [u for g in range(NG) for u in ((g, 0, 0, 4), (g, 1, 0, 2), (g, 1, 2, 2))]
NU = len(UNITS)

PRE, POST, SLOTS = 6, 4, NU + 2
STEPS = PRE + 2 * SLOTS + POST
NBEAT = 29
BEATS = [[] for _ in range(STEPS)]
for b in range(NBEAT):
    BEATS[b * STEPS // NBEAT].append(b)
HGROUPS = [(0, 4), (4, 4), (8, 4), (12, NCH - 12)]


class Signal:

    def __init__(self, sem, per):
        self.sem, self.per = sem, per

    def __call__(self, i, k):
        return self.sem, (i + 1) * self.per + k


def three_pass(pe, out, lhs_h, lhs_l, rhs_h, rhs_l, start, stop):
    pe.matmul(out, lhs_h, rhs_l, start=start, stop=False, skip_group_check=True)
    pe.matmul(out, lhs_h, rhs_h, start=False, stop=False, skip_group_check=True)
    return pe.matmul(out, lhs_l, rhs_h, start=False, stop=stop, skip_group_check=True)


def build(nc, a, out):
    ctx = ExitStack()
    with ctx:
        def sb(name, shape, dt=F32):
            return ctx.enter_context(nc.sbuf_tensor(name, shape, dt))

        def psum(name, shape):
            return ctx.enter_context(nc.psum_tensor(name, shape, F32))

        def sem(name):
            return ctx.enter_context(nc.semaphore(name))

        signals = []

        def sig(name, per):
            signals.append(Signal(sem(name), per))
            return signals[-1]

        wqkv_h, wqkv_l = (sb(n, [P, ND, QC + 2 * KC], F32R) for n in ("wqkv_h", "wqkv_l"))
        wo_h, wo_l = (sb(n, [P, NG, D], F32R) for n in ("wo_h", "wo_l"))
        ct_h, ct_l = (sb(n, [P, ND, E1, D], F32R) for n in ("ct_h", "ct_l"))
        gu_h, gu_l = (sb(n, [P, E2, ND, 2 * INNER], F32R) for n in ("gu_h", "gu_l"))
        sg_h, sg_l = (sb(n, [P, ND, SI + E2 + SI], F32R) for n in ("sg_h", "sg_l"))
        dn_h, dn_l = (sb(n, [P, NCH, D], F32R) for n in ("dn_h", "dn_l"))
        bias_r = sb("bias_r", [P, 2 * SI + D], F32R)

        const = sb("const", [P, NCONST])
        ident = const[:, C_ID:C_ID + P]
        ident_r = sb("ident_r", [P, P], F32R)
        two_r = sb("two_r", [P, P], F32R)
        ident_b = sb("ident_b", [P, P], BF16)
        mask_b = sb("mask_b", [P, 4, P], BF16)
        lam_in = sb("lam_in", [P, 4, DH])
        lam = sb("lam", [P, 8])
        gn_wb = sb("gn_wb", [P, 2, NG])

        x_in = sb("x_in", [P, NT, D])
        x_res = sb("x_res", [P, NT, D])
        x1 = sb("x1", [P, NT, D])
        stat_a = sb("stat_a", [P, NT, 6])
        mv_a = sb("mv_a", [P, NT, 2])
        rstd_a = sb("rstd_a", [P, NT, 2])
        xt_kt = sb("xt_kt", [P, 4 * T], F32R)
        xta_h = xt_kt[:, 0:2 * T].rearrange("p (c t) -> p c t", c=ND)
        xta_l = xt_kt[:, 2 * T:4 * T].rearrange("p (c t) -> p c t", c=ND)
        kt = xt_kt[:, :].rearrange("p (g t) -> p g t", g=KV)
        probs = sb("probs", [P, 2, 1024])
        rot = probs[:, :, :].rearrange("p a b -> p (a b)")
        qk = sb("qk", [P, NT, QC + KC])
        stack = sb("stack", [P, 2, 8, 4, DH], F32R)
        qt = sb("qt", [P, 2, 4, P], F32R)
        vpad = sb("vpad", [P, 2, NT, 96 + KV * P], F32R)
        nmax = sb("nmax", [P, 2, 8])
        rsum = sb("rsum", [P, 2, 8])
        rinv = sb("rinv", [P, 2, 8])
        dt_h, dt_l = (sb(n, [P, 2, 4 * P], F32R) for n in ("dt_h", "dt_l"))
        y_h = qt[:, :, :, :].rearrange("p a h t -> p (a h t)").rearrange("p (g t) -> p g t", g=NG)
        y_l = dt_h[:, :, :].rearrange("p a t -> p (a t)").rearrange("p (g t) -> p g t", g=NG)
        ao = sb("ao", [P, NG, T])
        gstat = sb("gstat", [P, NG, 6])
        gmv = sb("gmv", [P, NG, 2])
        gtmp = sb("gtmp", [P, 6, NG])

        xb = sb("xb", [P, NT, D])
        stat_b = sb("stat_b", [P, NT, 6])
        mv_b = sb("mv_b", [P, NT, 2])
        rstd_b = sb("rstd_b", [P, NT, 2])
        xtb_h, xtb_l = (sb(n, [P, ND, T], F32R) for n in ("xtb_h", "xtb_l"))
        hid = sb("hid", [P, HID])
        z = hid[:, 0:2 * D].rearrange("p (t d) -> p t d", t=NT)
        zt = hid[:, 2 * D:4 * D].rearrange("p (t d) -> p t d", t=NT)
        xnb = hid[:, 4 * D:6 * D].rearrange("p (t d) -> p t d", t=NT)
        ht_h, ht_l = (sb(n, [P, 2, 4 * P], F32R) for n in ("ht_h", "ht_l"))
        act_g = sb("act_g", [P, 2, SI])
        tok = sb("tok", [P, NT], I32)
        routed = sb("routed", [P, E1 - 1, NT], U32)
        rt = sb("rt", [P, 8, 8])
        top_i = sb("top_i", [P, 8], U32)
        comb = sb("comb", [P, E2])

        s_bank = psum("s_bank", [P, 4, 512])
        tr_bank = psum("tr_bank", [P, 512])
        o_bank = psum("o_bank", [P, 512])
        b_bank = psum("b_bank", [P, 2, 512])

        w_in = [sem("w_in0"), sem("w_in1")]
        s_const, s_lam, s_gn = sem("s_const"), sem("s_lam"), sem("s_gn")
        w_high, w_low, c_high, c_low = sem("w_high"), sem("w_low"), sem("c_high"), sem("c_low")
        s_bias, w_ready, pool_ready = sem("s_bias"), sem("w_ready"), sem("pool_ready")
        c_mm = sem("c_mm")
        dve_passed = sem("dve_passed")
        set_v, set_a = sem("set_v"), sem("set_a")
        SET_V = 14

        x_loaded, tok_loaded = sig("x_loaded", 16), sig("tok_loaded", 16)
        a_res, a_stat, a_aggr, a_rstd, a_xn = (sig("a_res", 1), sig("a_stat", 2), sig("a_aggr", 2),
                                               sig("a_rstd", 2), sig("a_xn", 2))
        a_xt_mm, a_xt_h, a_xt_l = sig("a_xt_mm", 1), sig("a_xt_h", 1), sig("a_xt_l", 1)
        a_qkv, a_mul, a_rot = sig("a_qkv", 2), sig("a_mul", 4), sig("a_rot", 4)
        a_vh, a_vl = sig("a_vh", 2), sig("a_vl", 2)
        a_st_h, a_st_l, a_st_mm, a_st = sig("a_st_h", 10), sig("a_st_l", 10), sig("a_st_mm", 10), sig("a_st", 10)
        a_s, a_max, a_exp = sig("a_s", NU), sig("a_max", NU), sig("a_exp", NU)
        a_inv, a_rho, a_p1, a_diff = sig("a_inv", NU), sig("a_rho", NU), sig("a_p1", NU), sig("a_diff", NU)
        a_dt_mm, a_dt_h, a_dt_l, a_pv = (sig("a_dt_mm", NU), sig("a_dt_h", NU), sig("a_dt_l", NU),
                                         sig("a_pv", NU))
        a_o, a_gst, a_gag = sig("a_o", NG), sig("a_gst", NG), sig("a_gag", NG)
        a_gmm, a_gv, a_gp = sig("a_gmm", 2), sig("a_gv", 5), sig("a_gp", 2)
        a_y, a_yh, a_yl = sig("a_y", NG), sig("a_yh", NG), sig("a_yl", NG)
        a_wo, a_x1 = sig("a_wo", 1), sig("a_x1", 1)

        b_x, b_stat, b_aggr, b_rstd, b_xn = (sig("b_x", 1), sig("b_stat", 4), sig("b_aggr", 4),
                                             sig("b_rstd", 4), sig("b_xn", 4))
        NTR = 3 + NT * len(HGROUPS)
        b_tr, b_tr_h, b_tr_l = sig("b_tr", NTR), sig("b_tr_h", NTR), sig("b_tr_l", NTR)
        b_mask, b_zy, b_e0, b_sel = sig("b_mask", 3), sig("b_zy", 4), sig("b_e0", 4), sig("b_sel", 12)
        b_zz, b_th, b_p, b_x2 = sig("b_zz", 2), sig("b_th", 2), sig("b_p", 2), sig("b_x2", 2)
        b_up, b_tanh, b_a, b_hid = (sig("b_up", NT * NGR), sig("b_tanh", NT * NGR), sig("b_a", NT * NGR),
                                    sig("b_hid", NT * NGR))
        RV = 12
        b_rv, b_re = sig("b_rv", NT * RV), sig("b_re", NT)
        b_down, b_out, b_store = sig("b_down", NT), sig("b_out", NT), sig("b_store", 16)

        def rows(w):
            return w.rearrange("(c p) n -> c p n", p=P)

        stage = [hid[:, 0:880], hid[:, 880:1760]]
        pieces = []
        for c in range(ND):
            pieces.append(([(wqkv_h[:, c, 0:QC], wqkv_l[:, c, 0:QC], 0, QC, P, 1.0),
                            (wqkv_h[:, c, QC:QC + KC], wqkv_l[:, c, QC:QC + KC], QC, KC, P, DH ** -0.5),
                            (wqkv_h[:, c, QC + KC:], wqkv_l[:, c, QC + KC:], QC + KC, KC, P, 1.0)],
                           [(0, QC, P, rows(a["L0_attn_Wq"])[c]), (QC, KC, P, rows(a["L0_attn_Wk"])[c]),
                            (QC + KC, KC, P, rows(a["L0_attn_Wv"])[c])]))
        for c in range(0, NG, 2):
            pieces.append(([(wo_h[:, c:c + 2, :], wo_l[:, c:c + 2, :], 0, 2 * D, P, 1.0)],
                           [(D * k, D, P, rows(a["L0_attn_Wo"])[c + k]) for k in range(2)]))
        for c in range(ND):
            pieces.append(([(sg_h[:, c, :], sg_l[:, c, :], 0, 2 * SI + E2, P, 1.0)],
                           [(0, SI, P, rows(a["L0_ffn_s_gate_w"])[c]),
                            (SI, E2, P, a["L0_ffn_router_w"].rearrange("e (c p) -> c p e", p=P)[c]),
                            (SI + E2, SI, P, rows(a["L0_ffn_s_up_w"])[c])]))
        for e in range(E2):
            pieces.append(([(gu_h[:, e, :, :], gu_l[:, e, :, :], 0, 4 * INNER, P, 1.0)],
                           [(k * INNER, INNER, P, rows(w[e])[k // 2])
                            for k, w in enumerate((a["L0_ffn_gate_w"], a["L0_ffn_up_w"]) * 2)]))
        down = a["L0_ffn_down_w"].rearrange("e i h -> (e i) h")
        down = rows(down)
        full = E2 * INNER // P
        for c in range(0, full, 3):
            n = min(3, full - c)
            pieces.append(([(dn_h[:, c:c + n, :], dn_l[:, c:c + n, :], 0, n * D, P, 1.0)],
                           [(D * k, D, P, down[c + k]) for k in range(n)]))
        s_down = a["L0_ffn_s_down_w"]
        n = NCH - 1 - full
        pieces.append(([(dn_h[:, full:full + n, :], dn_l[:, full:full + n, :], 0, n * D, P, 1.0),
                        (dn_h[0:LAST, NCH - 1, :], dn_l[0:LAST, NCH - 1, :], n * D, D, LAST, 1.0)],
                       [(D * k, D, P, s_down[k * P:(k + 1) * P, :]) for k in range(n)]
                       + [(n * D, D, LAST, s_down[n * P:SI, :])]))
        biases = [[(0, SI, "s_gate_b"), (SI, SI, "s_up_b")], [(2 * SI, D, "s_down_b")]]
        NW = len(pieces)
        landed, load_done = [0, 0], []
        for k, n_loads in enumerate([len(p[1]) for p in pieces] + [1] * E1 + [len(b) for b in biases]):
            landed[k % 2] += 16 * n_loads
            load_done.append(landed[k % 2])
        parts_done = [sum(len(p[0]) for p in pieces[:k + 1]) for k in range(NW)]
        NPARTS = parts_done[-1]

        def staged(k, off, cols, r):
            return stage[k % 2][0:r, off:off + cols]

        w_beats = [[] for _ in range(STEPS)]
        for n in range(2, NW + E1 + 1):
            w_beats[min(4 + (n - 2) * (STEPS - 8) // (NW + E1 - 2), STEPS - 1)].append(n)

        def like(ap, to):
            return ap.rearrange("p (a b) -> p a b", a=to.shape[1]) if len(to.shape) == 3 else ap

        x_dram = a["x"].rearrange("b (t p) d -> b p t d", p=P)
        out_dram = out.rearrange("b (t p) d -> b p t d", p=P)
        tok_dram = a["itok_BxS_13_99985"].rearrange("b (t p) -> b p t", p=P)

        def stack_parts(j):
            w = j - 2
            if j < 2:
                src, slots = qk[:, j, QC:QC + KC], (slice(0, 2), slice(2, 4))
            else:
                src, slots = qk[:, w % 2, (w // 2) * P:(w // 2 + 1) * P], (slice(0, 4, 2), slice(1, 4, 2))
            src = src.rearrange("p (m d) -> p m d", d=DH).unsqueeze(2).to_broadcast([P, 8, 2, DH])
            return src, stack[:, j % 2, :, slots[0], :], stack[:, j % 2, :, slots[1], :]

        def slot_of(k):
            return (k - PRE) // 2, (k - PRE) % 2

        def stack_job(s):
            g = (s + 2) // 3
            return 2 + 2 * g + (s % 3 == 2) if s >= 1 and s % 3 and g < NG else None

        block = ctx.enter_context(nc.Block())

        @block.sync
        def _(sp):
            sp.dma_start(const[:, :], a["consts"]).then_inc(s_const, 16)
            for s in signals:
                sp.sem_inc(s.sem, s.per)
            sp.dma_start(x_in[:, :, :], x_dram[0]).then_inc(x_loaded.sem, 16)
            for k, (_, loads) in enumerate(pieces):
                if k >= 2:
                    sp.wait_ge(w_low, parts_done[k - 2])
                for off, cols, r, src in loads:
                    sp.dma_start(staged(k, off, cols, r), src, allow_slow_non_contiguous=cols == E2
                                 ).then_inc(w_in[k % 2], 16)
                if k == 1:
                    for j, name in enumerate(("q1", "k1", "q2", "k2")):
                        v = a["L0_attn_lambda_" + name].rearrange("(o d) -> o d", o=1)
                        sp.dma_start(lam_in[:, j, :], v.to_broadcast([P, DH])).then_inc(s_lam, 16)
                    for j, name in enumerate(("w", "b")):
                        sp.dma_start(gn_wb[:, j, :], a["L0_attn_gn_" + name].rearrange("(g p) -> p g", p=P),
                                     allow_slow_non_contiguous=True).then_inc(s_gn, 16)
                if k == NW // 2:
                    sp.wait_ge(*a_xt_mm(0, 1))
                    sp.dma_start(x_in[:, :, :], x_dram[1]).then_inc(x_loaded.sem, 16)
                    sp.dma_start(tok[:, :], tok_dram[0], allow_slow_non_contiguous=True).then_inc(tok_loaded.sem, 16)
            for e in range(E1):
                k = NW + e
                if e < 2:
                    sp.wait_ge(w_low, parts_done[k - 2])
                else:
                    sp.wait_ge(c_mm, e - 1)
                sp.dma_start(staged(k, 0, 2 * D, P).rearrange("p (c d) -> p c d", c=ND),
                             a["ctx_2048"][e].rearrange("(c p) d -> p c d", p=P)).then_inc(w_in[k % 2], 16)
            for j, loads in enumerate(biases):
                k = NW + E1 + j
                sp.wait_ge(c_mm, E1 - 1 + j)
                for off, cols, name in loads:
                    v = a["L0_ffn_" + name].rearrange("(o n) -> o n", o=1)
                    sp.dma_start(staged(k, off - loads[0][0], cols, 2), v.to_broadcast([2, cols])
                                 ).then_inc(w_in[k % 2], 16)

            def next_tokens(i):
                sp.wait_ge(*b_mask(i, 3))
                sp.dma_start(tok[:, :], tok_dram[i + 1], allow_slow_non_contiguous=True
                             ).then_inc(tok_loaded.sem, 16)

            def store(i):
                sp.wait_ge(*b_out(i, NT))
                sp.dma_start(out_dram[i], xb[:, :, :]).then_inc(b_store.sem, 16)

            with sp.Fori(0, NB - 2) as i:
                sp.wait_ge(*a_xt_mm(i + 1, 1))
                sp.dma_start(x_in[:, :, :], x_dram[i + 2]).then_inc(x_loaded.sem, 16)
                next_tokens(i)
                store(i)
            next_tokens(NB - 2)
            store(NB - 2)
            store(NB - 1)
            sp.wait_ge(*b_store(NB, 0))

        @block.gpsimd
        def _(pool):
            def a_norm(i):
                pool.wait_ge(*a_aggr(i, 2))
                pool.tensor_tensor(rstd_a[:, :, 0], mv_a[:, :, 1], const[:, C_EPS:C_EPS + 1].to_broadcast([P, NT]),
                                   ALU.add).then_inc(a_rstd.sem, 1)
                pool.wait_ge(*a_rstd(i, 1))
                pool.tensor_tensor(rstd_a[:, :, 1], rstd_a[:, :, 0],
                                   const[:, C_HALF:C_HALF + 1].to_broadcast([P, NT]),
                                   ALU.pow).then_inc(a_rstd.sem, 1)

            def a_rotate(i, t):
                n = QC + KC
                c = rot[:, 0:n].rearrange("p (m two) -> p m two", two=2)
                s = rot[:, n:2 * n].rearrange("p (m two) -> p m two", two=2)
                o = qk[:, t, :].rearrange("p (m two) -> p m two", two=2)
                pool.wait_ge(*a_mul(i, 2 * t + 2))
                if t == 0:
                    pool.wait_ge(*a_st_l(i, 0))
                pool.tensor_tensor(o[:, :, 0], c[:, :, 0], s[:, :, 1], ALU.subtract).then_inc(a_rot.sem, 1)
                pool.tensor_tensor(o[:, :, 1], c[:, :, 1], s[:, :, 0], ALU.add).then_inc(a_rot.sem, 1)

            def a_stack(i, j):
                src, hi, lo = stack_parts(j)
                pool.wait_ge(*a_st_h(i, j + 1))
                pool.tensor_tensor(lo, src, hi.bitcast(F32), ALU.subtract).then_inc(a_st_l.sem, 1)

            def a_scale(i, u):
                g, t, h0, nh = UNITS[u]
                p1 = probs[:, u % 2, 0:512].rearrange("p (h s) -> p h s", h=nh)
                pool.wait_ge(*a_exp(i, u + 1))
                pool.wait_ge(*a_inv(i, u + 1))
                pool.tensor_tensor(p1, p1, rinv[:, u % 2, 0:nh].unsqueeze(2).to_broadcast([P, nh, 512 // nh]),
                                   ALU.mult).then_inc(a_p1.sem, 1)

            def a_group(i):
                pool.wait_ge(*a_gv(i, 5))
                pool.tensor_tensor(gtmp[:, 4, :], gtmp[:, 3, :], const[:, C_HALF:C_HALF + 1].to_broadcast([P, NG]),
                                   ALU.pow).then_inc(a_gp.sem, 1)
                pool.wait_ge(*a_gp(i, 1))
                pool.tensor_tensor(gtmp[:, 5, :], gtmp[:, 4, :], gn_wb[:, 0, :], ALU.mult).then_inc(a_gp.sem, 1)

            def b_norm(i, k):
                pool.wait_ge(*b_aggr(i, 2 * k + 2))
                pool.tensor_tensor(rstd_b[:, :, 0], mv_b[:, :, 1], const[:, C_EPS:C_EPS + 1].to_broadcast([P, NT]),
                                   ALU.add).then_inc(b_rstd.sem, 1)
                pool.wait_ge(*b_rstd(i, 2 * k + 1))
                pool.tensor_tensor(rstd_b[:, :, 1], rstd_b[:, :, 0],
                                   const[:, C_HALF:C_HALF + 1].to_broadcast([P, NT]),
                                   ALU.pow).then_inc(b_rstd.sem, 1)

            def b_square(i, t):
                pool.wait_ge(*b_th(i, t + 1))
                pool.tensor_tensor(z[:, t, :], z[:, t, :], z[:, t, :], ALU.mult).then_inc(b_zz.sem, 1)

            def w_piece(n):
                if n >= NW:
                    return
                at = parts_done[n - 1]
                for hi, lo, off, cols, r, scale in pieces[n][0]:
                    at += 1
                    pool.wait_ge(w_high, at)
                    pool.tensor_tensor(lo, like(staged(n, off, cols, r), hi), hi.bitcast(F32), ALU.subtract
                                       ).then_inc(w_low, 1)

            def a_step(i, k):
                s, part = slot_of(k)
                if k == 0:
                    a_norm(i)
                elif k in (2, 3):
                    a_rotate(i, k - 2)
                elif k in (4, 5):
                    a_stack(i, 2 * k - 8)
                    a_stack(i, 2 * k - 7)
                elif 0 <= s < SLOTS and part:
                    if stack_job(s + 1) is not None:
                        a_stack(i, stack_job(s + 1))
                    if s < NU:
                        a_scale(i, s)
                elif k == PRE + 2 * SLOTS:
                    a_group(i)

            def b_beat(i, b):
                if b == 0:
                    b_norm(i, 0)
                elif b == 2:
                    b_square(i, 0)
                elif b == 3:
                    b_square(i, 1)
                elif b == 7:
                    b_norm(i, 1)

            pool.wait_ge(s_const, 16)
            pool.wait_ge(s_gn, 32)
            pool.tensor_tensor(gn_wb[:, :, :], gn_wb[:, :, :],
                               const[:, C_OUT:C_OUT + 1].unsqueeze(1).to_broadcast([P, 2, NG]), ALU.mult
                               ).then_inc(pool_ready, 1)
            pool.wait_ge(pool_ready, 1)
            for k in range(STEPS):
                a_step(0, k)
                for n in w_beats[k]:
                    w_piece(n)
            with pool.Fori(0, NB - 1) as i:
                for k in range(STEPS):
                    a_step(i + 1, k)
                    for b in BEATS[k]:
                        b_beat(i, b)
            for b in range(NBEAT):
                b_beat(NB - 1, b)

        @block.scalar
        def _(act):
            act.preload_act_table(ACT.Exp)

            def w_piece(n):
                if n < NW:
                    act.wait_ge(w_in[n % 2], load_done[n])
                    for hi, lo, off, cols, r, scale in pieces[n][0]:
                        act.activation(hi, like(staged(n, off, cols, r), hi), ACT.Copy, scale=scale
                                       ).then_inc(w_high, 1)
                elif n < NW + E1:
                    e = n - NW
                    act.wait_ge(c_mm, e + 1)
                    act.activation(ct_h[:, :, e, :], b_bank[:, e % 2, :].rearrange("p (c f) -> p c f", c=ND),
                                   ACT.Copy).then_inc(c_high, 1)

            w_piece(0)
            w_piece(1)
            act.wait_ge(set_v, 3)
            act.activation(lam[:, 2:4], lam[:, 0:2], ACT.Exp).then_inc(set_a, 1)

            def a_keep(i):
                act.wait_ge(*x_loaded(i, 16))
                act.wait_ge(*a_x1(i, 0))
                act.activation(x_res[:, :, :], x_in[:, :, :], ACT.Copy).then_inc(a_res.sem, 1)

            def a_xt(i):
                act.wait_ge(*a_xt_mm(i, 1))
                act.wait_ge(*a_s(i, 0))
                act.activation(xt_kt[:, 0:2 * T], tr_bank[:, :], ACT.Copy).then_inc(a_xt_h.sem, 1)

            def a_values(i, t):
                act.wait_ge(*a_qkv(i, t + 1))
                act.wait_ge(*a_pv(i, 0))
                v = s_bank[:, 2 * t + 1, KC:2 * KC].rearrange("p (g d) -> p g d", g=KV)
                act.activation(vpad[:, 0, t, 96:].rearrange("p (g d) -> p g d", g=KV)[:, :, 0:VW], v, ACT.Copy
                               ).then_inc(a_vh.sem, 1)

            def a_stack(i, j):
                act.wait_ge(*a_st_mm(i, j + 1))
                if j < 2:
                    dst, w = kt[:, :, j * P:(j + 1) * P], 0
                else:
                    dst, w = qt[:, j % 2, :, :], j - 2
                    if w >= 2:
                        act.wait_ge(*a_s(i, 3 * ((w - 2) // 2) + (3 if w % 2 else 1)))
                    else:
                        act.wait_ge(*a_wo(i, 0))
                act.activation(dst, tr_bank[:, :].rearrange("p (g s) -> p g s", g=4), ACT.Copy
                               ).then_inc(a_st.sem, 1)

            def a_exps(i, u, half):
                g, t, h0, nh = UNITS[u]
                n = 512 // nh
                if half == 0:
                    act.wait_ge(*a_max(i, u + 1))
                if half:
                    pass
                elif u >= 2:
                    act.wait_ge(*a_dt_mm(i, u - 1))
                else:
                    act.wait_ge(*a_rot(i, 4))
                for h in range(nh):
                    o = half * 512 + h * n
                    j = half * nh + h
                    last = act.activation(probs[:, u % 2, o:o + n], s_bank[:, 2 * (u % 2) + half, h * n:(h + 1) * n],
                                          ACT.Exp, bias=nmax[:, u % 2, j:j + 1], accum_out=rsum[:, u % 2, j:j + 1])
                if half:
                    last.then_inc(a_exp.sem, 1)

            def a_diff_h(i, u):
                act.wait_ge(*a_dt_mm(i, u + 1))
                if u >= 2:
                    act.wait_ge(*a_pv(i, u - 1))
                else:
                    act.wait_ge(*a_wo(i, 0))
                act.activation(dt_h[:, u % 2, :], tr_bank[:, :], ACT.Copy).then_inc(a_dt_h.sem, 1)

            def a_out(i, g):
                act.wait_ge(*a_pv(i, 3 * g + 3))
                act.wait_ge(*a_yl(i, 0))
                act.activation(ao[:, g, :], o_bank[:, 0:T], ACT.Copy).then_inc(a_o.sem, 1)

            def a_y_high(i, g):
                act.wait_ge(*a_y(i, g + 1))
                act.activation(y_h[:, g, :], ao[:, g, :], ACT.Identity, bias=gn_wb[:, 1, g:g + 1]
                               ).then_inc(a_yh.sem, 1)

            def b_high(i, k, dst, src, r=P):
                act.wait_ge(*b_tr(i, k + 1))
                act.activation(dst, src, ACT.Copy).then_inc(b_tr_h.sem, 1)

            def b_first(i, k):
                act.wait_ge(*b_zy(i, k + 1))
                act.activation(z[:, k % 2, :], b_bank[:, 0, 0:D], ACT.Copy).then_inc(b_e0.sem, 1)

            def b_tanh_z(i, t):
                act.wait_ge(*b_sel(i, 3 * t + 3))
                act.activation(zt[:, t, :], z[:, t, :], ACT.Tanh, scale=0.5).then_inc(b_th.sem, 1)

            def b_router(i, t):
                act.wait_ge(*b_rv(i, RV * t + 1))
                act.activation(rt[:, 1, :], b_bank[:, 0, SI:SI + E2], ACT.Exp, bias=rt[:, 0, 0:1],
                               accum_out=rt[:, 0, 1:2]).then_inc(b_re.sem, 1)

            def b_act(i, t, n):
                k = NGR * t + n
                cols = SI if n == 0 else INNER
                act.wait_ge(*b_up(i, k + 1))
                if k >= 2:
                    act.wait_ge(*b_hid(i, k - 1))
                bank = 0 if n == 0 else n % 2
                act.activation(act_g[:, k % 2, 0:cols], b_bank[:, bank, 0:cols], ACT.Tanh, scale=0.5
                               ).then_inc(b_tanh.sem, 1)

            bb = b_bank[:, 0, :].rearrange("p (c t) -> p c t", c=ND)

            def a_step(i, k):
                s, part = slot_of(k)
                if k == 0:
                    a_keep(i)
                elif k == 1:
                    a_xt(i)
                elif k in (2, 3):
                    a_values(i, k - 2)
                elif k in (4, 5):
                    a_stack(i, 2 * k - 8)
                    a_stack(i, 2 * k - 7)
                elif 0 <= s < SLOTS and part == 0:
                    if stack_job(s) is not None:
                        a_stack(i, stack_job(s))
                    if s < NU:
                        a_exps(i, s, 0)
                elif 0 <= s < SLOTS:
                    if s < NU:
                        a_exps(i, s, 1)
                    if 1 <= s <= NU:
                        a_diff_h(i, s - 1)
                    if s >= 4 and s % 3 == 1:
                        a_out(i, (s - 4) // 3)
                elif k == PRE + 2 * SLOTS:
                    pass
                elif k == PRE + 2 * SLOTS + 1:
                    for g in range(NG):
                        a_y_high(i, g)

            def b_beat(i, b):
                t = (b - 9) // 10 if b >= 9 else 0
                if b == 1:
                    b_high(i, 0, xtb_h[:, :, :], bb)
                elif b in (2, 3):
                    b_first(i, b - 2)
                    b_tanh_z(i, b - 2)
                elif b == 4:
                    b_high(i, 1, xtb_h[:, :, :], bb)
                elif b in (5, 6):
                    b_first(i, b - 3)
                elif b == 8:
                    b_high(i, 2, xtb_h[:, :, :], bb)
                elif b >= 9:
                    r = (b - 9) % 10
                    if r == 0:
                        b_router(i, t)
                        b_act(i, t, 0)
                    elif r < 5:
                        b_act(i, t, 2 * r - 1)
                        b_act(i, t, 2 * r)
                    elif r < 9:
                        j = r - 5
                        n = HGROUPS[j][1]
                        b_high(i, 3 + 4 * t + j, ht_h[:, j % 2, 0:n * P], b_bank[:, 0, 0:n * P])

            for k in range(STEPS):
                a_step(0, k)
                for n in w_beats[k]:
                    w_piece(n)
            with act.Fori(0, NB - 1) as i:
                for k in range(STEPS):
                    a_step(i + 1, k)
                    for b in BEATS[k]:
                        b_beat(i, b)
            for b in range(NBEAT):
                b_beat(NB - 1, b)

        @block.vector
        def _(dve):
            done = [0]

            def step(ins):
                ins.then_inc(set_v, 1)
                done[0] += 1

            def after():
                dve.wait_ge(set_v, done[0])

            def w_piece(n):
                if n < 2:
                    at = parts_done[n - 1] if n else 0
                    for hi, lo, off, cols, r, scale in pieces[n][0]:
                        at += 1
                        dve.wait_ge(w_high, at)
                        dve.scalar_tensor_tensor(lo, like(staged(n, off, cols, r), hi), scale, hi.bitcast(F32),
                                                 ALU.mult, ALU.subtract).then_inc(w_low, 1)
                elif NW <= n < NW + E1:
                    e = n - NW
                    dve.wait_ge(c_high, e + 1)
                    dve.tensor_tensor(ct_l[:, :, e, :], b_bank[:, e % 2, :].rearrange("p (c f) -> p c f", c=ND),
                                      ct_h[:, :, e, :].bitcast(F32), ALU.subtract).then_inc(c_low, 1)
                elif n == NW + E1:
                    for j, loads in enumerate(biases):
                        m = n + j
                        c0, cols = loads[0][0], sum(x[1] for x in loads)
                        raw, parts = staged(m, 0, cols, 2), bias_r[0:2, c0:c0 + cols]
                        dve.wait_ge(w_in[m % 2], load_done[m])
                        dve.tensor_copy(parts, raw).then_inc(s_bias, 1)
                        dve.wait_ge(s_bias, 4 * j + 1)
                        dve.tensor_tensor(raw, raw, parts.bitcast(F32), ALU.subtract).then_inc(s_bias, 1)
                        dve.wait_ge(s_bias, 4 * j + 2)
                        dve.tensor_scalar(raw, raw, const[0:2, C_ROW1:C_ROW1 + 1], None, ALU.mult).then_inc(s_bias, 1)
                        dve.wait_ge(s_bias, 4 * j + 3)
                        dve.scalar_tensor_tensor(parts, parts.bitcast(F32), const[0:2, C_ROW0:C_ROW0 + 1], raw,
                                                 ALU.mult, ALU.add).then_inc(s_bias, 1)
                    dve.wait_ge(s_bias, 4 * len(biases))
                    dve.wait_ge(w_low, NPARTS)
                    dve.wait_ge(c_low, E1)
                    dve.tensor_copy(lam[:, 6:7], lam[:, 5:6]).then_inc(w_ready, 1)

            dve.wait_ge(s_lam, 64)
            step(dve.tensor_tensor(lam_in[:, 0, :], lam_in[:, 0, :], lam_in[:, 1, :], ALU.mult))
            step(dve.tensor_tensor(lam_in[:, 2, :], lam_in[:, 2, :], lam_in[:, 3, :], ALU.mult))
            after()
            step(dve.tensor_reduce(lam[:, 0:2], lam_in[:, 0:4:2, :], AX_X, ALU.add))
            dve.wait_ge(s_const, 16)
            step(dve.tensor_copy(ident_r[:, :], ident))
            step(dve.tensor_copy(ident_b[:, :], ident))
            step(dve.tensor_copy(two_r[:, :], const[:, C_TWO:C_TWO + P]))
            for j in range(4):
                step(dve.tensor_copy(mask_b[:, j, :], const[:, C_MASK:C_MASK + P]))
            step(dve.memset(vpad[:, :, :, :].bitcast(F32), 0.0))
            step(dve.memset(bias_r[:, :].bitcast(F32), 0.0))
            w_piece(0)
            w_piece(1)
            dve.wait_ge(set_a, 1)
            step(dve.tensor_tensor(lam[:, 4:5], lam[:, 3:4], lam[:, 2:3], ALU.subtract))
            after()
            step(dve.tensor_scalar(lam[:, 5:6], lam[:, 4:5], -LAMBDA_INIT, None, ALU.add))
            after()
            assert done[0] == SET_V
            neg_lam = lam[:, 5:6]
            iota = const[:, C_IOTA:C_IOTA + 8]

            def settled():
                dve.sem_inc(dve_passed, 1)

            def a_norm(i):
                dve.wait_ge(*x_loaded(i, 16))
                for t in range(NT):
                    dve.bn_stats(stat_a[:, t, :], x_in[:, t, :]).then_inc(a_stat.sem, 1)
                for t in range(NT):
                    dve.wait_ge(*a_stat(i, t + 1))
                    settled()
                    dve.bn_aggr(mv_a[:, t, :], stat_a[:, t, :]).then_inc(a_aggr.sem, 1)
                dve.wait_ge(*a_res(i, 1))
                dve.wait_ge(*a_rstd(i, 2))
                for t in range(NT):
                    dve.tensor_scalar(x_in[:, t, :], x_in[:, t, :], mv_a[:, t, 0:1], rstd_a[:, t, 1:2],
                                      ALU.subtract, ALU.mult).then_inc(a_xn.sem, 1)

            def a_xt(i):
                dve.wait_ge(*a_xt_h(i, 1))
                dve.tensor_tensor(xt_kt[:, 2 * T:4 * T], tr_bank[:, :], xt_kt[:, 0:2 * T].bitcast(F32), ALU.subtract
                                  ).then_inc(a_xt_l.sem, 1)

            def a_rotate(i, t):
                n = QC + KC
                x = s_bank[:, 2 * t:2 * t + 2, :].rearrange("p b c -> p (b c)")[:, 0:n]
                dve.wait_ge(*a_qkv(i, t + 1))
                dve.wait_ge(*a_vh(i, t + 1))
                if t == 0:
                    dve.wait_ge(*a_dt_mm(i, 0))
                else:
                    dve.wait_ge(*a_rot(i, 2))
                for k, c0 in enumerate((C_COS, C_SIN)):
                    tab = const[:, c0 + t * DH:c0 + (t + 1) * DH].unsqueeze(1).to_broadcast([P, n // DH, DH])
                    dve.tensor_tensor(rot[:, k * n:(k + 1) * n].rearrange("p (m d) -> p m d", d=DH),
                                      x.rearrange("p (m d) -> p m d", d=DH), tab, ALU.mult).then_inc(a_mul.sem, 1)
                v = s_bank[:, 2 * t + 1, KC:2 * KC].rearrange("p (g d) -> p g d", g=KV)
                vh, vl = (vpad[:, s, t, 96:].rearrange("p (g d) -> p g d", g=KV)[:, :, 0:VW] for s in range(2))
                dve.wait_ge(*a_pv(i, 0))
                dve.tensor_tensor(vl, v, vh.bitcast(F32), ALU.subtract).then_inc(a_vl.sem, 1)

            def a_stack(i, j):
                src, hi, lo = stack_parts(j)
                dve.wait_ge(*a_rot(i, 4))
                dve.wait_ge(*a_st_mm(i, max(j - 1, 0)))
                dve.tensor_copy(hi, src).then_inc(a_st_h.sem, 1)

            def a_maxima(i, u):
                g, t, h0, nh = UNITS[u]
                dve.wait_ge(*a_s(i, u + 1))
                if u >= 2:
                    dve.wait_ge(*a_exp(i, u - 1))
                dve.tensor_reduce(nmax[:, u % 2, 0:2 * nh],
                                  s_bank[:, 2 * (u % 2):2 * (u % 2) + 2, :].rearrange("p b (h s) -> p (b h) s", h=nh),
                                  AX_X, ALU.max, negate=True).then_inc(a_max.sem, 1)

            def a_inverse(i, u):
                g, t, h0, nh = UNITS[u]
                dve.wait_ge(*a_exp(i, u + 1))
                dve.reciprocal(rinv[:, u % 2, 0:2 * nh], rsum[:, u % 2, 0:2 * nh]).then_inc(a_inv.sem, 1)
                dve.wait_ge(*a_inv(i, u + 1))
                dve.tensor_scalar(rsum[:, u % 2, nh:2 * nh], rinv[:, u % 2, nh:2 * nh], neg_lam, None, ALU.mult
                                  ).then_inc(a_rho.sem, 1)

            def a_combine(i, u):
                g, t, h0, nh = UNITS[u]
                n = 512 // nh
                dve.wait_ge(*a_rho(i, u + 1))
                dve.wait_ge(*a_p1(i, u + 1))
                for h in range(nh):
                    p1 = probs[:, u % 2, h * n:(h + 1) * n]
                    last = dve.scalar_tensor_tensor(p1, probs[:, u % 2, 512 + h * n:512 + (h + 1) * n],
                                                    rsum[:, u % 2, nh + h:nh + h + 1], p1, ALU.mult, ALU.add)
                last.then_inc(a_diff.sem, 1)

            def a_diff_l(i, u):
                dve.wait_ge(*a_dt_h(i, u + 1))
                dve.tensor_tensor(dt_l[:, u % 2, :], tr_bank[:, :], dt_h[:, u % 2, :].bitcast(F32), ALU.subtract
                                  ).then_inc(a_dt_l.sem, 1)

            def a_gstat(i, g):
                dve.wait_ge(*a_o(i, g + 1))
                dve.bn_stats(gstat[:, g, :], ao[:, g, :]).then_inc(a_gst.sem, 1)
                dve.wait_ge(*a_gst(i, g + 1))
                settled()
                dve.bn_aggr(gmv[:, g, :], gstat[:, g, :]).then_inc(a_gag.sem, 1)

            def a_group(i):
                dve.wait_ge(*a_gmm(i, 1))
                dve.tensor_copy(gtmp[:, 0, :], o_bank[:, 0:NG]).then_inc(a_gv.sem, 1)
                dve.wait_ge(*a_gv(i, 1))
                dve.tensor_tensor(gtmp[:, 1, :], gmv[:, :, 0], gtmp[:, 0, :], ALU.subtract).then_inc(a_gv.sem, 1)
                dve.wait_ge(*a_gv(i, 2))
                dve.tensor_tensor(gtmp[:, 2, :], gtmp[:, 1, :], gtmp[:, 1, :], ALU.mult).then_inc(a_gv.sem, 1)
                dve.wait_ge(*a_gv(i, 3))
                dve.tensor_tensor(gtmp[:, 2, :], gtmp[:, 2, :], gmv[:, :, 1], ALU.add).then_inc(a_gv.sem, 1)
                dve.wait_ge(*a_gmm(i, 2))
                dve.tensor_scalar(gtmp[:, 3, :], o_bank[:, NG:2 * NG], EPS, None, ALU.add).then_inc(a_gv.sem, 1)
                dve.wait_ge(*a_gp(i, 2))
                for g in range(NG):
                    dve.tensor_scalar(ao[:, g, :], ao[:, g, :], gtmp[:, 0, g:g + 1], gtmp[:, 5, g:g + 1],
                                      ALU.subtract, ALU.mult).then_inc(a_y.sem, 1)

            def a_y_low(i):
                for g in range(NG):
                    dve.wait_ge(*a_yh(i, g + 1))
                    dve.scalar_tensor_tensor(y_l[:, g, :], ao[:, g, :], gn_wb[:, 1, g:g + 1],
                                             y_h[:, g, :].bitcast(F32), ALU.add, ALU.subtract).then_inc(a_yl.sem, 1)

            def a_residual(i):
                dve.wait_ge(*a_wo(i, 1))
                dve.wait_ge(*b_x(i, 0))
                dve.tensor_tensor(x1[:, :, :], tr_bank[:, :].rearrange("p (t d) -> p t d", t=NT), x_res[:, :, :], ALU.add
                                  ).then_inc(a_x1.sem, 1)

            def b_take(i):
                dve.wait_ge(*a_x1(i, 1))
                dve.wait_ge(*b_store(i, 0))
                dve.tensor_copy(xb[:, :, :], x1[:, :, :]).then_inc(b_x.sem, 1)
                dve.wait_ge(*b_x(i, 1))
                dve.wait_ge(*tok_loaded(i, 16))
                dve.wait_ge(*b_sel(i, 0))
                for e in range(1, E1):
                    dve.tensor_scalar(routed[:, e - 1, :], tok[:, :], float(e * (VOCAB // E1)), None, ALU.is_ge
                                      ).then_inc(b_mask.sem, 1)

            def b_norm(i, k):
                for t in range(NT):
                    dve.bn_stats(stat_b[:, t, :], xb[:, t, :]).then_inc(b_stat.sem, 1)
                for t in range(NT):
                    dve.wait_ge(*b_stat(i, 2 * k + t + 1))
                    settled()
                    dve.bn_aggr(mv_b[:, t, :], stat_b[:, t, :]).then_inc(b_aggr.sem, 1)
                dve.wait_ge(*b_rstd(i, 2 * k + 2))
                if k == 0:
                    dve.wait_ge(*b_tr(i, 0))
                for t in range(NT):
                    dve.tensor_scalar(xnb[:, t, :], xb[:, t, :], mv_b[:, t, 0:1], rstd_b[:, t, 1:2],
                                      ALU.subtract, ALU.mult).then_inc(b_xn.sem, 1)

            def b_low(i, k, dst, src, high):
                dve.wait_ge(*b_tr_h(i, k + 1))
                dve.tensor_tensor(dst, src, high.bitcast(F32), ALU.subtract).then_inc(b_tr_l.sem, 1)

            def b_select(i, k):
                t = k % 2
                dve.wait_ge(*b_e0(i, k + 1))
                if k == 0:
                    dve.wait_ge(*b_mask(i, 3))
                for e in range(1, E1):
                    if e > 1:
                        dve.wait_ge(*b_sel(i, 3 * k + e - 1))
                    settled()
                    dve.copy_predicated(z[:, t, :], routed[:, e - 1, t:t + 1].to_broadcast([P, D]),
                                        b_bank[:, e // 2, (e % 2) * D:(e % 2 + 1) * D]).then_inc(b_sel.sem, 1)

            def b_gate(i, t):
                dve.wait_ge(*b_zz(i, t + 1))
                dve.scalar_tensor_tensor(z[:, t, :], zt[:, t, :], 1.0, z[:, t, :], ALU.add, ALU.mult
                                         ).then_inc(b_p.sem, 1)

            def b_add(i, t):
                dve.wait_ge(*b_sel(i, 3 * (2 + t) + 3))
                dve.scalar_tensor_tensor(xb[:, t, :], z[:, t, :], 0.5, xb[:, t, :], ALU.mult, ALU.add
                                         ).then_inc(b_x2.sem, 1)

            def b_router(i, t):
                k = RV * t
                dve.wait_ge(*b_up(i, NGR * t + 1))
                dve.tensor_reduce(rt[:, 0, 0:1], b_bank[:, 0, SI:SI + E2], AX_X, ALU.max, negate=True
                                  ).then_inc(b_rv.sem, 1)
                dve.wait_ge(*b_re(i, t + 1))
                dve.reciprocal(rt[:, 0, 2:3], rt[:, 0, 1:2]).then_inc(b_rv.sem, 1)
                dve.wait_ge(*b_rv(i, k + 2))
                dve.tensor_scalar(rt[:, 2, :], rt[:, 1, :], rt[:, 0, 2:3], None, ALU.mult).then_inc(b_rv.sem, 1)
                dve.wait_ge(*b_rv(i, k + 3))
                settled()
                dve.max(rt[:, 3, :], rt[:, 2, :]).then_inc(b_rv.sem, 1)
                dve.wait_ge(*b_rv(i, k + 4))
                settled()
                dve.max_index(top_i[:, :], rt[:, 3, :], rt[:, 2, :]).then_inc(b_rv.sem, 1)
                dve.tensor_tensor(rt[:, 0, 3:4], rt[:, 3, 0:1], rt[:, 3, 1:2], ALU.add).then_inc(b_rv.sem, 1)
                dve.wait_ge(*b_rv(i, k + 6))
                dve.reciprocal(rt[:, 0, 4:5], rt[:, 0, 3:4]).then_inc(b_rv.sem, 1)
                dve.tensor_copy(rt[:, 4, :], top_i[:, :]).then_inc(b_rv.sem, 1)
                dve.wait_ge(*b_rv(i, k + 8))
                dve.tensor_scalar(rt[:, 5, 0:2], rt[:, 3, 0:2], rt[:, 0, 4:5], 0.5, ALU.mult, ALU.mult
                                  ).then_inc(b_rv.sem, 1)
                dve.wait_ge(*b_rv(i, k + 9))
                if t == 1:
                    dve.wait_ge(*b_hid(i, NGR))
                else:
                    dve.wait_ge(*b_hid(i, 0))
                dve.tensor_scalar(comb[:, :], iota, rt[:, 4, 0:1], rt[:, 5, 0:1], ALU.is_equal, ALU.mult
                                  ).then_inc(b_rv.sem, 1)
                dve.tensor_scalar(rt[:, 6, :], iota, rt[:, 4, 1:2], rt[:, 5, 1:2], ALU.is_equal, ALU.mult
                                  ).then_inc(b_rv.sem, 1)
                dve.wait_ge(*b_rv(i, k + 11))
                dve.tensor_tensor(comb[:, :], comb[:, :], rt[:, 6, :], ALU.add).then_inc(b_rv.sem, 1)

            def b_mul(i, t, n):
                k = NGR * t + n
                cols = SI if n == 0 else INNER
                gate = b_bank[:, 0 if n == 0 else n % 2, 0:cols]
                up = b_bank[:, 1, 0:SI] if n == 0 else b_bank[:, n % 2, INNER:2 * INNER]
                h = act_g[:, k % 2, 0:cols]
                dve.wait_ge(*b_tanh(i, k + 1))
                dve.scalar_tensor_tensor(h, h, 1.0, gate, ALU.add, ALU.mult).then_inc(b_a.sem, 1)
                dve.wait_ge(*b_a(i, k + 1))
                if n == 0 and t == 1:
                    dve.wait_ge(*b_tr(i, 3 + len(HGROUPS)))
                if n == 1:
                    dve.wait_ge(*b_rv(i, RV * t + RV))
                col = E2 * INNER if n == 0 else (n - 1) * INNER
                share = 0.5 if n == 0 else comb[:, n - 1:n]
                dve.scalar_tensor_tensor(hid[:, col:col + cols], h, share, up, ALU.mult, ALU.mult
                                         ).then_inc(b_hid.sem, 1)

            def b_final(i, t):
                dve.wait_ge(*b_down(i, t + 1))
                dve.tensor_tensor(xb[:, t, :], b_bank[:, 1, 0:D], xb[:, t, :], ALU.add).then_inc(b_out.sem, 1)

            bb = b_bank[:, 0, :].rearrange("p (c t) -> p c t", c=ND)

            def a_step(i, k):
                s, part = slot_of(k)
                if k == 0:
                    a_norm(i)
                elif k == 1:
                    a_xt(i)
                elif k in (2, 3):
                    a_rotate(i, k - 2)
                elif k == 4:
                    a_stack(i, 0)
                    a_stack(i, 1)
                elif k == 5:
                    a_stack(i, 2)
                    a_stack(i, 3)
                    a_maxima(i, 0)
                elif 0 <= s < SLOTS and part == 0:
                    if 1 <= s <= NU:
                        a_combine(i, s - 1)
                    if s + 1 < NU:
                        a_maxima(i, s + 1)
                elif 0 <= s < SLOTS:
                    if stack_job(s + 1) is not None:
                        a_stack(i, stack_job(s + 1))
                    if s >= 5 and s % 3 == 2:
                        a_gstat(i, (s - 5) // 3)
                    if s < NU:
                        a_inverse(i, s)
                    if 1 <= s <= NU:
                        a_diff_l(i, s - 1)
                elif k == PRE + 2 * SLOTS:
                    a_gstat(i, NG - 1)
                    a_group(i)
                elif k == PRE + 2 * SLOTS + 1:
                    a_y_low(i)
                elif k == PRE + 2 * SLOTS + 3:
                    a_residual(i)

            def b_beat(i, b):
                t = (b - 9) // 10 if b >= 9 else 0
                if b == 0:
                    b_take(i)
                    b_norm(i, 0)
                elif b == 1:
                    b_low(i, 0, xtb_l[:, :, :], bb, xtb_h[:, :, :])
                elif b in (2, 3):
                    b_select(i, b - 2)
                    b_gate(i, b - 2)
                elif b == 4:
                    b_low(i, 1, xtb_l[:, :, :], bb, xtb_h[:, :, :])
                elif b in (5, 6):
                    b_select(i, b - 3)
                    b_add(i, b - 5)
                elif b == 7:
                    dve.wait_ge(*b_x2(i, 2))
                    b_norm(i, 1)
                elif b == 8:
                    b_low(i, 2, xtb_l[:, :, :], bb, xtb_h[:, :, :])
                else:
                    r = (b - 9) % 10
                    if r == 0:
                        b_router(i, t)
                        b_mul(i, t, 0)
                    elif r < 5:
                        b_mul(i, t, 2 * r - 1)
                        b_mul(i, t, 2 * r)
                    elif r < 9:
                        j = r - 5
                        n = HGROUPS[j][1]
                        b_low(i, 3 + 4 * t + j, ht_l[:, j % 2, 0:n * P], b_bank[:, 0, 0:n * P],
                              ht_h[:, j % 2, 0:n * P])
                    else:
                        b_final(i, t)

            for k in range(STEPS):
                a_step(0, k)
                for n in w_beats[k]:
                    w_piece(n)
            with dve.Fori(0, NB - 1) as i:
                for k in range(STEPS):
                    a_step(i + 1, k)
                    for b in BEATS[k]:
                        b_beat(i, b)
            for b in range(NBEAT):
                b_beat(NB - 1, b)

        @block.tensor
        def _(pe):
            def w_piece(n):
                if NW <= n < NW + E1:
                    e = n - NW
                    pe.wait_ge(w_in[n % 2], load_done[n])
                    if e >= 2:
                        pe.wait_ge(c_low, e - 1)
                    for c in range(ND):
                        for f in range(ND):
                            last = pe.transpose(b_bank[:, e % 2, c * D + f * P:c * D + (f + 1) * P],
                                                stage[n % 2][:, f * D + c * P:f * D + (c + 1) * P], ident)
                    last.then_inc(c_mm, 1)

            def transposes(bank, src):
                for c in range(ND):
                    for t in range(NT):
                        last = pe.transpose(bank[:, c * T + t * P:c * T + (t + 1) * P], src[:, t, c * P:(c + 1) * P],
                                            ident)
                return last

            def a_xt(i):
                pe.wait_ge(*a_xn(i, 2))
                pe.wait_ge(*a_x1(i, 0))
                transposes(tr_bank, x_in).then_inc(a_xt_mm.sem, 1)

            def a_project(i, t):
                if t == 0:
                    pe.wait_ge(*a_xt_l(i, 1))
                    pe.wait_ge(*a_exp(i, 0))
                tok_t = slice(t * P, (t + 1) * P)
                for b, c0, n in ((0, 0, QC), (1, QC, 2 * KC)):
                    for c in range(ND):
                        last = three_pass(pe, s_bank[:, 2 * t + b, 0:n], xta_h[:, c, tok_t], xta_l[:, c, tok_t],
                                          wqkv_h[:, c, c0:c0 + n], wqkv_l[:, c, c0:c0 + n], c == 0, c == ND - 1)
                last.then_inc(a_qkv.sem, 1)

            def a_stack(i, j):
                pe.wait_ge(*a_st_l(i, j + 1))
                if j == 0:
                    pe.wait_ge(*a_xt_l(i, 1))
                elif j <= 4:
                    pe.wait_ge(*a_st(i, j))
                else:
                    pe.wait_ge(*a_dt_l(i, 3 * (j // 2 - 1) - (2 if j % 2 == 0 else 1) - 1))
                for b in range(4):
                    last = pe.matmul(tr_bank[:, b * P:(b + 1) * P],
                                     stack[:, j % 2, 2 * b:2 * b + 2, :, :].rearrange("p a b c -> p (a b c)"),
                                     ident_r[:, :], start=True, stop=True)
                last.then_inc(a_st_mm.sem, 1)

            def a_scores(i, u):
                g, t, h0, nh = UNITS[u]
                n = 512 // nh
                pe.wait_ge(*a_st(i, 2 * g + t + 3))
                if u >= 2:
                    pe.wait_ge(*a_exp(i, u - 1))
                else:
                    pe.wait_ge(*a_mul(i, 4))
                    pe.wait_ge(*a_vl(i, 2))
                for half in range(2):
                    s = s_bank[:, 2 * (u % 2) + half, :].rearrange("p (h s) -> p h s", h=nh)
                    pe.matmul(s[:, :, n - P:n], ident_b[:, :], mask_b[:, 0:nh, :], start=True, stop=False,
                              skip_group_check=True)
                for h in range(nh):
                    for half in range(2):
                        r = slice(half * 64, half * 64 + 64)
                        last = pe.matmul(s_bank[:, 2 * (u % 2) + half, h * n:(h + 1) * n],
                                         qt[r, (2 * g + t) % 2, h0 + h, :], kt[r, g, 0:n], start=False, stop=True,
                                         skip_group_check=True)
                last.then_inc(a_s.sem, 1)

            def a_diff_t(i, u):
                pe.wait_ge(*a_diff(i, u + 1))
                j = stack_job(u + 1)
                if j is None:
                    pe.wait_ge(*a_dt_l(i, u))
                else:
                    pe.wait_ge(*a_st(i, j + 1))
                for b in range(4):
                    last = pe.transpose(tr_bank[:, b * P:(b + 1) * P], probs[:, u % 2, b * P:(b + 1) * P], ident)
                last.then_inc(a_dt_mm.sem, 1)

            def a_values(i, u):
                g, t, h0, nh = UNITS[u]
                pe.wait_ge(*a_dt_l(i, u + 1))
                if u == 0:
                    pe.wait_ge(*a_gv(i, 0))
                elif u % 3 == 0:
                    pe.wait_ge(*a_o(i, g))
                o = o_bank[:, t * P:(t + 1) * P]
                for b in range(4):
                    h, s = (b, 0) if t == 0 else (h0 + b // 2, b % 2)
                    w0 = 96 + P * g - VW * h
                    cols = slice(b * P, (b + 1) * P)
                    last = three_pass(pe, o, vpad[:, 0, s, w0:w0 + P], vpad[:, 1, s, w0:w0 + P],
                                      dt_h[:, u % 2, cols], dt_l[:, u % 2, cols],
                                      u % 3 == 0 and b == 0, b == 3)
                last.then_inc(a_pv.sem, 1)

            def a_group(i):
                pe.wait_ge(*a_gag(i, NG))
                block_mean = const[:, C_BLK:C_BLK + P]
                pe.matmul(o_bank[:, 0:NG], block_mean, gmv[:, :, 0], start=True, stop=True).then_inc(a_gmm.sem, 1)
                pe.wait_ge(*a_gv(i, 4))
                pe.matmul(o_bank[:, NG:2 * NG], block_mean, gtmp[:, 2, :], start=True, stop=True
                          ).then_inc(a_gmm.sem, 1)

            def a_output(i):
                pe.wait_ge(*a_yl(i, NG))
                pe.wait_ge(*a_dt_l(i, NU))
                for t in range(NT):
                    for g in range(NG):
                        tt = slice(t * P, (t + 1) * P)
                        last = three_pass(pe, tr_bank[:, t * D:(t + 1) * D], y_h[:, g, tt], y_l[:, g, tt],
                                          wo_h[:, g, :], wo_l[:, g, :], t == 0 and g == 0, g == NG - 1)
                last.then_inc(a_wo.sem, 1)

            def b_xt(i, k, src):
                if k == 1:
                    pe.wait_ge(*b_p(i, 2))
                else:
                    pe.wait_ge(*b_xn(i, 2 + k))
                if k == 0:
                    pe.wait_ge(*b_out(i, 0))
                transposes(b_bank[:, 0, :], src).then_inc(b_tr.sem, 1)

            def b_routed(i, k):
                t = k % 2
                if t == 0:
                    pe.wait_ge(*b_tr_l(i, k // 2 + 1))
                else:
                    pe.wait_ge(*b_sel(i, 3 * k))
                tt = slice(t * P, (t + 1) * P)
                for b in range(2):
                    for c in range(ND):
                        last = three_pass(pe, b_bank[:, b, :], xtb_h[:, c, tt], xtb_l[:, c, tt],
                                          ct_h[:, c, 2 * b:2 * b + 2, :].rearrange("p e d -> p (e d)"),
                                          ct_l[:, c, 2 * b:2 * b + 2, :].rearrange("p e d -> p (e d)"),
                                          c == 0, c == ND - 1)
                last.then_inc(b_zy.sem, 1)

            def b_shared(i, t):
                if t == 0:
                    pe.wait_ge(*b_tr_l(i, 3))
                else:
                    pe.wait_ge(*b_out(i, 1))
                tt = slice(t * P, (t + 1) * P)
                for b, c0, n in ((0, 0, SI + E2), (1, SI + E2, SI)):
                    o = b_bank[:, b, 0:n]
                    for c in range(ND):
                        three_pass(pe, o, xtb_h[:, c, tt], xtb_l[:, c, tt], sg_h[:, c, c0:c0 + n],
                                   sg_l[:, c, c0:c0 + n], c == 0, False)
                    last = pe.matmul(b_bank[:, b, 0:SI], two_r[:, :], bias_r[:, b * SI:(b + 1) * SI], start=False, stop=True,
                                     skip_group_check=True)
                last.then_inc(b_up.sem, 1)

            def b_expert(i, t, n):
                pe.wait_ge(*b_hid(i, NGR * t + max(n - 1, 1)))
                tt = slice(t * P, (t + 1) * P)
                for c in range(ND):
                    last = three_pass(pe, b_bank[:, n % 2, 0:2 * INNER], xtb_h[:, c, tt], xtb_l[:, c, tt],
                                      gu_h[:, n - 1, c, :], gu_l[:, n - 1, c, :], c == 0, c == ND - 1)
                last.then_inc(b_up.sem, 1)

            def b_hidden_t(i, t, j):
                c0, n = HGROUPS[j]
                if j == 0:
                    pe.wait_ge(*b_hid(i, NGR * (t + 1)))
                for c in range(c0, c0 + n):
                    r = P if c < NCH - 1 else LAST
                    last = pe.transpose(b_bank[0:r, 0, (c - c0) * P:(c - c0 + 1) * P], hid[:, c * P:c * P + r], ident)
                last.then_inc(b_tr.sem, 1)

            def b_down_mm(i, t, j):
                c0, n = HGROUPS[j]
                o = b_bank[:, 1, 0:D]
                for c in range(c0, c0 + n):
                    r = P if c < NCH - 1 else LAST
                    cols = slice((c - c0) * P, (c - c0 + 1) * P)
                    three_pass(pe, o, ht_h[0:r, j % 2, cols], ht_l[0:r, j % 2, cols], dn_h[0:r, c, :], dn_l[0:r, c, :],
                               c == 0, False)
                if j == len(HGROUPS) - 1:
                    pe.matmul(o, two_r[:, :], bias_r[:, 2 * SI:], start=False, stop=True, skip_group_check=True
                              ).then_inc(b_down.sem, 1)

            def a_step(i, k):
                s, part = slot_of(k)
                if k == 1:
                    a_xt(i)
                elif k in (2, 3):
                    a_project(i, k - 2)
                elif k == 4:
                    a_stack(i, 0)
                    a_stack(i, 1)
                elif k == 5:
                    a_stack(i, 2)
                    a_stack(i, 3)
                    a_scores(i, 0)
                elif 0 <= s < SLOTS and part == 0:
                    if stack_job(s) is not None:
                        a_stack(i, stack_job(s))
                    if s + 1 < NU:
                        a_scores(i, s + 1)
                elif 0 <= s < SLOTS:
                    if s >= 2:
                        a_values(i, s - 2)
                    if 1 <= s <= NU:
                        a_diff_t(i, s - 1)
                elif k == PRE + 2 * SLOTS:
                    a_group(i)
                elif k == PRE + 2 * SLOTS + 2:
                    a_output(i)

            def b_beat(i, b):
                t = (b - 9) // 10 if b >= 9 else 0
                if b in (1, 4, 8):
                    b_xt(i, {1: 0, 4: 1, 8: 2}[b], z if b == 4 else xnb)
                elif b in (2, 3):
                    b_routed(i, b - 2)
                elif b in (5, 6):
                    b_routed(i, b - 3)
                elif b >= 9:
                    r = (b - 9) % 10
                    if r == 0:
                        b_shared(i, t)
                    elif r < 5:
                        b_expert(i, t, 2 * r - 1)
                        b_expert(i, t, 2 * r)
                    else:
                        if r >= 6:
                            pe.wait_ge(*b_tr_l(i, 3 + 4 * t + r - 5))
                        if r < 9:
                            b_hidden_t(i, t, r - 5)
                        if r >= 6:
                            b_down_mm(i, t, r - 6)

            pe.wait_ge(set_v, SET_V - 2)
            for k in range(STEPS):
                a_step(0, k)
                for n in w_beats[k]:
                    w_piece(n)
            pe.wait_ge(w_ready, 1)
            with pe.Fori(0, NB - 1) as i:
                for k in range(STEPS):
                    a_step(i + 1, k)
                    for b in BEATS[k]:
                        b_beat(i, b)
            for b in range(NBEAT):
                b_beat(NB - 1, b)


INPUTS = ["x", "itok_BxS_13_99985", "ctx_2048", "L0_attn_Wq", "L0_attn_Wk", "L0_attn_Wv", "L0_attn_Wo",
          "L0_attn_lambda_q1", "L0_attn_lambda_k1", "L0_attn_lambda_q2", "L0_attn_lambda_k2", "L0_attn_gn_w",
          "L0_attn_gn_b", "L0_ffn_router_w", "L0_ffn_gate_w", "L0_ffn_up_w", "L0_ffn_down_w", "L0_ffn_s_gate_w",
          "L0_ffn_s_gate_b", "L0_ffn_s_up_w", "L0_ffn_s_up_b", "L0_ffn_s_down_w", "L0_ffn_s_down_b"]


def constants():
    c = np.zeros((P, NCONST), np.float32)
    r = np.arange(P)
    c[:, C_ID:C_ID + P] = np.eye(P)
    c[:, C_BLK:C_BLK + P] = (r[:, None] // VW == r[None, :] // VW) / VW
    c[:, C_MASK:C_MASK + P] = np.where(r[None, :] > r[:, None], MASKED, 0.0)
    inv = (np.float32(1.0) / np.float32(10000.0) ** (np.arange(0, DH, 2, dtype=np.float32) / np.float32(DH)))
    angle = np.arange(T, dtype=np.float32)[:, None] * inv.astype(np.float32)[None, :]
    for col, f in ((C_COS, np.cos), (C_SIN, np.sin)):
        tab = np.repeat(f(angle), 2, axis=1).reshape(NT, P, DH).transpose(1, 0, 2)
        c[:, col:col + NT * DH] = tab.reshape(P, NT * DH)
    c[:, C_IOTA:C_IOTA + 8] = np.arange(8)
    c[0, C_ROW0] = 1.0
    c[1, C_ROW1] = 1.0
    c[:, C_EPS] = EPS
    c[:, C_HALF] = -0.5
    c[:, C_OUT] = 1.0 - LAMBDA_INIT
    c[0:2, C_TWO:C_TWO + P] = 1.0
    return c


def kernel(**inputs):
    import concourse.bacc as bacc
    from concourse.bass_utils import run_bass_kernel_spmd

    nc = bacc.Bacc("TRN2", target_bir_lowering=False, num_devices=1)
    arrays, aps = {}, {}
    for name in INPUTS:
        arr = np.ascontiguousarray(inputs[name])
        arrays["dram_" + name] = arr
        aps[name] = nc.dram_tensor("dram_" + name, arr.shape, mybir.dt.from_np(arr.dtype), kind="ExternalInput").ap()
    arrays["dram_consts"] = constants()
    aps["consts"] = nc.dram_tensor("dram_consts", (P, NCONST), F32, kind="ExternalInput").ap()
    out = nc.dram_tensor("out", (NB, T, D), F32, kind="ExternalOutput").ap()
    build(nc, aps, out)
    r = run_bass_kernel_spmd(nc, [arrays], core_ids=[0])
    return r.results[0]["out"]
```

```python
from contextlib import ExitStack

import numpy as np

import concourse.bass as bass
from concourse import mybir

F32 = mybir.dt.float32
F32R = mybir.dt.float32r
BF16 = mybir.dt.bfloat16
I32 = mybir.dt.int32
U32 = mybir.dt.uint32
ALU = mybir.AluOpType
ACT = mybir.ActivationFunctionType
AX_X = mybir.AxisListType.X

P = 128
NB, T, D = 4, 256, 256
NT, ND = T // P, D // P
H, KV, DH = 16, 4, 16
REP = H // KV
VW = 2 * DH
QC, KC = H * VW, KV * VW
NG = KV
LAMBDA_INIT = 0.2
EPS = 1e-5
E1, VOCAB = 4, 12500
E2, INNER = 8, 176
SI = 2 * INNER
HID = E2 * INNER + SI
NCH = (HID + P - 1) // P
LAST = HID - (NCH - 1) * P
NGR = 1 + E2
MASKED = -1.0e30
SLOTS = 3
PRE, A, B = "PRE", "A", "B"

C_ID, C_BLK, C_MASK, C_COS, C_SIN = 0, P, 2 * P, 3 * P, 3 * P + NT * DH
C_IOTA = C_SIN + NT * DH
C_ROW0, C_ROW1, C_EPS, C_HALF = C_IOTA + 8, C_IOTA + 9, C_IOTA + 10, C_IOTA + 11
C_OUT = C_IOTA + 12
C_TWO = C_IOTA + 13
NCONST = C_TWO + P

UNITS = [u for g in range(NG) for u in ((g, 0, 0, 4), (g, 1, 0, 2), (g, 1, 2, 2))]
NU = len(UNITS)

HGROUPS = [(0, 4), (4, 4), (8, 4), (12, NCH - 12)]


class Signal:

    def __init__(self, sem, per):
        self.sem, self.per = sem, per

    def __call__(self, i, k):
        return self.sem, (i + 1) * self.per + k


def three_pass(pe, out, lhs_h, lhs_l, rhs_h, rhs_l, start, stop):
    pe.matmul(out, lhs_h, rhs_l, start=start, stop=False, skip_group_check=True)
    pe.matmul(out, lhs_h, rhs_h, start=False, stop=False, skip_group_check=True)
    return pe.matmul(out, lhs_l, rhs_h, start=False, stop=stop, skip_group_check=True)


def build(nc, a, out):
    ctx = ExitStack()
    with ctx:
        def sb(name, shape, dt=F32):
            return ctx.enter_context(nc.sbuf_tensor(name, shape, dt))

        def psum(name, shape):
            return ctx.enter_context(nc.psum_tensor(name, shape, F32))

        def sem(name):
            return ctx.enter_context(nc.semaphore(name))

        signals = []

        def sig(name, per):
            signals.append(Signal(sem(name), per))
            return signals[-1]

        wqkv_h, wqkv_l = (sb(n, [P, ND, QC + 2 * KC], F32R) for n in ("wqkv_h", "wqkv_l"))
        wo_h, wo_l = (sb(n, [P, NG, D], F32R) for n in ("wo_h", "wo_l"))
        ct_h, ct_l = (sb(n, [P, ND, E1, D], F32R) for n in ("ct_h", "ct_l"))
        gu_h, gu_l = (sb(n, [P, E2, ND, 2 * INNER], F32R) for n in ("gu_h", "gu_l"))
        sg_h, sg_l = (sb(n, [P, ND, SI + E2 + SI], F32R) for n in ("sg_h", "sg_l"))
        dn_h, dn_l = (sb(n, [P, NCH, D], F32R) for n in ("dn_h", "dn_l"))
        bias_r = sb("bias_r", [P, 2 * SI + D], F32R)

        const = sb("const", [P, NCONST])
        ident = const[:, C_ID:C_ID + P]
        ident_r = sb("ident_r", [P, P], F32R)
        two_r = sb("two_r", [P, P], F32R)
        ident_b = sb("ident_b", [P, P], BF16)
        mask_b = sb("mask_b", [P, 4, P], BF16)
        lam_in = sb("lam_in", [P, 4, DH])
        lam = sb("lam", [P, 8])
        passed = sb("passed", [P, 32])
        gn_wb = sb("gn_wb", [P, 2, NG])

        x_in = sb("x_in", [P, NT, D])
        x_res = sb("x_res", [P, NT, D])
        x1 = sb("x1", [P, NT, D])
        stat_a = sb("stat_a", [P, NT, 6])
        mv_a = sb("mv_a", [P, NT, 2])
        rstd_a = sb("rstd_a", [P, NT, 2])
        xt_kt = sb("xt_kt", [P, 4 * T], F32R)
        xta_h = xt_kt[:, 0:2 * T].rearrange("p (c t) -> p c t", c=ND)
        xta_l = xt_kt[:, 2 * T:4 * T].rearrange("p (c t) -> p c t", c=ND)
        kt = xt_kt[:, :].rearrange("p (g t) -> p g t", g=KV)
        probs = sb("probs", [P, 2, 1024])
        rot = probs[:, :, :].rearrange("p a b -> p (a b)")
        qk = sb("qk", [P, NT, QC + KC])
        stack = sb("stack", [P, 2, 8, 4, DH], F32R)
        qt = sb("qt", [P, 2, 4, P], F32R)
        vpad = sb("vpad", [P, 2, NT, 96 + KV * P], F32R)
        nmax = sb("nmax", [P, 2, 8])
        rsum = sb("rsum", [P, 2, 8])
        rinv = sb("rinv", [P, 2, 8])
        dt = sb("dt", [P, 2, 4, 2, P], F32R)
        dt_h, dt_l = dt[:, :, :, 0, :], dt[:, :, :, 1, :]
        y_h = qt[:, :, :, :].rearrange("p a h t -> p (a h t)").rearrange("p (g t) -> p g t", g=NG)
        y_l = dt[:, 0, :, :, :].rearrange("p b l t -> p b (l t)")
        ao = sb("ao", [P, NG, T])
        gstat = sb("gstat", [P, NG, 6])
        gmv = sb("gmv", [P, NG, 2])
        gtmp = sb("gtmp", [P, 6, NG])

        stream = sb("stream", [P, 2 * NT * D])
        xb = stream[:, 0:NT * D].rearrange("p (t d) -> p t d", t=NT)
        result = stream[:, NT * D:].rearrange("p (t d) -> p t d", t=NT)
        stat_b = sb("stat_b", [P, NT, 6])
        mv_b = sb("mv_b", [P, NT, 2])
        rstd_b = sb("rstd_b", [P, NT, 2])
        xtb_h, xtb_l = (sb(n, [P, ND, T], F32R) for n in ("xtb_h", "xtb_l"))
        hid = sb("hid", [P, HID])
        z = hid[:, 0:2 * D].rearrange("p (t d) -> p t d", t=NT)
        zt = hid[:, 2 * D:4 * D].rearrange("p (t d) -> p t d", t=NT)
        xnb = hid[:, 4 * D:6 * D].rearrange("p (t d) -> p t d", t=NT)
        ht_h, ht_l = (sb(n, [P, 2, 4 * P], F32R) for n in ("ht_h", "ht_l"))
        act_g = sb("act_g", [P, 2, SI])
        tok = sb("tok", [P, NT], I32)
        routed = sb("routed", [P, E1 - 1, NT], U32)
        rt = sb("rt", [P, 8, 8])
        top_i = sb("top_i", [P, 8], U32)
        comb = sb("comb", [P, E2])

        s_bank = psum("s_bank", [P, 3, 512])
        tr_bank = psum("tr_bank", [P, 512])
        o_bank = psum("o_bank", [P, 512])
        b_bank = psum("b_bank", [P, 3, 512])
        o_halves = o_bank[:, :].rearrange("p (t l s) -> p t l s", t=NT, l=2)

        w_in = [sem(f"w_in{k}") for k in range(SLOTS)]
        s_const, s_lam, s_gn = sem("s_const"), sem("s_lam"), sem("s_gn")
        w_high, c_high, c_low = sem("w_high"), sem("c_high"), sem("c_low")
        w_low = [sem(f"w_low{k}") for k in range(SLOTS)]
        s_bias, w_ready, pool_ready = sem("s_bias"), sem("w_ready"), sem("pool_ready")
        c_mm = sem("c_mm")
        set_v, set_a = sem("set_v"), sem("set_a")
        SET_CONST, SET_SUM, SET_V = 9, 12, 14

        x_loaded, tok_loaded = sig("x_loaded", 16), sig("tok_loaded", 16)
        res_loaded = sig("res_loaded", 16)
        a_stat, a_aggr, a_rstd, a_xn = (sig("a_stat", 2), sig("a_aggr", 2),
                                               sig("a_rstd", 2), sig("a_xn", 2))
        a_xt_mm, a_xt_h, a_xt_l = sig("a_xt_mm", 1), sig("a_xt_h", 1), sig("a_xt_l", 1)
        a_qkv, a_mul, a_rot = sig("a_qkv", 3), sig("a_mul", 6), sig("a_rot", 6)
        a_vh, a_vl = sig("a_vh", 1), sig("a_vl", 1)
        a_st_h, a_st_l, a_st_mm, a_st = sig("a_st_h", 10), sig("a_st_l", 10), sig("a_st_mm", 10), sig("a_st", 10)
        a_s, a_max, a_exp = sig("a_s", 2 * NU), sig("a_max", 2 * NU), sig("a_exp", 2 * NU)
        a_inv, a_rho, a_p1, a_diff = sig("a_inv", 2 * NU), sig("a_rho", NU), sig("a_p1", NU), sig("a_diff", NU - NG)
        a_p2, a_diff_pool = sig("a_p2", NG), sig("a_diff_pool", NG)
        a_dt_mm, a_dt_h, a_dt_l, a_pv = (sig("a_dt_mm", NU), sig("a_dt_h", NU), sig("a_dt_l", NU),
                                         sig("a_pv", NU))
        a_oh, a_o, a_gst, a_gag = sig("a_oh", NG), sig("a_o", NG), sig("a_gst", NG), sig("a_gag", NG)
        a_gmm, a_gv, a_gp = sig("a_gmm", 2), sig("a_gv", 5), sig("a_gp", 2)
        a_y, a_yh, a_yl = sig("a_y", NG), sig("a_yh", NG), sig("a_yl", NG)
        a_wo, a_x1 = sig("a_wo", 1), sig("a_x1", 1)

        b_x, b_stat, b_aggr, b_rstd, b_xn = (sig("b_x", 1), sig("b_stat", 4), sig("b_aggr", 4),
                                             sig("b_rstd", 4), sig("b_xn", 4))
        NTR = 3 + NT * len(HGROUPS)
        b_tr, b_tr_h, b_tr_l = sig("b_tr", NTR), sig("b_tr_h", NTR), sig("b_tr_l", NTR)
        b_mask, b_zy, b_e0, b_sel = sig("b_mask", 3), sig("b_zy", 8), sig("b_e0", 4), sig("b_sel", 12)
        b_zz, b_th, b_p, b_x2 = sig("b_zz", 2), sig("b_th", 2), sig("b_p", 2), sig("b_x2", 2)
        b_up, b_tanh, b_a, b_hid = (sig("b_up", NT * NGR), sig("b_tanh", NT * NGR), sig("b_a", NT * NGR),
                                    sig("b_hid", NT * NGR))
        RV = 12
        b_rv, b_re = sig("b_rv", NT * RV), sig("b_re", NT)
        b_down, b_out, b_store = sig("b_down", NT), sig("b_out", NT), sig("b_store", 16)

        def rows(w):
            return w.rearrange("(c p) n -> c p n", p=P)

        stage = [hid[:, 0:880], hid[:, 880:1760], stream[:, 0:880]]
        pieces = []
        for c in range(ND):
            pieces.append(([(wqkv_h[:, c, 0:QC], wqkv_l[:, c, 0:QC], 0, QC, P, 1.0),
                            (wqkv_h[:, c, QC:QC + KC], wqkv_l[:, c, QC:QC + KC], QC, KC, P, DH ** -0.5),
                            (wqkv_h[:, c, QC + KC:], wqkv_l[:, c, QC + KC:], QC + KC, KC, P, 1.0)],
                           [(0, QC, P, rows(a["L0_attn_Wq"])[c]), (QC, KC, P, rows(a["L0_attn_Wk"])[c]),
                            (QC + KC, KC, P, rows(a["L0_attn_Wv"])[c])]))
        for c in range(0, NG, 2):
            pieces.append(([(wo_h[:, c:c + 2, :], wo_l[:, c:c + 2, :], 0, 2 * D, P, 1.0)],
                           [(D * k, D, P, rows(a["L0_attn_Wo"])[c + k]) for k in range(2)]))
        for c in range(ND):
            pieces.append(([(sg_h[:, c, :], sg_l[:, c, :], 0, 2 * SI + E2, P, 1.0)],
                           [(0, SI, P, rows(a["L0_ffn_s_gate_w"])[c]),
                            (SI, E2, P, a["L0_ffn_router_w"].rearrange("e (c p) -> c p e", p=P)[c]),
                            (SI + E2, SI, P, rows(a["L0_ffn_s_up_w"])[c])]))
        for e in range(E2):
            pieces.append(([(gu_h[:, e, :, :], gu_l[:, e, :, :], 0, 4 * INNER, P, 1.0)],
                           [(k * INNER, INNER, P, rows(w[e])[k // 2])
                            for k, w in enumerate((a["L0_ffn_gate_w"], a["L0_ffn_up_w"]) * 2)]))
        down = a["L0_ffn_down_w"].rearrange("e i h -> (e i) h")
        down = rows(down)
        full = E2 * INNER // P
        for c in range(0, full, 3):
            n = min(3, full - c)
            pieces.append(([(dn_h[:, c:c + n, :], dn_l[:, c:c + n, :], 0, n * D, P, 1.0)],
                           [(D * k, D, P, down[c + k]) for k in range(n)]))
        s_down = a["L0_ffn_s_down_w"]
        n = NCH - 1 - full
        pieces.append(([(dn_h[:, full:full + n, :], dn_l[:, full:full + n, :], 0, n * D, P, 1.0),
                        (dn_h[0:LAST, NCH - 1, :], dn_l[0:LAST, NCH - 1, :], n * D, D, LAST, 1.0)],
                       [(D * k, D, P, s_down[k * P:(k + 1) * P, :]) for k in range(n)]
                       + [(n * D, D, LAST, s_down[n * P:SI, :])]))
        biases = [[(0, SI, "s_gate_b"), (SI, SI, "s_up_b")], [(2 * SI, D, "s_down_b")]]
        NW = len(pieces)
        landed, load_done = [0] * SLOTS, []
        for k, n_loads in enumerate([len(p[1]) for p in pieces] + [1] * E1 + [len(b) for b in biases]):
            landed[k % SLOTS] += 16 * n_loads
            load_done.append(landed[k % SLOTS])
        parts_done = [sum(len(p[0]) for p in pieces[:k + 1]) for k in range(NW)]
        slot_parts = [sum(len(p[0]) for p in pieces[k % SLOTS:k + 1:SLOTS]) for k in range(NW)]

        def staged(k, off, cols, r):
            return stage[k % SLOTS][0:r, off:off + cols]

        w_behind = [[] for _ in range(NU)]
        for n in range(2, NW + E1 + 1):
            w_behind[(n - 1) * NU // (NW + E1)].append(n)

        def stages(order, i_p, i_a, i_b, behind=None):
            at_batch = {PRE: i_p, A: i_a, B: i_b}
            for stage, step, *at in order:
                if at_batch[stage] is not None:
                    step(at_batch[stage], *at)
                    if behind is not None:
                        behind(step, at)

        def like(ap, to):
            return ap.rearrange("p (a b) -> p a b", a=to.shape[1]) if len(to.shape) == 3 else ap

        x_dram = a["x"].rearrange("b (t p) d -> b p t d", p=P)
        out_dram = out.rearrange("b (t p) d -> b p t d", p=P)
        tok_dram = a["itok_BxS_13_99985"].rearrange("b (t p) -> b p t", p=P)

        def stack_parts(j):
            w = j - 2
            if j < 2:
                src, slots = qk[:, j, QC:QC + KC], (slice(0, 2), slice(2, 4))
            else:
                src, slots = qk[:, w % 2, (w // 2) * P:(w // 2 + 1) * P], (slice(0, 4, 2), slice(1, 4, 2))
            src = src.rearrange("p (m d) -> p m d", d=DH).unsqueeze(2).to_broadcast([P, 8, 2, DH])
            return src, stack[:, j % 2, :, slots[0], :], stack[:, j % 2, :, slots[1], :]

        n_rot = (NT * KC, QC, QC)
        cos_at = (0, 2 * NT * KC, 0)
        sin_at = (NT * KC, 2 * NT * KC + QC, 2 * NT * KC + 2 * QC)
        kv_bank = s_bank[:, 1, :].rearrange("p (t c) -> p t c", t=NT)
        v_parts = [vpad[:, part, :, 96:].rearrange("p t (g d) -> p t g d", g=KV)[:, :, :, 0:VW] for part in range(2)]
        v_new = kv_bank[:, :, KC:].rearrange("p t (g d) -> p t g d", g=KV)

        XT_BANK = (2, 1, 2)
        zy_banks = [b_bank[:, q % 3, :] for q in range(8)]
        gate_banks = [b_bank[:, (2 - n) % 3 if n else 0, :] for n in range(NGR)]

        def parts_of(k):
            if k < 3:
                return xtb_l[:, :, :], b_bank[:, XT_BANK[k], :].rearrange("p (c t) -> p c t", c=ND), xtb_h[:, :, :]
            j = (k - 3) % len(HGROUPS)
            n = HGROUPS[j][1] * P
            return ht_l[:, j % 2, 0:n], b_bank[:, 2 * (j % 2), 0:n], ht_h[:, j % 2, 0:n]

        def stack_job(s):
            g = (s + 2) // 3
            return 2 + 2 * g + (s % 3 == 2) if s >= 1 and s % 3 and g < NG else None

        block = ctx.enter_context(nc.Block())

        @block.sync
        def _(sp):
            sp.dma_start(x_in[:, :, :], x_dram[0]).then_inc(x_loaded.sem, 16)
            sp.dma_start(const[:, :], a["consts"]).then_inc(s_const, 16)
            for s in signals:
                sp.sem_inc(s.sem, s.per)
            for k, (_, loads) in enumerate(pieces):
                if k >= SLOTS:
                    sp.wait_ge(w_low[k % SLOTS], slot_parts[k - SLOTS])
                for off, cols, r, src in loads:
                    sp.dma_start(staged(k, off, cols, r), src, allow_slow_non_contiguous=cols == E2
                                 ).then_inc(w_in[k % SLOTS], 16)
                if k == 1:
                    for j, name in enumerate(("q1", "k1", "q2", "k2")):
                        v = a["L0_attn_lambda_" + name].rearrange("(o d) -> o d", o=1)
                        sp.dma_start(lam_in[:, j, :], v.to_broadcast([P, DH])).then_inc(s_lam, 16)
                    for j, name in enumerate(("w", "b")):
                        sp.dma_start(gn_wb[:, j, :], a["L0_attn_gn_" + name].rearrange("(g p) -> p g", p=P),
                                     allow_slow_non_contiguous=True).then_inc(s_gn, 16)
                if k == SLOTS:
                    sp.wait_ge(*a_xt_mm(0, 1))
                    sp.dma_start(x_in[:, :, :], x_dram[1]).then_inc(x_loaded.sem, 16)
                if k == NW // 2:
                    sp.dma_start(x_res[:, :, :], x_dram[0]).then_inc(res_loaded.sem, 16)
                    sp.dma_start(tok[:, :], tok_dram[0], allow_slow_non_contiguous=True).then_inc(tok_loaded.sem, 16)
            for e in range(E1):
                k = NW + e
                if e < SLOTS:
                    sp.wait_ge(w_low[k % SLOTS], slot_parts[k - SLOTS])
                else:
                    sp.wait_ge(c_mm, e - SLOTS + 1)
                sp.dma_start(staged(k, 0, 2 * D, P).rearrange("p (c d) -> p c d", c=ND),
                             a["ctx_2048"][e].rearrange("(c p) d -> p c d", p=P)).then_inc(w_in[k % SLOTS], 16)
            for j, loads in enumerate(biases):
                k = NW + E1 + j
                sp.wait_ge(c_mm, E1 - SLOTS + 1 + j)
                for off, cols, name in loads:
                    v = a["L0_ffn_" + name].rearrange("(o n) -> o n", o=1)
                    sp.dma_start(staged(k, off - loads[0][0], cols, 2), v.to_broadcast([2, cols])
                                 ).then_inc(w_in[k % SLOTS], 16)

            def next_tokens(i):
                sp.wait_ge(*b_mask(i, 3))
                sp.dma_start(tok[:, :], tok_dram[i + 1], allow_slow_non_contiguous=True
                             ).then_inc(tok_loaded.sem, 16)

            def store(i):
                sp.wait_ge(*b_out(i, NT))
                sp.dma_start(out_dram[i], result[:, :, :]).then_inc(b_store.sem, 16)

            def next_x(i):
                sp.wait_ge(*a_xt_mm(i - 1, 1))
                sp.dma_start(x_in[:, :, :], x_dram[i]).then_inc(x_loaded.sem, 16)

            def next_res(i):
                sp.wait_ge(*a_x1(i, 0))
                sp.dma_start(x_res[:, :, :], x_dram[i]).then_inc(res_loaded.sem, 16)

            next_x(2)
            next_res(1)
            for i in range(NB):
                if i + 1 < NB:
                    next_tokens(i)
                store(i)
                if i + 3 < NB:
                    next_x(i + 3)
                if i + 2 < NB:
                    next_res(i + 2)
            sp.wait_ge(*b_store(NB, 0))

        @block.gpsimd
        def _(pool):
            def a_norm(i):
                pool.wait_ge(*a_aggr(i, 2))
                pool.tensor_tensor(rstd_a[:, :, 0], mv_a[:, :, 1], const[:, C_EPS:C_EPS + 1].to_broadcast([P, NT]),
                                   ALU.add).then_inc(a_rstd.sem, 1)
                pool.wait_ge(*a_rstd(i, 1))
                pool.tensor_tensor(rstd_a[:, :, 1], rstd_a[:, :, 0],
                                   const[:, C_HALF:C_HALF + 1].to_broadcast([P, NT]),
                                   ALU.pow).then_inc(a_rstd.sem, 1)

            def a_rotate(i, j):
                n = n_rot[j]
                o = qk[:, :, QC:] if j == 0 else qk[:, j - 1:j, 0:QC]
                c, sn = (rot[:, k:k + n].rearrange("p (t m two) -> p t m two", t=o.shape[1], two=2)
                         for k in (cos_at[j], sin_at[j]))
                o = o.rearrange("p t (m two) -> p t m two", two=2)
                pool.wait_ge(*a_mul(i, 2 * j + 2))
                pool.wait_ge(*a_st_l(i, 0))
                pool.tensor_tensor(o[:, :, :, 0], c[:, :, :, 0], sn[:, :, :, 1], ALU.subtract).then_inc(a_rot.sem, 1)
                pool.tensor_tensor(o[:, :, :, 1], c[:, :, :, 1], sn[:, :, :, 0], ALU.add).then_inc(a_rot.sem, 1)

            def a_stack(i, j):
                src, hi, lo = stack_parts(j)
                pool.wait_ge(*a_st_h(i, j + 1))
                pool.tensor_tensor(lo, src, hi.bitcast(F32), ALU.subtract).then_inc(a_st_l.sem, 1)

            def a_scale(i, u):
                g, t, h0, nh = UNITS[u]
                p1 = probs[:, u % 2, 0:512].rearrange("p (h s) -> p h s", h=nh)
                pool.wait_ge(*a_exp(i, 2 * u + 1))
                pool.wait_ge(*a_inv(i, 2 * u + 1))
                pool.tensor_tensor(p1, p1, rinv[:, u % 2, 0:nh].unsqueeze(2).to_broadcast([P, nh, 512 // nh]),
                                   ALU.mult).then_inc(a_p1.sem, 1)

            def a_combine(i, u):
                g, t, h0, nh = UNITS[u]
                p1, p2 = probs[:, u % 2, 0:512], probs[:, u % 2, 512:1024]
                heads = p2.rearrange("p (h s) -> p h s", h=nh)
                pool.wait_ge(*a_exp(i, 2 * u + 2))
                pool.wait_ge(*a_rho(i, u + 1))
                pool.tensor_tensor(heads, heads, rsum[:, u % 2, nh:2 * nh].unsqueeze(2).to_broadcast([P, nh, 512 // nh]),
                                   ALU.mult).then_inc(a_p2.sem, 1)
                pool.wait_ge(*a_p1(i, u + 1))
                pool.wait_ge(*a_p2(i, g + 1))
                pool.tensor_tensor(p1, p1, p2, ALU.add).then_inc(a_diff_pool.sem, 1)

            def a_rhos(i, u):
                g, t, h0, nh = UNITS[u]
                pool.wait_ge(*a_inv(i, 2 * u + 2))
                pool.tensor_tensor(rsum[:, u % 2, nh:2 * nh], rinv[:, u % 2, nh:2 * nh],
                                   lam[:, 5:6].to_broadcast([P, nh]), ALU.mult).then_inc(a_rho.sem, 1)

            def a_group(i):
                pool.wait_ge(*a_gv(i, 5))
                pool.tensor_tensor(gtmp[:, 4, :], gtmp[:, 3, :], const[:, C_HALF:C_HALF + 1].to_broadcast([P, NG]),
                                   ALU.pow).then_inc(a_gp.sem, 1)
                pool.wait_ge(*a_gp(i, 1))
                pool.tensor_tensor(gtmp[:, 5, :], gtmp[:, 4, :], gn_wb[:, 0, :], ALU.mult).then_inc(a_gp.sem, 1)

            def b_norm(i, k):
                pool.wait_ge(*b_aggr(i, 2 * k + 2))
                pool.tensor_tensor(rstd_b[:, :, 0], mv_b[:, :, 1], const[:, C_EPS:C_EPS + 1].to_broadcast([P, NT]),
                                   ALU.add).then_inc(b_rstd.sem, 1)
                pool.wait_ge(*b_rstd(i, 2 * k + 1))
                pool.tensor_tensor(rstd_b[:, :, 1], rstd_b[:, :, 0],
                                   const[:, C_HALF:C_HALF + 1].to_broadcast([P, NT]),
                                   ALU.pow).then_inc(b_rstd.sem, 1)

            def w_piece(n):
                if n >= NW or n % 2:
                    return
                at = parts_done[n - 1]
                for hi, lo, off, cols, r, scale in pieces[n][0]:
                    at += 1
                    pool.wait_ge(w_high, at)
                    pool.tensor_tensor(lo, like(staged(n, off, cols, r), hi), hi.bitcast(F32), ALU.subtract
                                       ).then_inc(w_low[n % SLOTS], 1)

            order = [
                (A, a_stack, 0), (A, a_stack, 1), (A, a_stack, 2), (B, b_norm, 0), (A, a_stack, 3),
                (A, a_stack, 4), (A, a_scale, 0), (A, a_rhos, 0), (A, a_combine, 0), (A, a_stack, 5),
                (A, a_rhos, 1), (A, a_scale, 1), (A, a_scale, 2), (A, a_rhos, 2), (A, a_stack, 6), (A, a_stack, 7),
                (A, a_scale, 3), (A, a_rhos, 3), (A, a_combine, 3), (A, a_scale, 4), (A, a_rhos, 4),
                (B, b_norm, 1), (A, a_stack, 8), (A, a_rhos, 5), (A, a_scale, 5), (A, a_scale, 6), (A, a_rhos, 6),
                (A, a_combine, 6), (A, a_scale, 7), (A, a_stack, 9), (A, a_rhos, 7), (A, a_scale, 8),
                (A, a_rhos, 8), (PRE, a_norm), (A, a_scale, 9), (A, a_rhos, 9), (A, a_combine, 9),
                (A, a_scale, 10), (A, a_rhos, 10), (A, a_scale, 11), (A, a_rhos, 11), (A, a_group),
                (PRE, a_rotate, 0), (PRE, a_rotate, 1), (PRE, a_rotate, 2),
            ]

            def behind_pre(step, at):
                if step is a_rotate and at[0] == 2:
                    pool.wait_ge(s_gn, 32)
                    pool.tensor_tensor(gn_wb[:, :, :], gn_wb[:, :, :],
                                       const[:, C_OUT:C_OUT + 1].unsqueeze(1).to_broadcast([P, 2, NG]), ALU.mult
                                       ).then_inc(pool_ready, 1)
                    pool.wait_ge(pool_ready, 1)
                    pool.wait_ge(set_v, SET_V)
                    for n in w_behind[0]:
                        w_piece(n)

            def behind(step, at):
                if step is a_scale and at[0] > 0:
                    for n in w_behind[at[0]]:
                        w_piece(n)

            pool.wait_ge(s_const, 16)
            stages(order, 0, None, None, behind_pre)
            stages(order, 1, 0, None, behind)
            with pool.Fori(0, NB - 2) as i:
                stages(order, i + 2, i + 1, i)
            stages(order, None, NB - 1, NB - 2)
            stages(order, None, None, NB - 1)

        @block.scalar
        def _(act):
            act.preload_act_table(ACT.Exp)

            def w_piece(n):
                if n < NW:
                    act.wait_ge(w_in[n % SLOTS], load_done[n])
                    for hi, lo, off, cols, r, scale in pieces[n][0]:
                        act.activation(hi, like(staged(n, off, cols, r), hi), ACT.Copy, scale=scale
                                       ).then_inc(w_high, 1)
                elif n < NW + E1:
                    e = n - NW
                    act.wait_ge(c_mm, e + 1)
                    act.activation(ct_h[:, :, e, :], b_bank[:, e % 2, :].rearrange("p (c f) -> p c f", c=ND),
                                   ACT.Copy).then_inc(c_high, 1)

            def a_xt(i):
                act.wait_ge(*a_xt_mm(i, 1))
                act.wait_ge(*a_s(i, 0))
                act.activation(xt_kt[:, 0:2 * T], tr_bank[:, :], ACT.Copy).then_inc(a_xt_h.sem, 1)

            def a_values(i):
                act.wait_ge(*a_qkv(i, 1))
                act.wait_ge(*a_mul(i, 2))
                act.wait_ge(*a_pv(i, 0))
                act.activation(v_parts[0], v_new, ACT.Copy).then_inc(a_vh.sem, 1)

            def a_stack(i, j):
                act.wait_ge(*a_st_mm(i, j + 1))
                if j < 2:
                    dst, w = kt[:, :, j * P:(j + 1) * P], 0
                else:
                    dst, w = qt[:, j % 2, :, :], j - 2
                    if w >= 2:
                        act.wait_ge(*a_s(i, 2 * (3 * ((w - 2) // 2) + (3 if w % 2 else 1))))
                    else:
                        act.wait_ge(*a_wo(i, 0))
                act.activation(dst, tr_bank[:, :].rearrange("p (g s) -> p g s", g=4), ACT.Copy
                               ).then_inc(a_st.sem, 1)

            def a_split(i, j):
                src, hi, lo = stack_parts(j)
                act.wait_ge(*a_rot(i, 2 if j < 2 else 4 + 2 * (j % 2)))
                act.wait_ge(*a_st_mm(i, max(j - 1, 0)))
                act.activation(hi, src, ACT.Copy).then_inc(a_st_h.sem, 1)

            def a_exps(i, u, half):
                g, t, h0, nh = UNITS[u]
                n = 512 // nh
                act.wait_ge(*a_max(i, 2 * u + half + 1))
                if u >= 2:
                    act.wait_ge(*a_dt_mm(i, u - 1))
                else:
                    act.wait_ge(*a_rot(i, 6))
                for h in range(nh):
                    o = half * 512 + h * n
                    j = half * nh + h
                    last = act.activation(probs[:, u % 2, o:o + n], s_bank[:, (2 * u + half) % 3, h * n:(h + 1) * n],
                                          ACT.Exp, bias=nmax[:, u % 2, j:j + 1], accum_out=rsum[:, u % 2, j:j + 1])
                last.then_inc(a_exp.sem, 1)

            def a_diff_h(i, u):
                act.wait_ge(*a_dt_mm(i, u + 1))
                if u >= 2:
                    act.wait_ge(*a_pv(i, u - 1))
                else:
                    act.wait_ge(*a_wo(i, 0))
                act.activation(dt_h[:, u % 2], tr_bank[:, :].rearrange("p (b t) -> p b t", b=4), ACT.Copy).then_inc(a_dt_h.sem, 1)

            def a_out(i, g):
                act.wait_ge(*a_pv(i, 3 * g + 3))
                act.wait_ge(*a_yl(i, 0))
                act.activation(ao[:, g, :].rearrange("p (t s) -> p t s", t=NT), o_halves[:, :, 0, :], ACT.Copy
                               ).then_inc(a_oh.sem, 1)

            def a_y_high(i, g):
                act.wait_ge(*a_y(i, g + 1))
                act.activation(y_h[:, g, :], ao[:, g, :], ACT.Identity, bias=gn_wb[:, 1, g:g + 1]
                               ).then_inc(a_yh.sem, 1)

            def b_high(i, k):
                low, src, high = parts_of(k)
                act.wait_ge(*b_tr(i, k + 1))
                act.activation(high, src, ACT.Copy).then_inc(b_tr_h.sem, 1)

            def b_first(i, k):
                act.wait_ge(*b_zy(i, 2 * k + 1))
                act.activation(z[:, k % 2, :], zy_banks[2 * k][:, 0:D], ACT.Copy).then_inc(b_e0.sem, 1)

            def b_tanh_z(i, t):
                act.wait_ge(*b_sel(i, 3 * t + 3))
                act.activation(zt[:, t, :], z[:, t, :], ACT.Tanh, scale=0.5).then_inc(b_th.sem, 1)
                act.wait_ge(*b_hid(i, 0))
                act.activation(act_g[:, t, 0:D], z[:, t, :], ACT.Square).then_inc(b_zz.sem, 1)

            def b_router(i, t):
                act.wait_ge(*b_rv(i, RV * t + 1))
                act.activation(rt[:, 1, :], b_bank[:, 0, SI:SI + E2], ACT.Exp, bias=rt[:, 0, 0:1],
                               accum_out=rt[:, 0, 1:2]).then_inc(b_re.sem, 1)

            def b_act(i, t, n):
                k = NGR * t + n
                cols = SI if n == 0 else INNER
                act.wait_ge(*b_up(i, k + 1))
                if n == 0:
                    act.wait_ge(*b_rv(i, RV * t + 1))
                if k >= 2:
                    act.wait_ge(*b_hid(i, k - 1))
                act.activation(act_g[:, k % 2, 0:cols], gate_banks[n][:, 0:cols], ACT.Tanh, scale=0.5
                               ).then_inc(b_tanh.sem, 1)

            order = [
                (A, a_split, 0), (A, a_split, 1), (A, a_split, 2), (A, a_stack, 0), (A, a_stack, 1),
                (A, a_split, 3), (A, a_stack, 2), (B, b_high, 0), (A, a_split, 4), (A, a_stack, 3),
                (A, a_exps, 0, 0), (A, a_exps, 0, 1), (B, b_first, 0), (A, a_exps, 1, 0), (A, a_exps, 1, 1),
                (B, b_tanh_z, 0), (B, b_first, 1), (A, a_stack, 4), (A, a_split, 5), (A, a_split, 6),
                (A, a_diff_h, 0), (A, a_exps, 2, 0), (B, b_tanh_z, 1), (A, a_exps, 2, 1), (A, a_stack, 5),
                (B, b_high, 1), (A, a_split, 7), (A, a_diff_h, 1), (A, a_exps, 3, 0), (B, b_first, 2),
                (A, a_exps, 3, 1), (B, b_first, 3), (A, a_diff_h, 2), (A, a_exps, 4, 0), (A, a_exps, 4, 1),
                (A, a_stack, 6), (A, a_split, 8), (A, a_diff_h, 3), (A, a_exps, 5, 0), (A, a_exps, 5, 1),
                (A, a_stack, 7), (A, a_out, 0), (B, b_high, 2), (A, a_diff_h, 4), (A, a_exps, 6, 0),
                (A, a_exps, 6, 1), (B, b_router, 0), (B, b_act, 0, 0), (B, b_act, 0, 1), (A, a_diff_h, 5),
                (A, a_split, 9), (A, a_exps, 7, 0), (B, b_act, 0, 2), (A, a_stack, 8), (A, a_exps, 7, 1),
                (B, b_act, 0, 3), (A, a_out, 1), (A, a_diff_h, 6), (B, b_act, 0, 4), (A, a_exps, 8, 0),
                (B, b_act, 0, 5), (B, b_act, 0, 6), (A, a_stack, 9), (B, b_act, 0, 7), (B, b_act, 0, 8),
                (A, a_exps, 8, 1), (A, a_diff_h, 7), (B, b_high, 3), (B, b_high, 4), (A, a_exps, 9, 0),
                (A, a_exps, 9, 1), (B, b_high, 5), (B, b_high, 6), (A, a_diff_h, 8), (A, a_exps, 10, 0),
                (A, a_exps, 10, 1), (B, b_router, 1), (B, b_act, 1, 0), (A, a_exps, 11, 0), (A, a_diff_h, 9),
                (B, b_act, 1, 1), (A, a_exps, 11, 1), (A, a_out, 2), (B, b_act, 1, 2), (B, b_act, 1, 3),
                (B, b_act, 1, 4), (A, a_diff_h, 10), (A, a_diff_h, 11), (B, b_act, 1, 5), (B, b_act, 1, 6),
                (PRE, a_xt), (A, a_out, 3), (B, b_act, 1, 7), (B, b_act, 1, 8), (B, b_high, 7), (B, b_high, 8),
                (B, b_high, 9), (A, a_y_high, 0), (A, a_y_high, 1), (A, a_y_high, 2), (A, a_y_high, 3),
                (PRE, a_values), (B, b_high, 10),
            ]

            def behind_pre(step, at):
                if step is a_values:
                    act.wait_ge(set_v, SET_SUM)
                    act.activation(lam[:, 2:4], lam[:, 0:2], ACT.Exp).then_inc(set_a, 1)
                    for n in w_behind[0]:
                        w_piece(n)

            def behind(step, at):
                if step is a_exps and at[0] > 0 and at[1] == 1:
                    for n in w_behind[at[0]]:
                        w_piece(n)

            w_piece(0)
            w_piece(1)
            stages(order, 0, None, None, behind_pre)
            stages(order, 1, 0, None, behind)
            with act.Fori(0, NB - 2) as i:
                stages(order, i + 2, i + 1, i)
            stages(order, None, NB - 1, NB - 2)
            stages(order, None, None, NB - 1)

        @block.vector
        def _(dve):
            done = [0]

            def step(ins):
                ins.then_inc(set_v, 1)
                done[0] += 1

            def after():
                dve.wait_ge(set_v, done[0])

            def w_piece(n):
                if n < 2 or n < NW and n % 2:
                    at = parts_done[n - 1] if n else 0
                    for hi, lo, off, cols, r, scale in pieces[n][0]:
                        at += 1
                        dve.wait_ge(w_high, at)
                        dve.scalar_tensor_tensor(lo, like(staged(n, off, cols, r), hi), scale, hi.bitcast(F32),
                                                 ALU.mult, ALU.subtract).then_inc(w_low[n % SLOTS], 1)
                elif NW <= n < NW + E1:
                    e = n - NW
                    dve.wait_ge(c_high, e + 1)
                    dve.tensor_tensor(ct_l[:, :, e, :], b_bank[:, e % 2, :].rearrange("p (c f) -> p c f", c=ND),
                                      ct_h[:, :, e, :].bitcast(F32), ALU.subtract).then_inc(c_low, 1)
                elif n == NW + E1:
                    for j, loads in enumerate(biases):
                        m = n + j
                        c0, cols = loads[0][0], sum(x[1] for x in loads)
                        raw, parts = staged(m, 0, cols, 2), bias_r[0:2, c0:c0 + cols]
                        dve.wait_ge(w_in[m % SLOTS], load_done[m])
                        dve.tensor_copy(parts, raw).then_inc(s_bias, 1)
                        dve.wait_ge(s_bias, 4 * j + 1)
                        dve.tensor_tensor(raw, raw, parts.bitcast(F32), ALU.subtract).then_inc(s_bias, 1)
                        dve.wait_ge(s_bias, 4 * j + 2)
                        dve.tensor_scalar(raw, raw, const[0:2, C_ROW1:C_ROW1 + 1], None, ALU.mult).then_inc(s_bias, 1)
                        dve.wait_ge(s_bias, 4 * j + 3)
                        dve.scalar_tensor_tensor(parts, parts.bitcast(F32), const[0:2, C_ROW0:C_ROW0 + 1], raw,
                                                 ALU.mult, ALU.add).then_inc(s_bias, 1)
                    dve.wait_ge(s_bias, 4 * len(biases))
                    for n_last in range(NW - SLOTS, NW):
                        dve.wait_ge(w_low[n_last % SLOTS], slot_parts[n_last])
                    dve.wait_ge(c_low, E1)
                    dve.tensor_copy(lam[:, 6:7], lam[:, 5:6]).then_inc(w_ready, 1)

            step(dve.memset(vpad[:, :, :, :].bitcast(F32), 0.0))
            step(dve.memset(bias_r[:, :].bitcast(F32), 0.0))
            dve.wait_ge(s_const, 16)
            step(dve.tensor_copy(ident_r[:, :], ident))
            step(dve.tensor_copy(ident_b[:, :], ident))
            step(dve.tensor_copy(two_r[:, :], const[:, C_TWO:C_TWO + P]))
            for j in range(4):
                step(dve.tensor_copy(mask_b[:, j, :], const[:, C_MASK:C_MASK + P]))
            assert done[0] == SET_CONST

            def lambdas(first):
                if first:
                    dve.wait_ge(s_lam, 64)
                    step(dve.tensor_tensor(lam_in[:, 0, :], lam_in[:, 0, :], lam_in[:, 1, :], ALU.mult))
                    step(dve.tensor_tensor(lam_in[:, 2, :], lam_in[:, 2, :], lam_in[:, 3, :], ALU.mult))
                    after()
                    step(dve.tensor_reduce(lam[:, 0:2], lam_in[:, 0:4:2, :], AX_X, ALU.add))
                    assert done[0] == SET_SUM
                else:
                    dve.wait_ge(set_a, 1)
                    step(dve.tensor_tensor(lam[:, 4:5], lam[:, 3:4], lam[:, 2:3], ALU.subtract))
                    after()
                    step(dve.tensor_scalar(lam[:, 5:6], lam[:, 4:5], -LAMBDA_INIT, None, ALU.add))
                    after()
                    assert done[0] == SET_V

            iota = const[:, C_IOTA:C_IOTA + 8]

            turn = [0]

            def settled():
                k = turn[0] = (turn[0] + 1) % 32
                dve.tensor_copy(passed[:, k:k + 1], const[:, C_EPS:C_EPS + 1])

            def a_stats(i):
                dve.wait_ge(*x_loaded(i, 16))
                for t in range(NT):
                    dve.bn_stats(stat_a[:, t, :], x_in[:, t, :]).then_inc(a_stat.sem, 1)

            def a_moments(i, t):
                dve.wait_ge(*a_stat(i, t + 1))
                settled()
                dve.bn_aggr(mv_a[:, t, :], stat_a[:, t, :]).then_inc(a_aggr.sem, 1)

            def a_normed(i, t):
                dve.wait_ge(*a_rstd(i, 2))
                dve.tensor_scalar(x_in[:, t, :], x_in[:, t, :], mv_a[:, t, 0:1], rstd_a[:, t, 1:2],
                                  ALU.subtract, ALU.mult).then_inc(a_xn.sem, 1)

            def a_xt(i):
                dve.wait_ge(*a_xt_h(i, 1))
                dve.tensor_tensor(xt_kt[:, 2 * T:4 * T], tr_bank[:, :], xt_kt[:, 0:2 * T].bitcast(F32), ALU.subtract
                                  ).then_inc(a_xt_l.sem, 1)

            def a_rotate(i, j):
                n = n_rot[j]
                x = kv_bank[:, :, 0:KC] if j == 0 else s_bank[:, 2 * j - 2:2 * j - 1, :]
                x = x.rearrange("p t (m d) -> p t m d", d=DH)
                dve.wait_ge(*a_qkv(i, j + 1))
                if j < 2:
                    dve.wait_ge(*a_dt_mm(i, 0))
                else:
                    dve.wait_ge(*a_rot(i, 2))
                for at, c0 in ((cos_at[j], C_COS), (sin_at[j], C_SIN)):
                    tab = const[:, c0:c0 + NT * DH].rearrange("p (t d) -> p t d", t=NT)
                    tab = (tab if j == 0 else tab[:, j - 1:j, :]).unsqueeze(2).to_broadcast(list(x.shape))
                    dve.tensor_tensor(rot[:, at:at + n].rearrange("p (t m d) -> p t m d", t=x.shape[1], d=DH), x, tab,
                                      ALU.mult).then_inc(a_mul.sem, 1)

            def a_values(i):
                dve.wait_ge(*a_vh(i, 1))
                dve.wait_ge(*a_pv(i, 0))
                dve.tensor_tensor(v_parts[1], v_new, v_parts[0].bitcast(F32), ALU.subtract).then_inc(a_vl.sem, 1)

            def a_maxima(i, u, half):
                g, t, h0, nh = UNITS[u]
                m = 2 * u + half
                dve.wait_ge(*a_s(i, m + 1))
                if u >= 2:
                    dve.wait_ge(*a_exp(i, m - 3))
                dve.tensor_reduce(nmax[:, u % 2, half * nh:(half + 1) * nh],
                                  s_bank[:, m % 3, :].rearrange("p (h s) -> p h s", h=nh),
                                  AX_X, ALU.max, negate=True).then_inc(a_max.sem, 1)

            def a_inverse(i, u, half):
                g, t, h0, nh = UNITS[u]
                heads = slice(half * nh, (half + 1) * nh)
                dve.wait_ge(*a_exp(i, 2 * u + half + 1))
                dve.reciprocal(rinv[:, u % 2, heads], rsum[:, u % 2, heads]).then_inc(a_inv.sem, 1)

            def a_combine(i, u):
                g, t, h0, nh = UNITS[u]
                n = 512 // nh
                dve.wait_ge(*a_rho(i, u + 1))
                dve.wait_ge(*a_p1(i, u + 1))
                for h in range(nh):
                    p1 = probs[:, u % 2, h * n:(h + 1) * n]
                    last = dve.scalar_tensor_tensor(p1, probs[:, u % 2, 512 + h * n:512 + (h + 1) * n],
                                                    rsum[:, u % 2, nh + h:nh + h + 1], p1, ALU.mult, ALU.add)
                last.then_inc(a_diff.sem, 1)

            def a_diff_l(i, u):
                dve.wait_ge(*a_dt_h(i, u + 1))
                dve.tensor_tensor(dt_l[:, u % 2], tr_bank[:, :].rearrange("p (b t) -> p b t", b=4),
                                  dt_h[:, u % 2].bitcast(F32), ALU.subtract
                                  ).then_inc(a_dt_l.sem, 1)

            def a_out(i, g):
                dve.wait_ge(*a_oh(i, g + 1))
                out_g = ao[:, g, :].rearrange("p (t s) -> p t s", t=NT)
                dve.tensor_tensor(out_g, out_g, o_halves[:, :, 1, :], ALU.add).then_inc(a_o.sem, 1)

            def a_gstat(i, g):
                dve.wait_ge(*a_o(i, g + 1))
                dve.bn_stats(gstat[:, g, :], ao[:, g, :]).then_inc(a_gst.sem, 1)

            def a_gmoments(i, g):
                dve.wait_ge(*a_gst(i, g + 1))
                settled()
                dve.bn_aggr(gmv[:, g, :], gstat[:, g, :]).then_inc(a_gag.sem, 1)

            def a_group(i, k):
                if k == 0:
                    dve.wait_ge(*a_gmm(i, 1))
                    dve.tensor_copy(gtmp[:, 0, :], o_bank[:, 0:NG]).then_inc(a_gv.sem, 1)
                elif k == 1:
                    dve.wait_ge(*a_gv(i, 1))
                    dve.tensor_tensor(gtmp[:, 1, :], gmv[:, :, 0], gtmp[:, 0, :], ALU.subtract).then_inc(a_gv.sem, 1)
                elif k == 2:
                    dve.wait_ge(*a_gv(i, 2))
                    dve.tensor_tensor(gtmp[:, 2, :], gtmp[:, 1, :], gtmp[:, 1, :], ALU.mult).then_inc(a_gv.sem, 1)
                elif k == 3:
                    dve.wait_ge(*a_gv(i, 3))
                    dve.tensor_tensor(gtmp[:, 2, :], gtmp[:, 2, :], gmv[:, :, 1], ALU.add).then_inc(a_gv.sem, 1)
                else:
                    dve.wait_ge(*a_gmm(i, 2))
                    dve.tensor_scalar(gtmp[:, 3, :], o_bank[:, NG:2 * NG], EPS, None, ALU.add).then_inc(a_gv.sem, 1)

            def a_scaled(i, g):
                dve.wait_ge(*a_gp(i, 2))
                dve.tensor_scalar(ao[:, g, :], ao[:, g, :], gtmp[:, 0, g:g + 1], gtmp[:, 5, g:g + 1],
                                  ALU.subtract, ALU.mult).then_inc(a_y.sem, 1)

            def a_y_low(i, g):
                dve.wait_ge(*a_yh(i, g + 1))
                dve.scalar_tensor_tensor(y_l[:, g, :], ao[:, g, :], gn_wb[:, 1, g:g + 1],
                                         y_h[:, g, :].bitcast(F32), ALU.add, ALU.subtract).then_inc(a_yl.sem, 1)

            def a_residual(i):
                dve.wait_ge(*a_wo(i, 1))
                dve.wait_ge(*res_loaded(i, 16))
                dve.wait_ge(*b_x(i, 0))
                dve.tensor_tensor(x1[:, :, :], tr_bank[:, :].rearrange("p (t d) -> p t d", t=NT), x_res[:, :, :], ALU.add
                                  ).then_inc(a_x1.sem, 1)

            def b_take(i):
                dve.wait_ge(*a_x1(i, 1))
                dve.wait_ge(*b_out(i, 0))
                dve.tensor_copy(xb[:, :, :], x1[:, :, :]).then_inc(b_x.sem, 1)

            def b_masks(i):
                dve.wait_ge(*tok_loaded(i, 16))
                dve.wait_ge(*b_sel(i, 0))
                for e in range(1, E1):
                    dve.tensor_scalar(routed[:, e - 1, :], tok[:, :], float(e * (VOCAB // E1)), None, ALU.is_ge
                                      ).then_inc(b_mask.sem, 1)

            def b_stats(i, k, t):
                if k == 0:
                    dve.wait_ge(*b_x(i, 1))
                else:
                    dve.wait_ge(*b_x2(i, t + 1))
                dve.bn_stats(stat_b[:, t, :], xb[:, t, :]).then_inc(b_stat.sem, 1)

            def b_moments(i, k, t):
                dve.wait_ge(*b_stat(i, 2 * k + t + 1))
                settled()
                dve.bn_aggr(mv_b[:, t, :], stat_b[:, t, :]).then_inc(b_aggr.sem, 1)

            def b_normed(i, k, t):
                dve.wait_ge(*b_rstd(i, 2 * k + 2))
                if k == 0:
                    dve.wait_ge(*b_tr(i, 0))
                dve.tensor_scalar(xnb[:, t, :], xb[:, t, :], mv_b[:, t, 0:1], rstd_b[:, t, 1:2],
                                  ALU.subtract, ALU.mult).then_inc(b_xn.sem, 1)

            def b_low(i, k):
                dst, src, high = parts_of(k)
                dve.wait_ge(*b_tr_h(i, k + 1))
                dve.tensor_tensor(dst, src, high.bitcast(F32), ALU.subtract).then_inc(b_tr_l.sem, 1)

            def b_select(i, k, e):
                t = k % 2
                if e == 1:
                    dve.wait_ge(*b_e0(i, k + 1))
                else:
                    dve.wait_ge(*b_zy(i, 2 * k + 2))
                if k == 0:
                    dve.wait_ge(*b_mask(i, 3))
                if e > 1:
                    dve.wait_ge(*b_sel(i, 3 * k + e - 1))
                settled()
                dve.copy_predicated(z[:, t, :], routed[:, e - 1, t:t + 1].to_broadcast([P, D]),
                                    zy_banks[2 * k + e // 2][:, (e % 2) * D:(e % 2 + 1) * D]).then_inc(b_sel.sem, 1)

            def b_gate(i, t):
                dve.wait_ge(*b_zz(i, t + 1))
                dve.scalar_tensor_tensor(z[:, t, :], zt[:, t, :], 1.0, act_g[:, t, 0:D], ALU.add, ALU.mult
                                         ).then_inc(b_p.sem, 1)

            def b_add(i, t):
                dve.wait_ge(*b_sel(i, 3 * (2 + t) + 3))
                dve.scalar_tensor_tensor(xb[:, t, :], z[:, t, :], 0.5, xb[:, t, :], ALU.mult, ALU.add
                                         ).then_inc(b_x2.sem, 1)

            def b_router(i, t, part):
                k = RV * t
                if part == 0:
                    dve.wait_ge(*b_up(i, NGR * t + 1))
                    dve.tensor_reduce(rt[:, 0, 0:1], b_bank[:, 0, SI:SI + E2], AX_X, ALU.max, negate=True
                                      ).then_inc(b_rv.sem, 1)
                elif part == 1:
                    dve.wait_ge(*b_re(i, t + 1))
                    dve.reciprocal(rt[:, 0, 2:3], rt[:, 0, 1:2]).then_inc(b_rv.sem, 1)
                elif part == 2:
                    dve.wait_ge(*b_rv(i, k + 2))
                    dve.tensor_scalar(rt[:, 2, :], rt[:, 1, :], rt[:, 0, 2:3], None, ALU.mult).then_inc(b_rv.sem, 1)
                elif part == 3:
                    dve.wait_ge(*b_rv(i, k + 3))
                    settled()
                    dve.max(rt[:, 3, :], rt[:, 2, :]).then_inc(b_rv.sem, 1)
                elif part == 4:
                    dve.wait_ge(*b_rv(i, k + 4))
                    settled()
                    dve.max_index(top_i[:, :], rt[:, 3, :], rt[:, 2, :]).then_inc(b_rv.sem, 1)
                    dve.tensor_tensor(rt[:, 0, 3:4], rt[:, 3, 0:1], rt[:, 3, 1:2], ALU.add).then_inc(b_rv.sem, 1)
                elif part == 5:
                    dve.wait_ge(*b_rv(i, k + 6))
                    dve.reciprocal(rt[:, 0, 4:5], rt[:, 0, 3:4]).then_inc(b_rv.sem, 1)
                    dve.tensor_copy(rt[:, 4, :], top_i[:, :]).then_inc(b_rv.sem, 1)
                elif part == 6:
                    dve.wait_ge(*b_rv(i, k + 8))
                    dve.tensor_scalar(rt[:, 5, 0:2], rt[:, 3, 0:2], rt[:, 0, 4:5], 0.5, ALU.mult, ALU.mult
                                      ).then_inc(b_rv.sem, 1)
                elif part == 7:
                    dve.wait_ge(*b_rv(i, k + 9))
                    dve.wait_ge(*b_hid(i, NGR * t))
                    dve.tensor_scalar(comb[:, :], iota, rt[:, 4, 0:1], rt[:, 5, 0:1], ALU.is_equal, ALU.mult
                                      ).then_inc(b_rv.sem, 1)
                    dve.tensor_scalar(rt[:, 6, :], iota, rt[:, 4, 1:2], rt[:, 5, 1:2], ALU.is_equal, ALU.mult
                                      ).then_inc(b_rv.sem, 1)
                else:
                    dve.wait_ge(*b_rv(i, k + 11))
                    dve.tensor_tensor(comb[:, :], comb[:, :], rt[:, 6, :], ALU.add).then_inc(b_rv.sem, 1)

            def b_gated(i, t, n):
                k = NGR * t + n
                cols = SI if n == 0 else INNER
                gate = gate_banks[n][:, 0:cols]
                h = act_g[:, k % 2, 0:cols]
                dve.wait_ge(*b_tanh(i, k + 1))
                dve.scalar_tensor_tensor(h, h, 1.0, gate, ALU.add, ALU.mult).then_inc(b_a.sem, 1)

            def b_mul(i, t, n):
                k = NGR * t + n
                cols = SI if n == 0 else INNER
                up = b_bank[:, 2, 0:SI] if n == 0 else gate_banks[n][:, INNER:2 * INNER]
                h = act_g[:, k % 2, 0:cols]
                dve.wait_ge(*b_a(i, k + 1))
                if n == 0 and t == 1:
                    dve.wait_ge(*b_tr(i, 3 + len(HGROUPS)))
                if n == 1:
                    dve.wait_ge(*b_rv(i, RV * t + RV))
                col = E2 * INNER if n == 0 else (n - 1) * INNER
                share = 0.5 if n == 0 else comb[:, n - 1:n]
                dve.scalar_tensor_tensor(hid[:, col:col + cols], h, share, up, ALU.mult, ALU.mult
                                         ).then_inc(b_hid.sem, 1)

            def b_final(i, t):
                dve.wait_ge(*b_down(i, t + 1))
                dve.wait_ge(*b_store(i, 0))
                dve.tensor_tensor(result[:, t, :], b_bank[:, 1, 0:D], xb[:, t, :], ALU.add).then_inc(b_out.sem, 1)

            order = [
                (B, b_take), (B, b_stats, 0, 0), (B, b_stats, 0, 1), (B, b_moments, 0, 0), (B, b_moments, 0, 1),
                (B, b_normed, 0, 0), (B, b_normed, 0, 1), (B, b_low, 0), (PRE, a_stats), (B, b_masks),
                (A, a_maxima, 0, 0), (A, a_maxima, 0, 1), (A, a_inverse, 0, 0), (A, a_maxima, 1, 0),
                (A, a_inverse, 0, 1), (A, a_maxima, 1, 1), (B, b_select, 0, 1), (B, b_select, 0, 2),
                (A, a_inverse, 1, 0), (B, b_select, 0, 3), (A, a_inverse, 1, 1), (A, a_maxima, 2, 0),
                (B, b_select, 1, 1), (B, b_select, 1, 2), (B, b_select, 1, 3), (A, a_maxima, 2, 1), (B, b_gate, 0),
                (A, a_diff_l, 0), (A, a_inverse, 2, 0), (B, b_gate, 1), (A, a_combine, 1), (A, a_inverse, 2, 1),
                (A, a_maxima, 3, 0), (B, b_low, 1), (A, a_maxima, 3, 1), (A, a_maxima, 4, 0), (A, a_combine, 2),
                (A, a_diff_l, 1), (B, b_select, 2, 1), (A, a_inverse, 3, 0), (B, b_select, 2, 2),
                (A, a_maxima, 4, 1), (B, b_select, 2, 3), (A, a_inverse, 3, 1), (B, b_add, 0), (B, b_select, 3, 1),
                (B, b_stats, 1, 0), (A, a_diff_l, 2), (B, b_select, 3, 2), (B, b_moments, 1, 0),
                (B, b_select, 3, 3), (A, a_inverse, 4, 0), (B, b_add, 1), (A, a_maxima, 5, 0), (B, b_stats, 1, 1),
                (A, a_inverse, 4, 1), (B, b_moments, 1, 1), (A, a_maxima, 5, 1), (A, a_diff_l, 3),
                (B, b_normed, 1, 0), (B, b_normed, 1, 1), (A, a_combine, 4), (A, a_maxima, 6, 0), (A, a_out, 0),
                (B, b_low, 2), (A, a_inverse, 5, 0), (A, a_inverse, 5, 1), (A, a_maxima, 6, 1), (A, a_diff_l, 4),
                (A, a_gstat, 0), (A, a_combine, 5), (A, a_inverse, 6, 0), (B, b_router, 0, 0), (A, a_maxima, 7, 0),
                (A, a_inverse, 6, 1), (B, b_router, 0, 1), (B, b_router, 0, 2), (B, b_gated, 0, 0),
                (B, b_router, 0, 3), (A, a_gmoments, 0), (B, b_mul, 0, 0), (A, a_diff_l, 5), (B, b_router, 0, 4),
                (A, a_maxima, 7, 1), (B, b_router, 0, 5), (PRE, a_moments, 0), (B, b_router, 0, 6),
                (B, b_router, 0, 7), (B, b_gated, 0, 1), (A, a_inverse, 7, 0), (B, b_router, 0, 8),
                (B, b_mul, 0, 1), (B, b_gated, 0, 2), (A, a_maxima, 8, 0), (B, b_mul, 0, 2), (B, b_gated, 0, 3),
                (A, a_maxima, 8, 1), (B, b_mul, 0, 3), (B, b_gated, 0, 4), (A, a_diff_l, 6), (B, b_mul, 0, 4),
                (B, b_gated, 0, 5), (A, a_inverse, 7, 1), (B, b_mul, 0, 5), (A, a_inverse, 8, 0),
                (B, b_gated, 0, 6), (A, a_combine, 7), (B, b_mul, 0, 6), (B, b_gated, 0, 7), (B, b_mul, 0, 7),
                (B, b_gated, 0, 8), (B, b_mul, 0, 8), (PRE, a_moments, 1), (A, a_maxima, 9, 0), (A, a_out, 1),
                (B, b_low, 3), (B, b_low, 4), (A, a_inverse, 8, 1), (A, a_maxima, 9, 1), (A, a_combine, 8),
                (A, a_inverse, 9, 0), (A, a_diff_l, 7), (A, a_maxima, 10, 0), (A, a_inverse, 9, 1), (B, b_low, 5),
                (PRE, a_normed, 0), (B, b_low, 6), (PRE, a_normed, 1), (A, a_diff_l, 8), (A, a_maxima, 10, 1),
                (A, a_inverse, 10, 0), (A, a_maxima, 11, 0), (A, a_inverse, 10, 1), (A, a_maxima, 11, 1),
                (B, b_final, 0), (A, a_combine, 10), (B, b_router, 1, 0), (B, b_router, 1, 1), (B, b_router, 1, 2),
                (B, b_gated, 1, 0), (B, b_router, 1, 3), (B, b_mul, 1, 0), (B, b_router, 1, 4),
                (B, b_router, 1, 5), (A, a_inverse, 11, 0), (B, b_router, 1, 6), (B, b_router, 1, 7),
                (B, b_gated, 1, 1), (B, b_router, 1, 8), (B, b_mul, 1, 1), (A, a_diff_l, 9), (A, a_inverse, 11, 1),
                (B, b_gated, 1, 2), (A, a_out, 2), (B, b_mul, 1, 2), (A, a_combine, 11), (B, b_gated, 1, 3),
                (A, a_diff_l, 10), (B, b_mul, 1, 3), (B, b_gated, 1, 4), (A, a_gstat, 1), (A, a_gstat, 2),
                (B, b_mul, 1, 4), (A, a_diff_l, 11), (B, b_gated, 1, 5), (B, b_mul, 1, 5), (A, a_gmoments, 1),
                (A, a_gmoments, 2), (B, b_gated, 1, 6), (B, b_mul, 1, 6), (PRE, a_xt), (A, a_out, 3),
                (A, a_gstat, 3), (B, b_gated, 1, 7), (B, b_mul, 1, 7), (A, a_gmoments, 3), (B, b_gated, 1, 8),
                (B, b_mul, 1, 8), (A, a_group, 0), (A, a_group, 1), (A, a_group, 2), (A, a_group, 3),
                (PRE, a_rotate, 0), (B, b_low, 7), (A, a_group, 4), (PRE, a_rotate, 1), (B, b_low, 8),
                (A, a_scaled, 0), (A, a_scaled, 1), (A, a_scaled, 2), (A, a_scaled, 3), (B, b_low, 9),
                (A, a_y_low, 0), (A, a_y_low, 1), (A, a_y_low, 2), (A, a_y_low, 3), (PRE, a_rotate, 2),
                (B, b_low, 10), (PRE, a_values), (A, a_residual), (B, b_final, 1),
            ]

            def behind_pre(step, at):
                at_w = []
                if step is a_normed and at[0] == 1:
                    at_w = [0, 1]
                elif step is a_rotate and at[0] == 0:
                    lambdas(True)
                elif step is a_rotate and at[0] == 2:
                    lambdas(False)
                    at_w = w_behind[0]
                for n in at_w:
                    w_piece(n)

            def behind(step, at):
                if step is a_inverse and at[0] > 0 and at[1] == 1:
                    for n in w_behind[at[0]]:
                        w_piece(n)

            stages(order, 0, None, None, behind_pre)
            stages(order, 1, 0, None, behind)
            with dve.Fori(0, NB - 2) as i:
                stages(order, i + 2, i + 1, i)
            stages(order, None, NB - 1, NB - 2)
            stages(order, None, None, NB - 1)

        @block.tensor
        def _(pe):
            def w_piece(n):
                if NW <= n < NW + E1:
                    e = n - NW
                    pe.wait_ge(w_in[n % SLOTS], load_done[n])
                    if e >= 2:
                        pe.wait_ge(c_low, e - 1)
                    for c in range(ND):
                        for f in range(ND):
                            last = pe.transpose(b_bank[:, e % 2, c * D + f * P:c * D + (f + 1) * P],
                                                stage[n % SLOTS][:, f * D + c * P:f * D + (c + 1) * P], ident)
                    last.then_inc(c_mm, 1)

            def transposes(bank, src):
                for c in range(ND):
                    for t in range(NT):
                        last = pe.transpose(bank[:, c * T + t * P:c * T + (t + 1) * P], src[:, t, c * P:(c + 1) * P],
                                            ident)
                return last

            def a_xt(i):
                pe.wait_ge(*a_xn(i, 2))
                pe.wait_ge(*a_dt_l(i, 0))
                transposes(tr_bank, x_in).then_inc(a_xt_mm.sem, 1)

            def a_project(i, j):
                if j == 0:
                    pe.wait_ge(*a_xt_l(i, 1))
                    pe.wait_ge(*a_exp(i, 0))
                    jobs = [(kv_bank[:, t, :], t, QC, 2 * KC) for t in range(NT)]
                else:
                    jobs = [(s_bank[:, 2 * j - 2, :], j - 1, 0, QC)]
                for o, t, c0, n in jobs:
                    tok_t = slice(t * P, (t + 1) * P)
                    for c in range(ND):
                        last = three_pass(pe, o, xta_h[:, c, tok_t], xta_l[:, c, tok_t],
                                          wqkv_h[:, c, c0:c0 + n], wqkv_l[:, c, c0:c0 + n], c == 0, c == ND - 1)
                last.then_inc(a_qkv.sem, 1)

            def a_stack(i, j):
                pe.wait_ge(*a_st_l(i, j + 1))
                if j == 0:
                    pe.wait_ge(*a_x1(i, 0))
                elif j <= 4:
                    pe.wait_ge(*a_st(i, j))
                else:
                    pe.wait_ge(*a_dt_l(i, 3 * (j // 2 - 1) - (2 if j % 2 == 0 else 1) - 1))
                for b in range(4):
                    last = pe.matmul(tr_bank[:, b * P:(b + 1) * P],
                                     stack[:, j % 2, 2 * b:2 * b + 2, :, :].rearrange("p a b c -> p (a b c)"),
                                     ident_r[:, :], start=True, stop=True)
                last.then_inc(a_st_mm.sem, 1)

            def a_scores(i, u, half):
                g, t, h0, nh = UNITS[u]
                n = 512 // nh
                m = 2 * u + half
                bank = s_bank[:, m % 3, :]
                pe.wait_ge(*a_st(i, 2 * g + t + 3))
                if m >= 3:
                    pe.wait_ge(*a_exp(i, m - 2))
                else:
                    pe.wait_ge(*a_mul(i, 6))
                    pe.wait_ge(*a_vl(i, 1))
                pe.matmul(bank.rearrange("p (h s) -> p h s", h=nh)[:, :, n - P:n], ident_b[:, :], mask_b[:, 0:nh, :],
                          start=True, stop=False, skip_group_check=True)
                r = slice(half * 64, half * 64 + 64)
                for h in range(nh):
                    last = pe.matmul(bank[:, h * n:(h + 1) * n], qt[r, (2 * g + t) % 2, h0 + h, :], kt[r, g, 0:n],
                                     start=False, stop=True, skip_group_check=True)
                last.then_inc(a_s.sem, 1)

            def a_diff_t(i, u):
                if u % 3 == 0:
                    pe.wait_ge(*a_diff_pool(i, u // 3 + 1))
                else:
                    pe.wait_ge(*a_diff(i, u - u // 3))
                j = stack_job(u + 1)
                if j is None:
                    pe.wait_ge(*a_dt_l(i, u))
                else:
                    pe.wait_ge(*a_st(i, j + 1))
                for b in range(4):
                    last = pe.transpose(tr_bank[:, b * P:(b + 1) * P], probs[:, u % 2, b * P:(b + 1) * P], ident)
                last.then_inc(a_dt_mm.sem, 1)

            def a_values(i, u):
                g, t, h0, nh = UNITS[u]
                pe.wait_ge(*a_dt_l(i, u + 1))
                if u == 0:
                    pe.wait_ge(*a_gv(i, 0))
                elif u % 3 == 0:
                    pe.wait_ge(*a_o(i, g))
                for b in range(4):
                    h, s = (b, 0) if t == 0 else (h0 + b // 2, b % 2)
                    w0 = 96 + P * g - VW * h
                    pe.matmul(o_halves[:, t, :, :], vpad[:, 0, s, w0:w0 + P], dt[:, u % 2, b, :, :],
                              start=u % 3 == 0 and b == 0, stop=False, skip_group_check=True)
                    last = pe.matmul(o_halves[:, t, 1, :], vpad[:, 1, s, w0:w0 + P], dt_h[:, u % 2, b, :], start=False,
                                     stop=b == 3, skip_group_check=True)
                last.then_inc(a_pv.sem, 1)

            def a_group(i, k):
                block_mean = const[:, C_BLK:C_BLK + P]
                if k == 0:
                    pe.wait_ge(*a_gag(i, NG))
                    pe.matmul(o_bank[:, 0:NG], block_mean, gmv[:, :, 0], start=True, stop=True
                              ).then_inc(a_gmm.sem, 1)
                    return
                pe.wait_ge(*a_gv(i, 4))
                pe.matmul(o_bank[:, NG:2 * NG], block_mean, gtmp[:, 2, :], start=True, stop=True
                          ).then_inc(a_gmm.sem, 1)

            def a_output(i):
                pe.wait_ge(*a_yl(i, NG))
                pe.wait_ge(*a_dt_l(i, NU))
                if not (isinstance(i, int) and i == NB - 1):
                    pe.wait_ge(*a_xt_l(i + 1, 1))
                for t in range(NT):
                    for g in range(NG):
                        tt = slice(t * P, (t + 1) * P)
                        last = three_pass(pe, tr_bank[:, t * D:(t + 1) * D], y_h[:, g, tt], y_l[:, g, tt],
                                          wo_h[:, g, :], wo_l[:, g, :], t == 0 and g == 0, g == NG - 1)
                last.then_inc(a_wo.sem, 1)

            def b_xt(i, k):
                if k == 1:
                    pe.wait_ge(*b_p(i, 2))
                else:
                    pe.wait_ge(*b_xn(i, 2 + k))
                transposes(b_bank[:, XT_BANK[k], :], z if k == 1 else xnb).then_inc(b_tr.sem, 1)

            def b_routed(i, k, b):
                t, q = k % 2, 2 * k + b
                if q % 4 == 0:
                    pe.wait_ge(*b_tr_l(i, k // 2 + 1))
                if q == 1:
                    pe.wait_ge(*b_out(i, 0))
                if q >= 3:
                    pe.wait_ge(*b_sel(i, 3 * ((q - 3) // 2) + (3 if (q - 3) % 2 else 1)))
                tt = slice(t * P, (t + 1) * P)
                for c in range(ND):
                    last = three_pass(pe, zy_banks[q], xtb_h[:, c, tt], xtb_l[:, c, tt],
                                      ct_h[:, c, 2 * b:2 * b + 2, :].rearrange("p e d -> p (e d)"),
                                      ct_l[:, c, 2 * b:2 * b + 2, :].rearrange("p e d -> p (e d)"),
                                      c == 0, c == ND - 1)
                last.then_inc(b_zy.sem, 1)

            def b_shared(i, t):
                if t == 0:
                    pe.wait_ge(*b_tr_l(i, 3))
                tt = slice(t * P, (t + 1) * P)
                for b, c0, n in ((0, 0, SI + E2), (1, SI + E2, SI)):
                    o = b_bank[:, 2 * b, 0:n]
                    for c in range(ND):
                        three_pass(pe, o, xtb_h[:, c, tt], xtb_l[:, c, tt], sg_h[:, c, c0:c0 + n],
                                   sg_l[:, c, c0:c0 + n], c == 0, False)
                    last = pe.matmul(b_bank[:, 2 * b, 0:SI], two_r[:, :], bias_r[:, b * SI:(b + 1) * SI], start=False, stop=True,
                                     skip_group_check=True)
                last.then_inc(b_up.sem, 1)

            def b_expert(i, t, n):
                if n == 1:
                    pe.wait_ge(*b_out(i, t))
                else:
                    pe.wait_ge(*b_hid(i, NGR * t + max(n - 2, 1)))
                tt = slice(t * P, (t + 1) * P)
                for c in range(ND):
                    last = three_pass(pe, gate_banks[n][:, 0:2 * INNER], xtb_h[:, c, tt], xtb_l[:, c, tt],
                                      gu_h[:, n - 1, c, :], gu_l[:, n - 1, c, :], c == 0, c == ND - 1)
                last.then_inc(b_up.sem, 1)

            def b_hidden_t(i, t, j):
                c0, n = HGROUPS[j]
                if j < 2:
                    pe.wait_ge(*b_hid(i, NGR * (t + 1)))
                else:
                    pe.wait_ge(*b_tr_l(i, 2 + 4 * t + j))
                for c in range(c0, c0 + n):
                    r = P if c < NCH - 1 else LAST
                    last = pe.transpose(b_bank[0:r, 2 * (j % 2), (c - c0) * P:(c - c0 + 1) * P], hid[:, c * P:c * P + r], ident)
                last.then_inc(b_tr.sem, 1)

            def b_down_mm(i, t, j):
                c0, n = HGROUPS[j]
                o = b_bank[:, 1, 0:D]
                pe.wait_ge(*b_tr_l(i, 4 + 4 * t + j))
                for c in range(c0, c0 + n):
                    r = P if c < NCH - 1 else LAST
                    cols = slice((c - c0) * P, (c - c0 + 1) * P)
                    three_pass(pe, o, ht_h[0:r, j % 2, cols], ht_l[0:r, j % 2, cols], dn_h[0:r, c, :], dn_l[0:r, c, :],
                               c == 0, False)
                if j == len(HGROUPS) - 1:
                    pe.matmul(o, two_r[:, :], bias_r[:, 2 * SI:], start=False, stop=True, skip_group_check=True
                              ).then_inc(b_down.sem, 1)

            order = [
                (A, a_stack, 0), (A, a_stack, 1), (A, a_stack, 2), (B, b_xt, 0), (A, a_scores, 0, 0),
                (A, a_stack, 3), (A, a_scores, 0, 1), (B, b_routed, 0, 0), (A, a_scores, 1, 0),
                (A, a_scores, 1, 1), (A, a_stack, 4), (B, b_routed, 0, 1), (B, b_routed, 1, 0),
                (A, a_scores, 2, 0), (B, b_routed, 1, 1), (A, a_diff_t, 0), (A, a_scores, 2, 1),
                (A, a_scores, 3, 0), (A, a_scores, 3, 1), (A, a_stack, 5), (B, b_xt, 1), (A, a_values, 0),
                (A, a_diff_t, 1), (A, a_scores, 4, 0), (B, b_routed, 2, 0), (B, b_routed, 2, 1),
                (A, a_scores, 4, 1), (B, b_routed, 3, 0), (A, a_diff_t, 2), (B, b_routed, 3, 1),
                (A, a_scores, 5, 0), (A, a_scores, 5, 1), (A, a_stack, 6), (A, a_values, 1), (A, a_diff_t, 3),
                (A, a_values, 2), (A, a_scores, 6, 0), (A, a_stack, 7), (A, a_scores, 6, 1), (B, b_xt, 2),
                (A, a_diff_t, 4), (A, a_scores, 7, 0), (A, a_values, 3), (B, b_shared, 0), (B, b_expert, 0, 1),
                (A, a_diff_t, 5), (A, a_scores, 7, 1), (A, a_scores, 8, 0), (A, a_values, 4), (B, b_expert, 0, 2),
                (B, b_expert, 0, 3), (A, a_stack, 8), (A, a_scores, 8, 1), (A, a_values, 5), (A, a_diff_t, 6),
                (B, b_expert, 0, 4), (B, b_expert, 0, 5), (B, b_expert, 0, 6), (A, a_stack, 9),
                (B, b_expert, 0, 7), (B, b_expert, 0, 8), (A, a_scores, 9, 0), (A, a_diff_t, 7),
                (A, a_scores, 9, 1), (B, b_hidden_t, 0, 0), (B, b_hidden_t, 0, 1), (A, a_scores, 10, 0),
                (A, a_values, 6), (B, b_down_mm, 0, 0), (B, b_hidden_t, 0, 2), (B, b_down_mm, 0, 1),
                (B, b_hidden_t, 0, 3), (A, a_diff_t, 8), (A, a_scores, 10, 1), (A, a_scores, 11, 0),
                (B, b_down_mm, 0, 2), (B, b_down_mm, 0, 3), (A, a_scores, 11, 1), (B, b_shared, 1),
                (B, b_expert, 1, 1), (A, a_diff_t, 9), (A, a_values, 7), (A, a_values, 8), (B, b_expert, 1, 2),
                (B, b_expert, 1, 3), (B, b_expert, 1, 4), (A, a_diff_t, 10), (B, b_expert, 1, 5), (A, a_values, 9),
                (A, a_diff_t, 11), (A, a_values, 10), (B, b_expert, 1, 6), (PRE, a_xt), (A, a_values, 11),
                (B, b_expert, 1, 7), (B, b_expert, 1, 8), (PRE, a_project, 0), (A, a_group, 0),
                (B, b_hidden_t, 1, 0), (PRE, a_project, 1), (A, a_group, 1), (B, b_hidden_t, 1, 1),
                (B, b_down_mm, 1, 0), (B, b_hidden_t, 1, 2), (PRE, a_project, 2), (B, b_down_mm, 1, 1),
                (B, b_hidden_t, 1, 3), (B, b_down_mm, 1, 2), (A, a_output), (B, b_down_mm, 1, 3),
            ]

            def behind_pre(step, at):
                if step is a_project and at[0] == 2:
                    for n in w_behind[0]:
                        w_piece(n)

            def behind(step, at):
                if step is a_diff_t and at[0] < NU - 1:
                    for n in w_behind[at[0] + 1]:
                        w_piece(n)

            pe.wait_ge(set_v, SET_CONST)
            stages(order, 0, None, None, behind_pre)
            stages(order, 1, 0, None, behind)
            pe.wait_ge(w_ready, 1)
            with pe.Fori(0, NB - 2) as i:
                stages(order, i + 2, i + 1, i)
            stages(order, None, NB - 1, NB - 2)
            stages(order, None, None, NB - 1)


INPUTS = ["x", "itok_BxS_13_99985", "ctx_2048", "L0_attn_Wq", "L0_attn_Wk", "L0_attn_Wv", "L0_attn_Wo",
          "L0_attn_lambda_q1", "L0_attn_lambda_k1", "L0_attn_lambda_q2", "L0_attn_lambda_k2", "L0_attn_gn_w",
          "L0_attn_gn_b", "L0_ffn_router_w", "L0_ffn_gate_w", "L0_ffn_up_w", "L0_ffn_down_w", "L0_ffn_s_gate_w",
          "L0_ffn_s_gate_b", "L0_ffn_s_up_w", "L0_ffn_s_up_b", "L0_ffn_s_down_w", "L0_ffn_s_down_b"]


def constants():
    c = np.zeros((P, NCONST), np.float32)
    r = np.arange(P)
    c[:, C_ID:C_ID + P] = np.eye(P)
    c[:, C_BLK:C_BLK + P] = (r[:, None] // VW == r[None, :] // VW) / VW
    c[:, C_MASK:C_MASK + P] = np.where(r[None, :] > r[:, None], MASKED, 0.0)
    inv = (np.float32(1.0) / np.float32(10000.0) ** (np.arange(0, DH, 2, dtype=np.float32) / np.float32(DH)))
    angle = np.arange(T, dtype=np.float32)[:, None] * inv.astype(np.float32)[None, :]
    for col, f in ((C_COS, np.cos), (C_SIN, np.sin)):
        tab = np.repeat(f(angle), 2, axis=1).reshape(NT, P, DH).transpose(1, 0, 2)
        c[:, col:col + NT * DH] = tab.reshape(P, NT * DH)
    c[:, C_IOTA:C_IOTA + 8] = np.arange(8)
    c[0, C_ROW0] = 1.0
    c[1, C_ROW1] = 1.0
    c[:, C_EPS] = EPS
    c[:, C_HALF] = -0.5
    c[:, C_OUT] = 1.0 - LAMBDA_INIT
    c[0:2, C_TWO:C_TWO + P] = 1.0
    return c


def kernel(**inputs):
    import concourse.bacc as bacc
    from concourse.bass_utils import run_bass_kernel_spmd

    nc = bacc.Bacc("TRN2", target_bir_lowering=False, num_devices=1)
    arrays, aps = {}, {}
    for name in INPUTS:
        arr = np.ascontiguousarray(inputs[name])
        arrays["dram_" + name] = arr
        aps[name] = nc.dram_tensor("dram_" + name, arr.shape, mybir.dt.from_np(arr.dtype), kind="ExternalInput").ap()
    arrays["dram_consts"] = constants()
    aps["consts"] = nc.dram_tensor("dram_consts", (P, NCONST), F32, kind="ExternalInput").ap()
    out = nc.dram_tensor("out", (NB, T, D), F32, kind="ExternalOutput").ap()
    build(nc, aps, out)
    r = run_bass_kernel_spmd(nc, [arrays], core_ids=[0])
    return r.results[0]["out"]
```
